# Optimizing a Trainium2 kernel written in Bass

```python
import numpy as np
import jax
import jax.numpy as jnp

def _softmax(x, axis=-1):
    return jax.nn.softmax(x, axis=axis)

def _gelu(x):
    return jax.nn.gelu(x, approximate=True)

def _silu(x):
    return jax.nn.silu(x)

def _sigmoid(x):
    return jax.nn.sigmoid(x)

def _layernorm(x, axis=-1, eps=1e-05):
    m = jnp.mean(x, axis=axis, keepdims=True)
    v = jnp.var(x, axis=axis, keepdims=True)
    return (x - m) / jnp.sqrt(v + eps)

def _scatter_add(tgt, idx, src, axis=0):
    return tgt.at[idx].add(src)

def _segment_sum(src, seg, n):
    return jax.ops.segment_sum(src, seg, n)
kernel_name = 'mk_prb_d1_jaxref_r4_0f5a1b'

def setup_inputs(seed: int=0):
    np.random.seed(seed)
    _w = jnp.asarray

    def _L0_attn_setup():
        import jax, jax.numpy as jnp
        import numpy as np
        NUM_HEAD = 16
        D_Q = 128
        D_KV = 128
        ROPE_BASE = 10000.0

        def _cos_sin(seq_len, dim):
            pos = jnp.arange(seq_len, dtype=jnp.float32)[:, None]
            ids = jnp.arange(dim // 2, dtype=jnp.float32)
            theta = ROPE_BASE ** (-2.0 * ids) / (dim // 2)
            r = pos * theta[None, :]
            return (jnp.cos(r), jnp.sin(r))

        def _rope(x, cos, sin):
            b, s, d = x.shape
            xv = x.reshape(b, s, d // 2, 2)
            x0, x1 = (xv[..., 0], xv[..., 1])
            out = jnp.stack([x0 * cos - x1 * sin, x1 * cos + x0 * sin], axis=-1)
            return out.reshape(b, s, d)
        key = jax.random.key(seed)
        ks = jax.random.split(key, 10)
        d_model, d_q, d_kv = (256, D_Q, D_KV)
        b, s = (2, 512)
        w = lambda k, i, o: jax.random.normal(k, (i, o), dtype=jnp.float32) * 0.02
        return {'x': jax.random.normal(ks[0], (b, s, d_model), dtype=jnp.float32), 'Wd_q_w': w(ks[1], d_model, d_q), 'Wd_q_b': jnp.zeros((d_q,), jnp.float32), 'Wu_q_w': w(ks[2], d_q, d_model), 'Wu_q_b': jnp.zeros((d_model,), jnp.float32), 'Wq_r_w': w(ks[3], d_q, d_model), 'Wq_r_b': jnp.zeros((d_model,), jnp.float32), 'Wk_r_w': w(ks[4], d_model, d_model), 'Wk_r_b': jnp.zeros((d_model,), jnp.float32), 'Wd_kv_w': w(ks[5], d_model, d_kv), 'Wd_kv_b': jnp.zeros((d_kv,), jnp.float32), 'Wu_k_w': w(ks[6], d_kv, d_model), 'Wu_k_b': jnp.zeros((d_model,), jnp.float32), 'Wu_v_w': w(ks[7], d_kv, d_model), 'Wu_v_b': jnp.zeros((d_model,), jnp.float32), 'Wo_w': w(ks[8], d_model, d_model), 'Wo_b': jnp.zeros((d_model,), jnp.float32)}
    _L0_attn_in = _L0_attn_setup()

    def _L0_ffn_setup():
        import jax, jax.numpy as jnp
        import numpy as np
        EMBED_DIM = 256
        MLP_RATIO = 4
        NUM_EXPERTS = 8
        CAPACITY = 1.0
        LN_EPS = 1e-05

        def _layernorm(y, gamma, beta):
            mu = jnp.mean(y, axis=-1, keepdims=True)
            var = jnp.mean(jnp.square(y - mu), axis=-1, keepdims=True)
            return (y - mu) * jax.lax.rsqrt(var + LN_EPS) * gamma + beta
        key = jax.random.key(seed)
        k0, k1, k2, k3, k4, k5 = jax.random.split(key, 6)
        d = EMBED_DIM
        dd = EMBED_DIM * MLP_RATIO
        n = NUM_EXPERTS
        x = jax.random.normal(k0, (4, 512, d), dtype=jnp.float32)
        gate_w = jax.random.normal(k1, (n, d), dtype=jnp.float32) * 0.02
        ln_gamma = jnp.ones((d,), dtype=jnp.float32)
        ln_beta = jnp.zeros((d,), dtype=jnp.float32)
        fc1s = jax.random.normal(k2, (n, dd, d), dtype=jnp.float32) * (1.0 / np.sqrt(d))
        b1s = jax.random.normal(k3, (n, dd), dtype=jnp.float32) * 0.02
        fc2s = jax.random.normal(k4, (n, d, dd), dtype=jnp.float32) * (1.0 / np.sqrt(dd))
        b2s = jax.random.normal(k5, (n, d), dtype=jnp.float32) * 0.02
        return {'x': x, 'gate_w': gate_w, 'ln_gamma': ln_gamma, 'ln_beta': ln_beta, 'fc1s': fc1s, 'b1s': b1s, 'fc2s': fc2s, 'b2s': b2s}
    _L0_ffn_in = _L0_ffn_setup()
    _d = {'L0_attn_x': _L0_attn_in['x'], 'L0_attn_Wd_q_w': _L0_attn_in['Wd_q_w'], 'L0_attn_Wd_q_b': _L0_attn_in['Wd_q_b'], 'L0_attn_Wu_q_w': _L0_attn_in['Wu_q_w'], 'L0_attn_Wu_q_b': _L0_attn_in['Wu_q_b'], 'L0_attn_Wq_r_w': _L0_attn_in['Wq_r_w'], 'L0_attn_Wq_r_b': _L0_attn_in['Wq_r_b'], 'L0_attn_Wk_r_w': _L0_attn_in['Wk_r_w'], 'L0_attn_Wk_r_b': _L0_attn_in['Wk_r_b'], 'L0_attn_Wd_kv_w': _L0_attn_in['Wd_kv_w'], 'L0_attn_Wd_kv_b': _L0_attn_in['Wd_kv_b'], 'L0_attn_Wu_k_w': _L0_attn_in['Wu_k_w'], 'L0_attn_Wu_k_b': _L0_attn_in['Wu_k_b'], 'L0_attn_Wu_v_w': _L0_attn_in['Wu_v_w'], 'L0_attn_Wu_v_b': _L0_attn_in['Wu_v_b'], 'L0_attn_Wo_w': _L0_attn_in['Wo_w'], 'L0_attn_Wo_b': _L0_attn_in['Wo_b'], 'L0_ffn_gate_w': _L0_ffn_in['gate_w'], 'L0_ffn_ln_gamma': _L0_ffn_in['ln_gamma'], 'L0_ffn_ln_beta': _L0_ffn_in['ln_beta'], 'L0_ffn_fc1s': _L0_ffn_in['fc1s'], 'L0_ffn_b1s': _L0_ffn_in['b1s'], 'L0_ffn_fc2s': _L0_ffn_in['fc2s'], 'L0_ffn_b2s': _L0_ffn_in['b2s']}
    _x0 = _d['L0_attn_x']
    _d['L0_attn_x'] = jax.random.normal(jax.random.fold_in(jax.random.key(seed), 1), (4, 1024, 256), dtype=_x0.dtype)
    del _x0
    return _d

def reference(L0_attn_x, L0_attn_Wd_q_w, L0_attn_Wd_q_b, L0_attn_Wu_q_w, L0_attn_Wu_q_b, L0_attn_Wq_r_w, L0_attn_Wq_r_b, L0_attn_Wk_r_w, L0_attn_Wk_r_b, L0_attn_Wd_kv_w, L0_attn_Wd_kv_b, L0_attn_Wu_k_w, L0_attn_Wu_k_b, L0_attn_Wu_v_w, L0_attn_Wu_v_b, L0_attn_Wo_w, L0_attn_Wo_b, L0_ffn_gate_w, L0_ffn_ln_gamma, L0_ffn_ln_beta, L0_ffn_fc1s, L0_ffn_b1s, L0_ffn_fc2s, L0_ffn_b2s):

    def _L0_attn_ref(x, Wd_q_w, Wd_q_b, Wu_q_w, Wu_q_b, Wq_r_w, Wq_r_b, Wk_r_w, Wk_r_b, Wd_kv_w, Wd_kv_b, Wu_k_w, Wu_k_b, Wu_v_w, Wu_v_b, Wo_w, Wo_b):
        import jax, jax.numpy as jnp
        import numpy as np
        NUM_HEAD = 16
        D_Q = 128
        D_KV = 128
        ROPE_BASE = 10000.0

        def _cos_sin(seq_len, dim):
            pos = jnp.arange(seq_len, dtype=jnp.float32)[:, None]
            ids = jnp.arange(dim // 2, dtype=jnp.float32)
            theta = ROPE_BASE ** (-2.0 * ids) / (dim // 2)
            r = pos * theta[None, :]
            return (jnp.cos(r), jnp.sin(r))

        def _rope(x, cos, sin):
            b, s, d = x.shape
            xv = x.reshape(b, s, d // 2, 2)
            x0, x1 = (xv[..., 0], xv[..., 1])
            out = jnp.stack([x0 * cos - x1 * sin, x1 * cos + x0 * sin], axis=-1)
            return out.reshape(b, s, d)
        b, s, d_model = x.shape
        h = NUM_HEAD
        hd = d_model // h
        scale = jnp.sqrt(jnp.float32(h + D_KV + D_Q))

        def heads(t):
            return t.reshape(b, s, h, hd).transpose(0, 2, 1, 3)
        cos, sin = _cos_sin(s, d_model)
        ct_q = x @ Wd_q_w + Wd_q_b
        qt_c = heads(ct_q @ Wu_q_w + Wu_q_b)
        qt_r = heads(_rope(ct_q @ Wq_r_w + Wq_r_b, cos, sin))
        query = qt_c + qt_r
        ct_kv = x @ Wd_kv_w + Wd_kv_b
        kt_c = heads(ct_kv @ Wu_k_w + Wu_k_b)
        kt_r = heads(_rope(x @ Wk_r_w + Wk_r_b, cos, sin))
        key = kt_c + kt_r
        value = heads(ct_kv @ Wu_v_w + Wu_v_b)
        attn = jnp.einsum('bhqd,bhkd->bhqk', query, key) / scale
        attn = jax.nn.softmax(attn, axis=-1)
        out = jnp.einsum('bhqk,bhkd->bhqd', attn, value)
        out = out.transpose(0, 2, 1, 3).reshape(b, s, d_model)
        return out @ Wo_w + Wo_b

    def _L0_ffn_ref(x, gate_w, ln_gamma, ln_beta, fc1s, b1s, fc2s, b2s):
        import jax, jax.numpy as jnp
        import numpy as np
        EMBED_DIM = 256
        MLP_RATIO = 4
        NUM_EXPERTS = 8
        CAPACITY = 1.0
        LN_EPS = 1e-05

        def _layernorm(y, gamma, beta):
            mu = jnp.mean(y, axis=-1, keepdims=True)
            var = jnp.mean(jnp.square(y - mu), axis=-1, keepdims=True)
            return (y - mu) * jax.lax.rsqrt(var + LN_EPS) * gamma + beta
        og_shape = x.shape
        d = og_shape[-1]
        xf = x.reshape(-1, d)
        bs = xf.shape[0]
        n = gate_w.shape[0]
        k = int(bs * CAPACITY) // n
        scores = xf @ gate_w.T
        scores = (jnp.tanh(scores) + 1.0) * 0.5
        vals, idx = jax.lax.top_k(scores.T, k)
        kept_w = vals.T
        flat_idx = idx.T.reshape(-1)
        y = xf[flat_idx].reshape(k, n, d)
        y = _layernorm(y, ln_gamma, ln_beta)
        h = jnp.einsum('knd,nfd->knf', y, fc1s) + b1s
        h = jax.nn.gelu(h, approximate=True)
        o = jnp.einsum('knf,ndf->knd', h, fc2s) + b2s
        o = o * kept_w[:, :, None]
        out = xf.at[flat_idx].add(o.reshape(k * n, d))
        return out.reshape(og_shape)
    x = L0_attn_x
    xn = _layernorm(x, axis=-1)
    x = x + _L0_attn_ref(xn, L0_attn_Wd_q_w, L0_attn_Wd_q_b, L0_attn_Wu_q_w, L0_attn_Wu_q_b, L0_attn_Wq_r_w, L0_attn_Wq_r_b, L0_attn_Wk_r_w, L0_attn_Wk_r_b, L0_attn_Wd_kv_w, L0_attn_Wd_kv_b, L0_attn_Wu_k_w, L0_attn_Wu_k_b, L0_attn_Wu_v_w, L0_attn_Wu_v_b, L0_attn_Wo_w, L0_attn_Wo_b) + _L0_ffn_ref(xn, L0_ffn_gate_w, L0_ffn_ln_gamma, L0_ffn_ln_beta, L0_ffn_fc1s, L0_ffn_b1s, L0_ffn_fc2s, L0_ffn_b2s)
    return x

_drawn_inputs = setup_inputs


def setup_inputs(seed=0):
    import zlib

    import numpy as np

    out = dict(_drawn_inputs(seed))
    spreads = {'L0_attn_Wd_q_b': (0.0, 0.8),
     'L0_attn_Wu_q_b': (0.0, 0.8),
     'L0_attn_Wq_r_b': (0.0, 0.8),
     'L0_attn_Wk_r_b': (0.0, 2.0),
     'L0_attn_Wd_kv_b': (0.0, 0.8),
     'L0_attn_Wu_k_b': (0.0, 2.0),
     'L0_attn_Wu_v_b': (0.0, 0.514),
     'L0_attn_Wo_b': (0.0, 0.439),
     'L0_ffn_ln_gamma': (1.0, 0.6),
     'L0_ffn_ln_beta': (0.0, 0.323)}
    factors = {'L0_attn_Wd_q_w': 8.0,
     'L0_attn_Wu_q_w': 8.0,
     'L0_attn_Wq_r_w': 8.0,
     'L0_attn_Wk_r_w': 8.0,
     'L0_attn_Wd_kv_w': 8.0,
     'L0_attn_Wu_k_w': 8.0,
     'L0_attn_Wu_v_w': 8.0,
     'L0_attn_Wo_w': 3.665,
     'L0_ffn_b1s': 28.939,
     'L0_ffn_b2s': 7.583}
    for name, (base, spread) in spreads.items():
        noise = np.random.default_rng([zlib.crc32(name.encode()), seed]).standard_normal(out[name].shape)
        drawn = base * np.exp(spread * noise) if base else spread * noise
        out[name] = jnp.asarray(drawn.astype(out[name].dtype))
    for name, factor in factors.items():
        out[name] = (out[name] * factor).astype(out[name].dtype)
    return out
```

```python
from contextlib import ExitStack

import numpy as np
import concourse.bass as bass
from concourse import mybir

F32 = mybir.dt.float32
BF16 = mybir.dt.bfloat16
I32 = mybir.dt.int32
U32 = mybir.dt.uint32
ALU = mybir.AluOpType
ACT = mybir.ActivationFunctionType
AX = mybir.AxisListType

P = 128
B, S, D = 4, 1024, 256
TOK = B * S
H, HD = 16, 16
LAT = 128
SCALE = float(np.float32(1.0) / np.sqrt(np.float32(H + LAT + LAT)))
E, FF = 8, 1024
KEEP = TOK // E
EPS = 1e-5
CH = 512
NCH = TOK // CH
TPC = CH // P
NT = TOK // P
KB = D // P
ROW = D + E
RUN = TOK // 16
G4 = 4
NG = H // G4
KT = S // P
QT = S // P
VW = HD + 1
ARENA = 18688
TERMS = 6
PAIR = HD // 2
KROWS = TERMS * HD
AUG = KROWS + 3
BISECT = 26
LO, HI = 32, 16


def rope_tables():
    pos = np.arange(S, dtype=np.float32)[:, None]
    ids = np.arange(D // 2, dtype=np.float32)
    theta = (np.float32(10000.0) ** (np.float32(-2.0) * ids)) / np.float32(D // 2)
    r = (pos * theta[None, :].astype(np.float32)).astype(np.float32)
    return np.cos(r).T.astype(np.float32), -np.sin(r).T.astype(np.float32), np.sin(r).T.astype(np.float32)


def constants():
    i = np.arange(P)
    same = i[:, None] // 16 == i[None, :] // 16
    parts = [np.eye(P), same, same & (i[:, None] < i[None, :]), np.tile(np.arange(LO), (P, 1)), i[:, None]]
    return np.ascontiguousarray(np.concatenate([p.astype(np.float32) for p in parts] + list(rope_tables()), 1))


class Chain:

    def __init__(self, eng, sem):
        self.eng, self.sem, self.base, self.k = eng, sem, 0, 0

    def start(self, base):
        self.base, self.k = base, 0

    def __call__(self, ins):
        ins.then_inc(self.sem, 1)
        self.k += 1
        self.eng.wait_ge(self.sem, self.base + self.k)

    def end(self, n):
        assert self.k == n, (self.k, n)
        return self.base + n


SLOTS = 3
MAXES = 2 * G4 * QT
AHEAD = 12


def side_stream(g, first, last):
    steps = G4 * KT
    more = [] if last and g == NG - 1 else [("max", n, 1) for n in range(AHEAD, MAXES)]
    late = [("neg",)] if more else []
    if not (last and g >= NG - 2):
        late = [("max", 0, 2), ("max", 1, 2)] + late + [("max", n, 2) for n in range(2, AHEAD)]
    early = [] if first and g == 0 else [("norm", 0), ("norm", 1)]
    if g == 0 and not first:
        early += more[16:18] + [("turn", n) for n in range(4)]
        seq = more[:16] + early + more[18:] + late
    else:
        if g == 1 and not first:
            early += [("out", n) for n in range(4)]
        seq = more[:16] + early + more[16:] + late
    begin = 0 if more else 8
    busy = steps - begin - (0 if len(late) > 1 or not more else AHEAD // 2)
    out = [[[] for _ in range(SLOTS)] for _ in range(steps)]
    per = len(seq) / busy
    at = 0
    for st in range(begin, steps):
        take = min(len(seq), int(per * (st - begin + 1) + 1e-6)) - at
        places = {0: [], 1: [2], 2: [1, 2], 3: [0, 1, 2]}[take]
        for p in places:
            out[st][p].append(seq[at])
            at += 1
    assert at == len(seq)
    return out


def uses(first, last):
    return [sum(len(p) for st in side_stream(g, first, last) for p in st) for g in range(NG)]


def program(nc, x, wdq, wdkv, wuq, wqr, wkr, wuk, wuv, wo, cols, buv, bo, gate, fc1, b1, fc2, b2, const,
            acc, table, qk, out):
    ctx = ExitStack()
    with ctx:
        def sb(name, shape, dt=F32):
            return ctx.enter_context(nc.sbuf_tensor(name, shape, dt))

        def sem(name):
            return ctx.enter_context(nc.semaphore(name))

        consts = sb("consts", [P, 3 * P + LO + 1 + 3 * S])
        ident, same, before = (consts[:, n * P:(n + 1) * P] for n in range(3))
        ramp = consts[:, 3 * P:3 * P + LO]
        part_id = consts[:, 3 * P + LO:3 * P + LO + 1]
        cos, nsin, sin = (consts[:, 3 * P + LO + 1 + n * S:3 * P + LO + 1 + (n + 1) * S] for n in range(3))
        w_dq = sb("w_dq", [P, KB, LAT])
        w_dkv = sb("w_dkv", [P, KB, LAT])
        w_uq = sb("w_uq", [P, D])
        w_qr = sb("w_qr", [P, D])
        w_kr = sb("w_kr", [P, KB, D])
        w_uk = sb("w_uk", [P, D])
        w_uv = sb("w_uv", [P, D])
        w_o = sb("w_o", [P, KB, D])
        w_gate = sb("w_gate", [P, KB, E])
        col = sb("col", [P, 14])
        b_dq, b_dkv = col[:, 0:1], col[:, 1:2]
        b_uq, b_qr, b_kr, b_uk, gamma, beta = ([col[:, n:n + 1], col[:, n + 1:n + 2]] for n in range(2, 14, 2))
        b_uv = sb("b_uv", [P, D])
        b_o = sb("b_o", [P, D])
        V = sb("V", [P, NT, H, VW])
        Vg = sb("Vg", [P, 2, KT, G4, VW])
        marks = sb("marks", [P, RUN])
        idx = sb("idx", [P, E, 4], U32)
        scores = sb("scores", [P, RUN])
        minus_half = sb("minus_half", [P, TPC])
        eps = sb("eps", [P, TPC])
        held = sb("held", [P, 1])
        ones = sb("ones", [P, RUN])
        thr = sb("thr", [P, 1])
        step = sb("step", [P, 1])
        cand = sb("cand", [P, 1])
        cnt = sb("cnt", [P, 1])
        stat = sb("stat", [P, 2, TPC, 6])
        mv = sb("mv", [P, 2, 2, TPC, 2])
        rstd = sb("rstd", [P, 2, 2, TPC])
        ve = sb("ve", [P, 2, 2, TPC])
        small = sb("small", [P, 16])

        expP = sb("expP", [P, 2, G4, S])
        flat = expP[:, :, :, :].rearrange("p a h s -> p (a h s)")
        fc1_s = [flat[:, n * 4096:n * 4096 + 2048].rearrange("p (k f) -> p k f", k=KB) for n in range(2)]
        fc2_s = [flat[:, n * 4096 + 2048:(n + 1) * 4096].rearrange("p (k d) -> p k d", k=FF // P) for n in range(2)]
        logits = flat[0:E, 4096:4096 + TOK]
        qkbuf = sb("qkbuf", [P, 2, 2, G4, S], BF16)
        tu = qkbuf[:, :, :, :, :].rearrange("p a b h s -> p (a b h s)").bitcast(F32)
        tu = tu.rearrange("p (c o w e t) -> p c o w e t", c=2, o=2, w=2, e=2)
        arena = sb("arena", [P, ARENA])
        at = [0]

        def view(n, dt=F32):
            a = arena[:, at[0]:at[0] + n]
            at[0] += n
            assert at[0] <= ARENA, at[0]
            return a if dt == F32 else a.bitcast(dt)

        xnT = view(KB * TOK).rearrange("p (k t) -> p k t", k=KB)
        after_xnT = at[0]
        xs = view(2 * TPC * D).rearrange("p (c t d) -> p c t d", c=2, t=TPC)
        xn = view(2 * TPC * D).rearrange("p (c t d) -> p c t d", c=2, t=TPC)
        rows = view(2 * TPC * D).rearrange("p (c t d) -> p c t d", c=2, t=TPC)
        base = view(2 * TPC * D).rearrange("p (c t d) -> p c t d", c=2, t=TPC)
        at[0] = after_xnT
        full = view(2 * 2 * 2 * CH).rearrange("p (c o e t) -> p c o e t", c=2, o=2, e=2)
        parts = view(2 * 2 * 3 * CH, BF16).rearrange("p (c o r e t) -> p c o r e t", c=2, o=2, r=3, e=2)
        latents = Vg[:, :, :, :, :].rearrange("p a k h d -> p (a k h d)")
        ctq, ctkv = latents[:, 0:CH], latents[:, CH:2 * CH]
        at[0] = 0
        oh_lo = view(NT * E * LO // 2, BF16).rearrange("p (t e l) -> p t e l", t=NT, e=E)
        oh_hi = view(NT * E * 2 * HI // 2, BF16).rearrange("p (t e w l) -> p t e w l", t=NT, e=E, w=2)
        gt = view(RUN)
        eq = view(RUN)
        rank = view(RUN)
        taken = view(RUN)
        pos = view(RUN)
        posi = view(RUN, I32).rearrange("p (t e) -> p t e", t=NT)
        loi = view(RUN, I32).rearrange("p (t e) -> p t e", t=NT)
        hii = view(RUN, I32).rearrange("p (t e) -> p t e", t=NT)
        lof = view(RUN).rearrange("p (t e) -> p t e", t=NT)
        hif = view(RUN).rearrange("p (t e) -> p t e", t=NT)
        wtok = view(RUN).rearrange("p (t e) -> p t e", t=NT)
        tok = view(E * 2 * HI).rearrange("p (e w l) -> p e w l", e=E, w=2)
        idx32 = view(E * HI, U32).rearrange("p (e l) -> p e l", e=E)
        at[0] = 0
        hT = view(FF // P * KEEP).rearrange("p (f s) -> p f s", f=FF // P)
        yT = view(KB * KEEP).rearrange("p (k s) -> p k s", k=KB)
        got = view(2 * 4 * ROW).rearrange("p (c s r) -> p c s r", c=2, s=4)
        wsel = view(2 * 4).rearrange("p (c s) -> p c s", c=2)
        res = view(2 * 4 * D).rearrange("p (c s d) -> p c s d", c=2, s=4)
        b2_s = view(2 * D).rearrange("p (c d) -> p c d", c=2)
        b1_s = view(2 * FF // P).rearrange("p (c f) -> p c f", c=2)
        hmax = view(2 * MAXES).rearrange("p (c n) -> p c n", c=2)
        nmax = view(G4 * QT)
        rsum = view(2 * 16).rearrange("p (c t h) -> p c t h", c=2, t=4)
        nrest = view(P)[0:G4 * QT, :]
        nparts = view(3 * P // 2, BF16)[0:G4 * QT, :].rearrange("p (r q) -> p r q", r=3)
        assert at[0] <= ARENA - 2 * 4096, at[0]
        at[0] = 0
        accb = view(QT * D).rearrange("p (t d) -> p t d", t=QT)
        outs = view(QT * D).rearrange("p (t d) -> p t d", t=QT)
        O = view(QT * D).rearrange("p (t d) -> p t d", t=QT)
        OT = view(KB * S).rearrange("p (k t) -> p k t", k=KB)
        pvs = view(S)
        qkb = [qkbuf[:, n, :, :, :] for n in range(2)]
        qkb += [arena[:, ARENA - (2 - n) * 4096:ARENA - (1 - n) * 4096].bitcast(BF16).rearrange("p (o h s) -> p o h s", o=2, h=G4)
                for n in range(2)]

        PS = ctx.enter_context(nc.psum_tensor("PS", [P, 8, 512], F32))

        names = """w_in x_in0 x_in1 mv_done rstd_done xn_done rows_done base_done xnT_ready xnT_done lg_ready lg_done
            acc_out0 acc_out1 tab_out0 tab_out1 s_in tanh_done
            cnt_ready cnt_sum ct_ready ct_done kr_ready qr_ready qc_ready kc_ready v_ready kr_done qr_done qc_done
            kc_done v_done added cast1 cast2 resid parts_done qk_out0 qk_out1 parts_free res_free
            sum_ready sums_done pos_ready pos_done oh_done hi_done tok_ready tok_done idx_in wcol_ready wcol_done wcol_out
            fc_in0 fc_in1 got_in0 got_in1 wsel_done yT_ready yT_done hT_ready hT_done o_ready o_done o_out0 o_out1
            qk_in0 qk_in1 qk_in2 qk_in3 aug_in ones_rows_done side_ready side_done nmax_done sc_ready exp_done pv_half pv_ready pv_done
            vg_done accb_in accb_done out_out ones_done dve_chain pool_chain""".split()
        s = {n: sem(n) for n in names}

        block = ctx.enter_context(nc.Block())

        PER_EXPERT = MAXES // E
        lead_uses = [("max", 0, 2), ("max", 1, 2), ("neg",)] + [("max", n, 2) for n in range(2, AHEAD)]
        LEAD = MAXES + len(lead_uses)
        U_FIRST, U_MID = sum(uses(True, False)), sum(uses(False, False))

        def side_base(b):
            if isinstance(b, int):
                return LEAD if b == 0 else LEAD + U_FIRST + (b - 1) * U_MID
            return b * U_MID + (LEAD + U_FIRST - U_MID)

        assert LEAD % 2 == 1 and U_FIRST % 2 == 0 and U_MID % 2 == 0

        def flat_stream(g, first, last):
            return [u for st in side_stream(g, first, last) for p in st for u in p]

        def before_group(g, first, last):
            return sum(uses(first, last)[:g])

        def at_neg(g, first, last):
            return before_group(g, first, last) + flat_stream(g, first, last).index(("neg",)) + 1

        TAIL = side_base(B - 1) + sum(uses(False, True))
        tail_uses = [("norm", 0), ("norm", 1)] + [("turn", n) for n in range(4)] + [("out", n) for n in range(4)]

        @block.sync
        def _(sp):
            x_c = x.rearrange("(c t p) d -> c p t d", p=P, t=TPC)
            acc_c = acc.rearrange("(c t p) d -> c p t d", p=P, t=TPC)
            tab_c = table[:, 0:D].rearrange("(c t p) d -> c p t d", p=P, t=TPC)
            sp.sem_inc(s["parts_free"], 2)
            for c in range(2):
                sp.dma_start(xs[:, c, :, :], x_c[c, :, :, :]).then_inc(s[f"x_in{c}"], 16)
            loads = [(consts[:, :], const), (col[:, :], cols), (w_gate[:, :, :], gate.rearrange("(k p) e -> p k e", p=P)),
                     (w_dq[:, :, :], wdq.rearrange("(k p) m -> p k m", p=P)), (w_dkv[:, :, :], wdkv.rearrange("(k p) m -> p k m", p=P)),
                     (w_uq[:, :], wuq), (w_qr[:, :], wqr), (w_kr[:, :, :], wkr.rearrange("(k p) m -> p k m", p=P)),
                     (w_uk[:, :], wuk), (w_uv[:, :], wuv), (w_o[:, :, :], wo.rearrange("(k p) m -> p k m", p=P)),
                     (b_uv[:, :], buv.partition_broadcast(P)), (b_o[:, :], bo.partition_broadcast(P))]
            for dst, src in loads:
                sp.dma_start(dst, src).then_inc(s["w_in"], 16)

            def norm_chunk(b, cc, load):
                c = b * 2 + cc
                sp.wait_ge(s["base_done"], c + 3)
                sp.dma_start(acc_c[bass.ds(c, 1), :, :, :].rearrange("c p t d -> (c p) t d"), base[:, cc, :, :]).then_inc(s[f"acc_out{cc}"], 16)
                sp.wait_ge(s["rows_done"], c + 1)
                sp.dma_start(tab_c[bass.ds(c, 1), :, :, :].rearrange("c p t d -> (c p) t d"), rows[:, cc, :, :]).then_inc(s[f"tab_out{cc}"], 16)
                if load:
                    sp.wait_ge(s[f"acc_out{cc}"], b * 16 + 16)
                    sp.wait_ge(s[f"tab_out{cc}"], b * 16 + 16)
                    sp.dma_start(xs[:, cc, :, :], x_c[bass.ds(c + 2, 1), :, :, :].rearrange("c p t d -> (c p) t d")).then_inc(s[f"x_in{cc}"], 16)

            with sp.Fori(0, NCH // 2 - 1) as b:
                for cc in range(2):
                    norm_chunk(b, cc, True)
            for cc in range(2):
                norm_chunk(NCH // 2 - 1, cc, False)
            sp.wait_ge(s["lg_done"], NCH + 2)
            sp.dma_start(scores[:, :], logits.rearrange("e (r t) -> e r t", t=RUN)).then_inc(s["s_in"], 16)

            def load_expert(e, cc):
                sem_in = s[f"fc_in{cc}"]
                one = bass.ds(e, 1)
                sp.dma_start(fc1_s[cc], fc1[one, :, :].rearrange("e (k p) f -> p (e k) f", p=P)).then_inc(sem_in, 16)
                sp.dma_start(fc2_s[cc], fc2[one, :, :].rearrange("e (k p) d -> p (e k) d", p=P)).then_inc(sem_in, 16)

            def load_biases(e, cc):
                sem_in = s[f"fc_in{cc}"]
                one = bass.ds(e, 1)
                sp.dma_start(b1_s[:, cc, :], b1[one, :, :].rearrange("e p f -> (e p) f")).then_inc(sem_in, 16)
                sp.dma_start(b2_s[:, cc, :], b2[one, :].rearrange("e d -> (e d)").partition_broadcast(P)).then_inc(sem_in, 16)

            load_expert(0, 0)
            sp.wait_ge(s["s_in"], 16)
            load_expert(1, 1)

            with sp.Fori(0, NCH // 2) as b:
                for cc in range(2):
                    sp.wait_ge(s["parts_done"], (b * 2 + cc) * 2 + 6)
                    for o in range(2):
                        for r in range(3):
                            for eo in range(2):
                                dst = qk[o, bass.ds(b, 1), eo, :, r, :, cc * CH:(cc + 1) * CH].rearrange("b h j t -> (b h) j t")
                                sp.dma_start(dst, parts[:, cc, o, r, eo, :]).then_inc(s[f"qk_out{cc}"], 16)
                    sp.wait_ge(s[f"qk_out{cc}"], b * 192 + 192)
                    sp.sem_inc(s["parts_free"], 1)

            def load_qk(b, g):
                sem_in = s[f"qk_in{g}"]
                for eo in range(2):
                    row = eo * KROWS // 2
                    for n0, n in ((0, 3), (3, 2), (5, 1)):
                        src = qk[0, bass.ds(b, 1), eo, g * G4:(g + 1) * G4, 0:n, :, :].rearrange("b h r j t -> (b r j) h t")
                        lo = row + n0 * PAIR
                        sp.dma_start(qkb[g][lo:lo + n * PAIR, 0, :, :], src).then_inc(sem_in, 16)
                    for n, part in enumerate((0, 0, 0, 1, 1, 2)):
                        src = qk[1, bass.ds(b, 1), eo, g * G4:(g + 1) * G4, part, :, :].rearrange("b h j t -> (b j) h t")
                        lo = row + n * PAIR
                        sp.dma_start(qkb[g][lo:lo + PAIR, 1, :, :], src).then_inc(sem_in, 16)

            for c in range(2):
                sp.wait_ge(s[f"qk_out{c}"], 192 * (NCH // 2))
            sp.wait_ge(s["parts_done"], 2 * NCH + 4)
            for g in range(2):
                load_qk(0, g)

            sp.wait_ge(s["wcol_done"], 1)
            with nc.allow_non_contiguous_dma(reason="eight scores of a token"):
                sp.dma_start(table[:, D:ROW].rearrange("(t p) e -> p t e", p=P), wtok).then_inc(s["wcol_out"], 16)
            sp.wait_ge(s["tok_done"], 1)
            for q in range(4):
                sp.dma_start(idx[LO * q:LO * (q + 1), :, :], idx32[0:LO, :, 4 * q:4 * q + 4]).then_inc(s["idx_in"], 16)

            sp.wait_ge(s["idx_in"], 64)
            load_biases(0, 0)
            load_biases(1, 1)
            for g in range(2, NG):
                load_qk(0, g)

            with sp.Fori(0, E // 2 - 1) as h:
                for cc in range(2):
                    sp.wait_ge(s["o_ready"], h * 2 + cc + 2)
                    sp.wait_ge(s["o_done"], h * 2 + cc + 2)
                    load_expert(h * 2 + cc + 2, cc)
                    load_biases(h * 2 + cc + 2, cc)

            def load_aug(g, count):
                sp.wait_ge(s["side_done"], count)
                for part in range(3):
                    sp.dma_start(qkb[g][KROWS + part:KROWS + part + 1, 0, :, :].rearrange("p h (t q) -> p (h t) q", q=P),
                                 nparts[:, part, :]).then_inc(s["aug_in"], 16)

            load_aug(0, MAXES + 3)

            def attend_row(b, first, last):
                for g in range(NG):
                    if g == 0 and not first:
                        sp.dma_start(accb, acc[bass.ds((b - 1) * S, S), :].rearrange("(t p) d -> p t d", p=P)).then_inc(s["accb_in"], 16)
                    if g == 2 and not first:
                        sp.wait_ge(s["side_done"], side_base(b) + before_group(2, first, last))
                        sp.dma_start(out[bass.ds((b - 1) * S, S), :].rearrange("(t p) d -> p t d", p=P), outs).then_inc(s["out_out"], 16)
                    if not (last and g == NG - 1):
                        load_aug((g + 1) % NG, side_base(b) + at_neg(g, first, last))
                    if g == 3 and not first:
                        sp.wait_ge(s["out_out"], b * 16)
                    if not last:
                        sp.wait_ge(s["sc_ready"], (b * NG + g + 1) * (G4 * KT))
                        load_qk(b + 1, g)

            for c in range(2):
                sp.wait_ge(s[f"o_out{c}"], 64 * E // 2)
            attend_row(0, True, False)
            with sp.Fori(1, B - 1) as b:
                attend_row(b, False, False)
            attend_row(B - 1, False, True)
            sp.dma_start(accb, acc[(B - 1) * S:B * S, :].rearrange("(t p) d -> p t d", p=P)).then_inc(s["accb_in"], 16)
            sp.wait_ge(s["side_done"], TAIL + len(tail_uses))
            sp.dma_start(out[(B - 1) * S:B * S, :].rearrange("(t p) d -> p t d", p=P), outs).then_inc(s["out_out"], 16)
            sp.wait_ge(s["out_out"], 16 * B)
            for c in range(2):
                sp.wait_ge(s[f"acc_out{c}"], 16 * (NCH // 2))
                sp.wait_ge(s[f"tab_out{c}"], 16 * (NCH // 2))

        @block.gpsimd
        def _(pool):
            chain = Chain(pool, s["pool_chain"])
            nc.gpsimd.memset(minus_half[:, :], -0.5)
            nc.gpsimd.memset(eps[:, :], EPS)
            nc.gpsimd.memset(ones[:, :], 1.0)
            nc.gpsimd.memset(V[:, :, :, HD:VW], 1.0).then_inc(s["ones_done"], 1)
            pool.wait_ge(s["ones_done"], 1)
            pool.sem_inc(s["base_done"], 2)
            pool.sem_inc(s["parts_done"], 4)

            def rsqrt(cc, which):
                chain(nc.gpsimd.tensor_tensor(out=ve[:, cc, which, :], in0=mv[:, cc, which, :, 1], in1=eps[:, :], op=ALU.add))
                nc.gpsimd.tensor_tensor(out=rstd[:, cc, which, :], in0=ve[:, cc, which, :], in1=minus_half[:, :],
                                        op=ALU.pow).then_inc(s["rstd_done"], 1)

            with pool.Fori(0, NCH // 2) as b:
                for cc in range(2):
                    c = b * 2 + cc
                    chain.start(c * 2)
                    pool.wait_ge(s["mv_done"], c * 2 + 1)
                    rsqrt(cc, 0)
                    pool.wait_ge(s["mv_done"], c * 2 + 2)
                    rsqrt(cc, 1)
                    pool.wait_ge(s["xn_done"], c + 1)
                    nc.gpsimd.tensor_tensor(out=base[:, cc, :, :], in0=xs[:, cc, :, :], in1=xn[:, cc, :, :],
                                            op=ALU.add).then_inc(s["base_done"], 1)
                    chain.end(2)

            with pool.Fori(0, NCH // 2) as b:
                for cc in range(2):
                    c = b * 2 + cc
                    for o, done in ((0, "qc_done"), (1, "kc_done")):
                        pool.wait_ge(s[done], c + 1 + (o == 1))
                        nc.gpsimd.tensor_tensor(out=full[:, cc, o, :, :], in0=full[:, cc, o, :, :], in1=tu[:, cc, o, 1, :, :],
                                                op=ALU.add).then_inc(s["added"], 1)
                    for o in range(2):
                        pool.wait_ge(s["cast1"], c * 2 + o + 1)
                        nc.gpsimd.tensor_tensor(out=full[:, cc, o, :, :], in0=full[:, cc, o, :, :], in1=parts[:, cc, o, 0, :, :],
                                                op=ALU.subtract).then_inc(s["resid"], 1)
                    for o in range(2):
                        pool.wait_ge(s["cast2"], c * 2 + o + 1)
                        nc.gpsimd.tensor_tensor(out=parts[:, cc, o, 2, :, :], in0=full[:, cc, o, :, :], in1=parts[:, cc, o, 1, :, :],
                                                op=ALU.subtract).then_inc(s["parts_done"], 1)

            pool.wait_ge(s["oh_done"], 1)
            chain.start(2 * NCH)
            wide = [P, NT, E, HI]
            chain(nc.gpsimd.tensor_tensor(out=oh_hi[:, :, :, 1, :], in0=oh_hi[:, :, :, 0, :],
                                          in1=ramp[:, 0:NT].unsqueeze(2).unsqueeze(3).broadcast_to(wide), op=ALU.mult))
            nc.gpsimd.tensor_scalar(oh_hi[:, :, :, 0, :], oh_hi[:, :, :, 0, :], part_id, None, ALU.mult).then_inc(s["hi_done"], 1)

            def gather(e):
                cc = e % 2
                if e >= 2:
                    pool.wait_ge(s["yT_ready"], e - 1)
                    pool.wait_ge(s["wsel_done"], e - 1)
                for sl in range(4):
                    nc.gpsimd.indirect_dma_start(got[:, cc, sl, :], None, table,
                                                 bass.IndirectOffsetOnAxis(ap=idx[:, e, sl:sl + 1], axis=0)).then_inc(s[f"got_in{cc}"], 16)

            for c in range(2):
                pool.wait_ge(s[f"tab_out{c}"], 16 * (NCH // 2))
                pool.wait_ge(s[f"acc_out{c}"], 16 * (NCH // 2))
            pool.wait_ge(s["wcol_out"], 16)
            pool.wait_ge(s["idx_in"], 64)
            pool.sem_inc(s["res_free"], 2)
            gather(0)
            gather(1)
            for c in range(2):
                pool.wait_ge(s[f"qk_out{c}"], 192 * (NCH // 2))
            for g in range(NG):
                nc.gpsimd.memset(qkb[g][KROWS:AUG, 1, :, :], 1.0).then_inc(s["ones_rows_done"], 1)
            pool.wait_ge(s["ones_rows_done"], NG)
            for e in range(E):
                cc = e % 2
                pool.wait_ge(s[f"got_in{cc}"], 64 * (e // 2 + 1))
                if e >= 2:
                    pool.wait_ge(s["o_done"], e)
                nc.gpsimd.tensor_copy(wsel[:, cc, :], got[:, cc, :, D + e]).then_inc(s["wsel_done"], 1)
                if 1 <= e < E - 1:
                    gather(e + 1)
                pool.wait_ge(s["o_done"], e + 2)
                if e >= 1:
                    pool.wait_ge(s[f"o_out{1 - cc}"], 64 * ((e - 1) // 2 + 1))
                    pool.sem_inc(s["res_free"], 1)
                for sl in range(4):
                    nc.gpsimd.indirect_dma_start(acc, bass.IndirectOffsetOnAxis(ap=idx[:, e, sl:sl + 1], axis=0), res[:, cc, sl, :], None,
                                                 compute_op=ALU.add).then_inc(s[f"o_out{cc}"], 16)

            def add_bias(b):
                pool.wait_ge(s["accb_in"], b * 16)
                nc.gpsimd.tensor_tensor(out=accb, in0=accb, in1=b_o[:, :].unsqueeze(1).broadcast_to([P, QT, D]),
                                        op=ALU.add).then_inc(s["accb_done"], 1)

            def values_row(b, first):
                for g in range(NG):
                    if not (first and g < 2):
                        pool.wait_ge(s["pv_ready"], (b * NG + g - 1) * KT)
                    nc.gpsimd.tensor_copy(Vg[:, g % 2, :, :, :], V[:, bass.ds(b * KT, KT), g * G4:(g + 1) * G4, :]).then_inc(s["vg_done"], 1)
                    if g == 0 and not first:
                        add_bias(b)

            pool.wait_ge(s["v_done"], NCH + 1)
            values_row(0, True)
            with pool.Fori(1, B) as b:
                values_row(b, False)
            add_bias(B)

        @block.scalar
        def _(act):
            act.sem_inc(s["xnT_done"], 2)
            act.sem_inc(s["lg_done"], 2)
            with act.Fori(0, NCH // 2) as b:
                for cc in range(2):
                    c = b * 2 + cc
                    act.wait_ge(s["xnT_ready"], c + 3)
                    nc.scalar.activation(xnT[:, :, bass.ds(c * CH, CH)], PS[:, 2 * cc:2 * cc + 2, :], ACT.Copy).then_inc(s["xnT_done"], 1)
                    act.wait_ge(s["lg_ready"], c + 1)
                    nc.scalar.activation(logits[:, bass.ds(c * CH, CH)], PS[0:E, 4 + cc, :], ACT.Copy).then_inc(s["lg_done"], 1)
            act.wait_ge(s["s_in"], 16)
            nc.scalar.activation(scores[:, :], scores[:, :], ACT.Tanh).then_inc(s["tanh_done"], 1)

            for c in range(2):
                act.wait_ge(s[f"tab_out{c}"], 16 * (NCH // 2))
                act.wait_ge(s[f"acc_out{c}"], 16 * (NCH // 2))
            with act.Fori(0, NCH // 2) as b:
                for cc in range(2):
                    c = b * 2 + cc
                    act.wait_ge(s["ct_ready"], c + 1)
                    act.wait_ge(s["v_ready"], c + 1)
                    nc.scalar.activation(ctq, PS[:, 0, :], ACT.Identity, bias=b_dq)
                    nc.scalar.activation(ctkv, PS[:, 1, :], ACT.Identity, bias=b_dkv).then_inc(s["ct_done"], 1)
                    act.wait_ge(s["parts_free"], c + 1)
                    for o in range(2):
                        act.wait_ge(s["added"], c * 2 + o + 1)
                        nc.scalar.activation(parts[:, cc, o, 0, :, :], full[:, cc, o, :, :], ACT.Copy).then_inc(s["cast1"], 1)
                    for o in range(2):
                        act.wait_ge(s["resid"], c * 2 + o + 1)
                        nc.scalar.activation(parts[:, cc, o, 1, :, :], full[:, cc, o, :, :], ACT.Copy).then_inc(s["cast2"], 1)

            with act.Fori(0, E // 2) as h:
                for cc in range(2):
                    e = h * 2 + cc
                    act.wait_ge(s[f"fc_in{cc}"], h * 64 + 64)
                    for f in range(FF // P):
                        act.wait_ge(s["hT_ready"], e * 8 + f + 1)
                        if f == 0:
                            act.wait_ge(s["o_ready"], e + 1)
                        nc.scalar.activation(hT[:, f, :], PS[:, 2 + f % 2, :], ACT.Gelu_apprx_tanh,
                                             bias=b1_s[:, cc, f:f + 1]).then_inc(s["hT_done"], 1)

            def outputs(n, half):
                if half == 0:
                    act.wait_ge(s["pv_half"], n)
                else:
                    act.wait_ge(s["pv_ready"], n * KT)
                nc.scalar.activation(pvs[:, half * 512:(half + 1) * 512], PS[:, 4 + half, :], ACT.Copy).then_inc(s["pv_done"], 1)

            def attend_row(b, first, last):
                for g in range(NG):
                    n = b * NG + g
                    if first and g == 1:
                        for c in range(2):
                            act.wait_ge(s[f"o_out{c}"], 64 * E // 2)
                    for st in range(G4 * KT):
                        kt, j = divmod(st, G4)
                        act.wait_ge(s["sc_ready"], n * (G4 * KT) + st + 1)
                        if not (first and g == 0 and kt < 2):
                            act.wait_ge(s["pv_ready"], n * KT + kt - 1)
                        nc.scalar.activation(expP[:, kt % 2, j, :], PS[:, 2 * (st % 2):2 * (st % 2) + 2, :],
                                             ACT.Exp, scale=SCALE).then_inc(s["exp_done"], 1)
                        if not (first and g == 0) and st in (2, 4):
                            outputs(n, st // 2 - 1)

            attend_row(0, True, False)
            with act.Fori(1, B - 1) as b:
                attend_row(b, False, False)
            attend_row(B - 1, False, True)
            for half in range(2):
                outputs(B * NG, half)

        @block.vector
        def _(dve):
            chain = Chain(dve, s["dve_chain"])
            dve.sem_inc(s["kc_done"], 1)
            dve.sem_inc(s["v_done"], 1)
            dve.sem_inc(s["o_done"], 1)
            chain.start(0)
            nc.vector.memset(thr[:, :], 0.0)
            chain(nc.vector.memset(step[:, :], 1.0))
            chain.end(1)
            NORM = 2

            def stats(src, cc, which):
                for t in range(TPC):
                    last = nc.vector.bn_stats(stat[:, which, t, :], src[:, cc, t, :])
                chain(last)
                nc.vector.memset(held[:, :], 0.0)
                for t in range(TPC):
                    last = nc.vector.bn_aggr(mv[:, cc, which, t, :], stat[:, which, t, :])
                last.then_inc(s["mv_done"], 1)

            with dve.Fori(0, NCH // 2) as b:
                for cc in range(2):
                    c = b * 2 + cc
                    chain.start(c * NORM + 1)
                    dve.wait_ge(s[f"x_in{cc}"], b * 16 + 16)
                    stats(xs, cc, 0)
                    dve.wait_ge(s["mv_done"], c * 2 + 1)
                    dve.wait_ge(s["rstd_done"], c * 2 + 1)
                    dve.wait_ge(s["xnT_ready"], c + 1)
                    dve.wait_ge(s["base_done"], c + 1)
                    for t in range(TPC):
                        last = nc.vector.tensor_scalar(xn[:, cc, t, :], xs[:, cc, t, :], mv[:, cc, 0, t, 0:1], rstd[:, cc, 0, t:t + 1],
                                                       ALU.subtract, ALU.mult)
                    last.then_inc(s["xn_done"], 1)
                    dve.wait_ge(s["xn_done"], c + 1)
                    stats(xn, cc, 1)
                    dve.wait_ge(s["mv_done"], c * 2 + 2)
                    dve.wait_ge(s["rstd_done"], c * 2 + 2)
                    for t in range(TPC):
                        last = nc.vector.tensor_scalar(rows[:, cc, t, :], xn[:, cc, t, :], mv[:, cc, 1, t, 0:1], rstd[:, cc, 1, t:t + 1],
                                                       ALU.subtract, ALU.mult)
                    last.then_inc(s["rows_done"], 1)
                    chain.end(NORM)
            done = 1 + NCH * NORM

            chain.start(done)
            dve.wait_ge(s["tanh_done"], 1)
            chain(nc.vector.tensor_scalar(scores[:, :], scores[:, :], 1.0, 0.5, ALU.add, ALU.mult))

            def probe_start():
                chain(nc.vector.tensor_tensor(out=cand[:, :], in0=thr[:, :], in1=step[:, :], op=ALU.add))
                nc.vector.tensor_scalar(marks[:, :], scores[:, :], cand[:, :], None, ALU.is_ge, ALU.add,
                                        accum_out=cnt[:, :]).then_inc(s["cnt_ready"], 1)

            def probe_end(n):
                dve.wait_ge(s["cnt_sum"], n)
                chain(nc.vector.tensor_scalar(cand[:, :], PS[:, 7, 0:1], float(KEEP), step[:, :], ALU.is_ge, ALU.mult))
                nc.vector.tensor_tensor(out=thr[:, :], in0=thr[:, :], in1=cand[:, :], op=ALU.add)
                chain(nc.vector.tensor_scalar(step[:, :], step[:, :], 0.5, None, ALU.mult))

            PROBE = 3
            lead = BISECT - 3 * NCH
            probe_start()
            for n in range(lead):
                probe_end(n + 1)
                probe_start()
            done = chain.end(2 + lead * PROBE)

            dve.wait_ge(s["w_in"], 16 * 13)
            dve.wait_ge(s["xnT_ready"], NCH + 2)
            dve.wait_ge(s["base_done"], NCH + 2)
            for c in range(2):
                dve.wait_ge(s[f"tab_out{c}"], 16 * (NCH // 2))
                dve.wait_ge(s[f"acc_out{c}"], 16 * (NCH // 2))
            dve.wait_ge(s["ones_done"], 1)
            with dve.Fori(0, NCH // 2) as b:
                for cc in range(2):
                    c = b * 2 + cc
                    chain.start(c * 9 + done)
                    csl = slice(cc * CH, (cc + 1) * CH)

                    def rotate(o, banks, bias):
                        for eo in range(2):
                            nc.vector.scalar_tensor_tensor(out=tu[:, cc, o, 0, eo, :], in0=PS[:, banks[eo], :], scalar=bias[eo],
                                                           in1=cos[:, csl], op0=ALU.add, op1=ALU.mult)
                        for eo, tab in ((1, nsin), (0, sin)):
                            last = nc.vector.scalar_tensor_tensor(out=tu[:, cc, o, 1, 1 - eo, :], in0=PS[:, banks[eo], :], scalar=bias[eo],
                                                                  in1=tab[:, csl], op0=ALU.add, op1=ALU.mult)
                        return last

                    def combine(o, banks, bias):
                        for eo in range(2):
                            last = nc.vector.scalar_tensor_tensor(out=full[:, cc, o, eo, :], in0=PS[:, banks[eo], :], scalar=bias[eo],
                                                                  in1=tu[:, cc, o, 0, eo, :], op0=ALU.add, op1=ALU.add)
                        return last

                    probe_end(c * 3 + lead + 1)
                    probe_start()
                    dve.wait_ge(s["kr_ready"], c + 1)
                    dve.wait_ge(s["parts_done"], c * 2 + 2)
                    rotate(1, (2, 3), b_kr).then_inc(s["kr_done"], 1)
                    probe_end(c * 3 + lead + 2)
                    probe_start()
                    dve.wait_ge(s["qr_ready"], c + 1)
                    rotate(0, (4, 5), b_qr).then_inc(s["qr_done"], 1)
                    dve.wait_ge(s["qr_done"], c + 1)
                    dve.wait_ge(s["kr_done"], c + 1)
                    probe_end(c * 3 + lead + 3)
                    probe_start()
                    dve.wait_ge(s["qc_ready"], c + 1)
                    combine(0, (6, 0), b_uq).then_inc(s["qc_done"], 1)
                    dve.wait_ge(s["kc_ready"], c + 1)
                    combine(1, (1, 2), b_uk).then_inc(s["kc_done"], 1)
                    dve.wait_ge(s["v_ready"], c + 2)
                    for i in range(2):
                        last = nc.vector.tensor_tensor(
                            out=V[:, bass.ds(c * TPC + 2 * i, 2), :, 0:HD],
                            in0=PS[:, 3 + i, :].rearrange("p (t h d) -> p t h d", t=2, h=H),
                            in1=b_uv[:, :].rearrange("p (h d) -> p h d", h=H).unsqueeze(1).broadcast_to([P, 2, H, HD]), op=ALU.add)
                    last.then_inc(s["v_done"], 1)
                    chain.end(9)
            done = done + 9 * NCH

            chain.start(done)
            dve.wait_ge(s["parts_done"], 2 * NCH + 4)
            nc.vector.tensor_scalar(gt, scores[:, :], thr[:, :], None, ALU.is_gt, ALU.add, accum_out=small[:, 0:1])
            nc.vector.tensor_scalar(eq, scores[:, :], thr[:, :], None, ALU.is_equal, ALU.add, accum_out=small[:, 1:2]).then_inc(s["sum_ready"], 1)
            dve.wait_ge(s["sum_ready"], 1)
            chain(nc.vector.tensor_tensor_scan(out=rank, data0=ones[:, :], data1=eq, initial=0.0, op0=ALU.mult, op1=ALU.add))
            dve.wait_ge(s["sums_done"], 1)
            chain(nc.vector.tensor_scalar(small[:, 2:3], PS[:, 7, 1:2], -1.0, float(KEEP), ALU.mult, ALU.add))
            chain(nc.vector.tensor_tensor(out=small[:, 3:4], in0=small[:, 2:3], in1=PS[:, 7, 2:3], op=ALU.subtract))
            chain(nc.vector.scalar_tensor_tensor(out=taken, in0=rank, scalar=small[:, 3:4], in1=eq, op0=ALU.is_le, op1=ALU.mult))
            nc.vector.scalar_tensor_tensor(out=gt, in0=taken, scalar=1.0, in1=gt, op0=ALU.mult, op1=ALU.add,
                                           accum_out=small[:, 4:5]).then_inc(s["sum_ready"], 1)
            dve.wait_ge(s["sum_ready"], 2)
            chain(nc.vector.tensor_tensor_scan(out=rank, data0=ones[:, :], data1=gt, initial=0.0, op0=ALU.mult, op1=ALU.add))
            dve.wait_ge(s["sums_done"], 2)
            chain(nc.vector.tensor_scalar(rank, rank, PS[:, 7, 3:4], -1025.0, ALU.add, ALU.add))
            nc.vector.tensor_tensor(out=pos, in0=rank, in1=gt, op=ALU.mult).then_inc(s["pos_ready"], 1)
            dve.wait_ge(s["wcol_ready"], 1)
            for i in range(2):
                tiles = slice(i, NT, 2)
                nc.vector.tensor_copy(wtok[:, tiles, :], PS[:, 1, i * P:(i + 1) * P].rearrange("p (e r) -> p r e", e=E))
                last = nc.vector.tensor_scalar(posi[:, tiles, :], PS[:, 0, i * P:(i + 1) * P].rearrange("p (e r) -> p r e", e=E),
                                               1024.0, None, ALU.add)
            last.then_inc(s["wcol_done"], 1)
            dve.wait_ge(s["wcol_done"], 1)
            nc.vector.tensor_scalar(loi, posi, LO - 1, None, ALU.bitwise_and)
            chain(nc.vector.tensor_scalar(hii, posi, 5, None, ALU.logical_shift_right))
            nc.vector.tensor_copy(lof, loi)
            nc.vector.tensor_copy(hif, hii).then_inc(s["pos_done"], 1)
            dve.wait_ge(s["pos_done"], 1)
            wide = [P, NT, E, HI]
            nc.vector.tensor_tensor(out=oh_hi[:, :, :, 0, :], in0=hif.unsqueeze(3).broadcast_to(wide),
                                    in1=ramp[:, 0:HI].unsqueeze(1).unsqueeze(1).broadcast_to(wide), op=ALU.is_equal).then_inc(s["oh_done"], 1)
            nc.vector.tensor_tensor(out=oh_lo, in0=lof.unsqueeze(3).broadcast_to([P, NT, E, LO]),
                                    in1=ramp[:, :].unsqueeze(1).unsqueeze(1).broadcast_to([P, NT, E, LO]),
                                    op=ALU.is_equal).then_inc(s["oh_done"], 1)
            dve.wait_ge(s["tok_ready"], 1)
            chain(nc.vector.tensor_copy(tok[0:LO, :, :, :].rearrange("p e w l -> p (e w l)"), PS[0:LO, 0, 0:E * 2 * HI]))
            nc.vector.scalar_tensor_tensor(out=idx32[0:LO, :, :], in0=tok[0:LO, :, 1, :], scalar=float(P), in1=tok[0:LO, :, 0, :],
                                           op0=ALU.mult, op1=ALU.add).then_inc(s["tok_done"], 1)
            done = chain.end(8)

            with dve.Fori(0, E // 2) as h:
                for cc in range(2):
                    e = h * 2 + cc
                    chain.start(e + done)
                    dve.wait_ge(s["yT_ready"], e + 1)
                    for k in range(KB):
                        last = nc.vector.tensor_scalar(yT[:, k, :], PS[:, k, :], gamma[k], beta[k], ALU.mult, ALU.add)
                    last.then_inc(s["yT_done"], 1)
                    for i in range(PER_EXPERT):
                        dve.wait_ge(s["side_ready"], e * PER_EXPERT + i + 1)
                        nc.vector.tensor_reduce(hmax[:, 0, bass.ds(e * PER_EXPERT + i, 1)], PS[:, 6 + i % 2, :], AX.X,
                                                ALU.max).then_inc(s["side_done"], 1)
                    dve.wait_ge(s[f"fc_in{cc}"], h * 64 + 64)
                    dve.wait_ge(s["wsel_done"], e + 1)
                    dve.wait_ge(s["res_free"], e + 1)
                    dve.wait_ge(s["o_ready"], e + 2)
                    chain(nc.vector.tensor_tensor(out=res[:, cc, :, :], in0=PS[:, 4:6, :].rearrange("p a (b d) -> p (a b) d", b=2),
                                                  in1=b2_s[:, cc, :].unsqueeze(1).broadcast_to([P, 4, D]), op=ALU.add))
                    for sl in range(4):
                        last = nc.vector.tensor_scalar(res[:, cc, sl, :], res[:, cc, sl, :], wsel[:, cc, sl:sl + 1], None, ALU.mult)
                    last.then_inc(s["o_done"], 1)
                    chain.end(1)
            done = done + E

            def negate_maxima(which, count):
                dve.wait_ge(s["side_done"], count)
                nc.vector.tensor_reduce(nmax, hmax[:, which, :].rearrange("p (t k) -> p t k", k=2), AX.X, ALU.max, negate=True).then_inc(s["nmax_done"], 1)

            def run_side(seq, count, parity, g, row):
                for k, u in enumerate(seq):
                    bank = 6 + (parity + k) % 2
                    dve.wait_ge(s["side_ready"], count + k + 1)
                    if u[0] == "max":
                        which = (g + u[2]) % 2
                        nc.vector.tensor_reduce(hmax[:, which, u[1]:u[1] + 1], PS[:, bank, :], AX.X, ALU.max).then_inc(s["side_done"], 1)
                        if u == ("max", 0, 2):
                            negate_maxima(1 - which, count + k)
                        elif u[1] == MAXES - 1 and seq[k + 1] == ("neg",):
                            negate_maxima(which, count + k + 1)
                    elif u[0] == "neg":
                        m = PS[0:G4 * QT, bank, 0:P]
                        chain(nc.vector.tensor_copy(nparts[:, 0, :], m))
                        chain(nc.vector.tensor_tensor(out=nrest, in0=m, in1=nparts[:, 0, :], op=ALU.subtract))
                        chain(nc.vector.tensor_copy(nparts[:, 1, :], nrest))
                        nc.vector.tensor_tensor(out=nparts[:, 2, :], in0=nrest, in1=nparts[:, 1, :], op=ALU.subtract).then_inc(s["side_done"], 1)
                    elif u[0] == "norm":
                        half, pg = u[1], (g - 1) % NG
                        o4 = PS[:, bank, :].rearrange("p (t h d) -> p t h d", t=4, h=G4)
                        dst = O[:, half * 4:half * 4 + 4, pg * G4 * HD:(pg + 1) * G4 * HD].rearrange("p t (h d) -> p t h d", h=G4)
                        chain(nc.vector.reciprocal(rsum[:, half, :, :], o4[:, :, :, HD]))
                        nc.vector.tensor_tensor(out=dst, in0=o4[:, :, :, 0:HD], in1=rsum[:, half, :, :].unsqueeze(3).broadcast_to([P, 4, G4, HD]),
                                                op=ALU.mult).then_inc(s["side_done"], 1)
                    elif u[0] == "turn":
                        kb, half = divmod(u[1], 2)
                        nc.vector.tensor_copy(OT[:, kb, half * 512:(half + 1) * 512], PS[:, bank, :]).then_inc(s["side_done"], 1)
                    else:
                        if u[1] == 0:
                            dve.wait_ge(s["accb_done"], row)
                        i = u[1]
                        nc.vector.tensor_tensor(out=outs[:, 2 * i:2 * i + 2, :], in0=PS[:, bank, :].rearrange("p (t d) -> p t d", t=2),
                                                in1=accb[:, 2 * i:2 * i + 2, :], op=ALU.add).then_inc(s["side_done"], 1)

            chain.start(done)
            run_side(lead_uses, MAXES, 0, NG - 1, None)
            done = chain.end(3)

            def chained(first, last):
                kinds = [u[0] for g in range(NG) for u in flat_stream(g, first, last)]
                return 3 * kinds.count("neg") + kinds.count("norm")

            C_FIRST, C_MID, C_LAST = chained(True, False), chained(False, False), chained(False, True)

            def attend_row(b, first, last):
                chain.start(done if first else b * C_MID + (done + C_FIRST - C_MID))
                for g in range(NG):
                    if first and g == 1:
                        for c in range(2):
                            dve.wait_ge(s[f"o_out{c}"], 64 * E // 2)
                    ahead = before_group(g, first, last)
                    run_side(flat_stream(g, first, last), side_base(b) + ahead, 1 + ahead, g, b)
                chain.end(chained(first, last))

            attend_row(0, True, False)
            with dve.Fori(1, B - 1) as b:
                attend_row(b, False, False)
            attend_row(B - 1, False, True)
            chain.start(done + C_FIRST + C_MID * (B - 2) + C_LAST)
            run_side(tail_uses, TAIL, TAIL, 0, B)

        @block.tensor
        def _(pe):
            pe.sem_inc(s["xnT_ready"], 2)
            pe.sem_inc(s["v_ready"], 1)
            pe.sem_inc(s["o_ready"], 1)
            pe.wait_ge(s["w_in"], 16 * 13)
            mm = nc.tensor.matmul
            with pe.Fori(0, NCH // 2) as b:
                for cc in range(2):
                    c = b * 2 + cc
                    pe.wait_ge(s["xn_done"], c + 1)
                    pe.wait_ge(s["xnT_done"], c + 1)
                    for k in range(KB):
                        for t in range(TPC):
                            last = nc.tensor.transpose(PS[:, 2 * cc + k, t * P:(t + 1) * P], xn[:, cc, t, k * P:(k + 1) * P], ident)
                    last.then_inc(s["xnT_ready"], 1)
                    pe.wait_ge(s["xnT_done"], c + 3)
                    pe.wait_ge(s["lg_done"], c + 1)
                    for k in range(KB):
                        last = mm(PS[0:E, 4 + cc, :], w_gate[:, k, :], xnT[:, k, bass.ds(c * CH, CH)], start=k == 0, stop=k == KB - 1)
                    last.then_inc(s["lg_ready"], 1)

            def count(n):
                pe.wait_ge(s["cnt_ready"], n)
                mm(PS[:, 7, 0:1], same, cnt[:, :], start=True, stop=True).then_inc(s["cnt_sum"], 1)

            lead = BISECT - 3 * NCH
            for n in range(lead):
                count(n + 1)
            pe.wait_ge(s["lg_done"], NCH + 2)
            with pe.Fori(0, NCH // 2) as b:
                for cc in range(2):
                    c = b * 2 + cc

                    def xT(k):
                        return xnT[:, k, bass.ds(c * CH, CH)]

                    def single(bank, w, src):
                        return mm(PS[:, bank, :], w, src, start=True, stop=True)

                    pe.wait_ge(s["kc_done"], c + 1)
                    for bank, w in ((0, w_dq), (1, w_dkv)):
                        for k in range(KB):
                            last = mm(PS[:, bank, :], w[:, k, :], xT(k), start=k == 0, stop=k == KB - 1)
                    last.then_inc(s["ct_ready"], 1)
                    pe.wait_ge(s["v_done"], c + 1)
                    for eo in range(2):
                        for k in range(KB):
                            last = mm(PS[:, 2 + eo, :], w_kr[:, k, eo * P:(eo + 1) * P], xT(k), start=k == 0, stop=k == KB - 1)
                    last.then_inc(s["kr_ready"], 1)
                    count(c * 3 + lead + 1)
                    pe.wait_ge(s["ct_done"], c + 1)
                    for eo in range(2):
                        last = single(4 + eo, w_qr[:, eo * P:(eo + 1) * P], ctq)
                    last.then_inc(s["qr_ready"], 1)
                    for eo, bank in ((0, 6), (1, 0)):
                        last = single(bank, w_uq[:, eo * P:(eo + 1) * P], ctq)
                    last.then_inc(s["qc_ready"], 1)
                    count(c * 3 + lead + 2)
                    pe.wait_ge(s["kr_done"], c + 1)
                    for eo, bank in ((0, 1), (1, 2)):
                        last = single(bank, w_uk[:, eo * P:(eo + 1) * P], ctkv)
                    last.then_inc(s["kc_ready"], 1)
                    pe.wait_ge(s["qr_done"], c + 1)
                    for t in range(TPC):
                        last = mm(PS[:, 3 + t // 2, (t % 2) * D:(t % 2 + 1) * D], ctkv[:, t * P:(t + 1) * P], w_uv[:, :], start=True, stop=True)
                    last.then_inc(s["v_ready"], 1)
                    count(c * 3 + lead + 3)

            pe.wait_ge(s["sum_ready"], 1)
            mm(PS[:, 7, 1:2], same, small[:, 0:1], start=True, stop=True)
            mm(PS[:, 7, 2:3], before, small[:, 1:2], start=True, stop=True).then_inc(s["sums_done"], 1)
            pe.wait_ge(s["sum_ready"], 2)
            mm(PS[:, 7, 3:4], before, small[:, 4:5], start=True, stop=True).then_inc(s["sums_done"], 1)
            pe.wait_ge(s["v_done"], NCH + 1)
            pe.wait_ge(s["kc_done"], NCH + 1)
            pe.wait_ge(s["pos_ready"], 1)
            for i in range(2):
                nc.tensor.transpose(PS[:, 1, i * P:(i + 1) * P], scores[:, i * P:(i + 1) * P], ident)
                last = nc.tensor.transpose(PS[:, 0, i * P:(i + 1) * P], pos[:, i * P:(i + 1) * P], ident)
            last.then_inc(s["wcol_ready"], 1)
            pe.wait_ge(s["oh_done"], 2)
            pe.wait_ge(s["hi_done"], 1)
            for e in range(E):
                for t in range(NT):
                    last = mm(PS[0:LO, 0, e * 2 * HI:(e + 1) * 2 * HI], oh_lo[:, t, e, :], oh_hi[:, t, e, :, :].rearrange("p w l -> p (w l)"),
                              start=t == 0, stop=t == NT - 1)
            last.then_inc(s["tok_ready"], 1)

            with pe.Fori(0, E // 2) as h:
                for cc in range(2):
                    e = h * 2 + cc
                    pe.wait_ge(s[f"got_in{cc}"], h * 64 + 64)
                    if cc == 0:
                        pe.wait_ge(s["tok_done"], 1)
                    for k in range(KB):
                        for sl in range(4):
                            last = nc.tensor.transpose(PS[:, k, sl * P:(sl + 1) * P], got[:, cc, sl, k * P:(k + 1) * P], ident)
                    last.then_inc(s["yT_ready"], 1)
                    pe.wait_ge(s["yT_done"], e + 1)
                    pe.wait_ge(s[f"fc_in{cc}"], h * 64 + 64)
                    for f in range(FF // P):
                        if f >= 2:
                            pe.wait_ge(s["hT_done"], e * 8 + f - 1)
                        for k in range(KB):
                            last = mm(PS[:, 2 + f % 2, :], fc1_s[cc][:, k, f * P:(f + 1) * P], yT[:, k, :], start=k == 0, stop=k == KB - 1)
                        last.then_inc(s["hT_ready"], 1)
                        if f == 0:
                            pe.wait_ge(s["o_done"], e + 1)
                            pe.wait_ge(s["qk_in0"], 18 * 16)
                        for i in range(f, f + 1):
                            if i >= 2:
                                pe.wait_ge(s["side_done"], e * PER_EXPERT + i - 1)
                            qt, half = cc * QT // 2 + i // 2, i % 2
                            q, k2 = (qkb[0][0:KROWS, o, bass.ds(h, 1), :].rearrange("p h s -> p (h s)") for o in range(2))
                            mm(PS[:, 6 + i % 2, :], q[:, qt * P:(qt + 1) * P], k2[:, half * 512:(half + 1) * 512],
                               start=True, stop=True).then_inc(s["side_ready"], 1)
                    for sl in range(4):
                        for f in range(FF // P):
                            if sl == 0:
                                pe.wait_ge(s["hT_done"], e * 8 + f + 1)
                            last = mm(PS[:, 4 + sl // 2, sl % 2 * D:(sl % 2 + 1) * D], hT[:, f, sl * P:(sl + 1) * P], fc2_s[cc][:, f, :], start=f == 0, stop=f == FF // P - 1)
                    last.then_inc(s["o_ready"], 1)

            def side_use(u, count, parity, g, n):
                bank = 6 + parity % 2
                if not (isinstance(count, int) and count < 2):
                    pe.wait_ge(s["side_done"], count - 1)
                if u[0] == "max":
                    q, k = (qkb[(g + u[2]) % NG][0:KROWS, o, :, :] for o in range(2))
                    j, rest = divmod(u[1], 2 * QT)
                    qt, half = divmod(rest, 2)
                    ins = mm(PS[:, bank, :], q[:, j, qt * P:(qt + 1) * P], k[:, j, half * 512:(half + 1) * 512], start=True, stop=True)
                elif u[0] == "neg":
                    pe.wait_ge(s["nmax_done"], n + 2)
                    ins = nc.tensor.transpose(PS[0:G4 * QT, bank, 0:P], nmax, ident)
                elif u[0] == "norm":
                    pe.wait_ge(s["pv_done"], 2 * n - 1 + u[1])
                    for t in range(4):
                        q0 = (u[1] * 4 + t) * P
                        ins = nc.tensor.transpose(PS[:, bank, t * P:(t + 1) * P], pvs[:, q0:q0 + P], ident)
                elif u[0] == "turn":
                    if u[1] == 0 and isinstance(count, int) and count >= TAIL:
                        pe.wait_ge(s["side_done"], count)
                    kb, half = divmod(u[1], 2)
                    for t in range(4):
                        ins = nc.tensor.transpose(PS[:, bank, t * P:(t + 1) * P], O[:, half * 4 + t, kb * P:(kb + 1) * P], ident)
                else:
                    if u[1] == 0 and isinstance(count, int) and count >= TAIL:
                        pe.wait_ge(s["side_done"], count)
                    for t in range(2):
                        q0 = (u[1] * 2 + t) * P
                        for kb in range(KB):
                            ins = mm(PS[:, bank, t * D:(t + 1) * D], OT[:, kb, q0:q0 + P], w_o[:, kb, :], start=kb == 0, stop=kb == KB - 1)
                ins.then_inc(s["side_ready"], 1)

            pe.wait_ge(s["qk_in1"], 18 * 16)
            pe.wait_ge(s["o_done"], E + 1)
            pe.wait_ge(s["ones_rows_done"], NG)
            for k, u in enumerate(lead_uses):
                side_use(u, MAXES + k, k, NG - 1, -1)

            def values(g, n, kt, quarter, first):
                if quarter == 0:
                    pe.wait_ge(s["exp_done"], n * (G4 * KT) + (kt + 1) * G4)
                    if kt == 0:
                        pe.wait_ge(s["vg_done"], n + 1)
                if kt == 0 and quarter % 2 == 0 and not (first and g == 0):
                    pe.wait_ge(s["pv_done"], 2 * n - 1 + quarter // 2)
                half, q0 = quarter // 2, quarter % 2 * 256
                for j in range(G4):
                    ins = mm(PS[LO * j:LO * j + VW, 4 + half, q0:q0 + 256], Vg[:, g % 2, kt, j, :], expP[:, kt % 2, j, quarter * 256:(quarter + 1) * 256],
                             start=kt == 0 and q0 == 0, stop=kt == KT - 1, skip_group_check=True)
                if quarter == 1 and kt == KT - 1:
                    ins.then_inc(s["pv_half"], 1)
                if quarter == 3:
                    ins.then_inc(s["pv_ready"], 1)

            def attend_row(b, first, last):
                for g in range(NG):
                    n = b * NG + g
                    k = before_group(g, first, last)
                    pe.wait_ge(s["aug_in"], n * 48 + 48)
                    if not (last and g >= NG - 2):
                        pe.wait_ge(s[f"qk_in{(g + 2) % NG}"], (b + (g + 2) // NG) * 288 + 288)
                    for st, places in enumerate(side_stream(g, first, last)):
                        kt, j = divmod(st, G4)
                        for place, todo in enumerate(places):
                            if place == 1:
                                if not (first and g == 0 and st < 2):
                                    pe.wait_ge(s["exp_done"], n * (G4 * KT) + st - 1)
                                for half in range(2):
                                    ins = mm(PS[:, 2 * (st % 2) + half, :], qkb[g][0:AUG, 1, j, kt * P:(kt + 1) * P],
                                             qkb[g][0:AUG, 0, j, half * 512:(half + 1) * 512], start=True, stop=True)
                                ins.then_inc(s["sc_ready"], 1)
                            if place == 2 and kt > 0:
                                values(g, n, kt - 1, j, first)
                            if place == 2 and kt == 0 and not (first and g == 0):
                                values((g - 1) % NG, n - 1, KT - 1, j, first)
                            for u in todo:
                                side_use(u, side_base(b) + k, 1 + k, g, n)
                                k += 1

            attend_row(0, True, False)
            with pe.Fori(1, B - 1) as b:
                attend_row(b, False, False)
            attend_row(B - 1, False, True)
            for quarter in range(4):
                values(NG - 1, B * NG - 1, KT - 1, quarter, False)
            for k, u in enumerate(tail_uses):
                side_use(u, TAIL + k, TAIL + k, 0, B * NG)


def kernel(**inputs):
    import concourse.bacc as bacc
    from concourse.bass_utils import run_bass_kernel_spmd

    a = {n.removeprefix("L0_"): np.asarray(v) for n, v in inputs.items()}

    def apart(w):
        return np.ascontiguousarray(np.concatenate([w[..., 0::2], w[..., 1::2]], -1))

    def halves(v):
        return np.ascontiguousarray(v.reshape(2, P).T)

    cols = [a["attn_Wd_q_b"][:, None], a["attn_Wd_kv_b"][:, None]]
    cols += [halves(apart(a[f"attn_{n}_b"])) for n in ("Wu_q", "Wq_r", "Wk_r", "Wu_k")]
    cols += [halves(a["ffn_ln_gamma"]), halves(a["ffn_ln_beta"])]
    arrays = {
        "x": a["attn_x"].reshape(TOK, D), "wdq": a["attn_Wd_q_w"], "wdkv": a["attn_Wd_kv_w"],
        "wuq": apart(a["attn_Wu_q_w"]), "wqr": apart(a["attn_Wq_r_w"]), "wkr": apart(a["attn_Wk_r_w"]), "wuk": apart(a["attn_Wu_k_w"]),
        "wuv": a["attn_Wu_v_w"], "wo": a["attn_Wo_w"], "cols": np.concatenate(cols, 1), "buv": a["attn_Wu_v_b"], "bo": a["attn_Wo_b"],
        "gate": a["ffn_gate_w"].T, "fc1": a["ffn_fc1s"].transpose(0, 2, 1),
        "b1": a["ffn_b1s"].reshape(E, FF // P, P).transpose(0, 2, 1), "fc2": a["ffn_fc2s"].transpose(0, 2, 1), "b2": a["ffn_b2s"],
        "const": constants(),
    }
    arrays = {n: np.ascontiguousarray(v) for n, v in arrays.items()}
    nc = bacc.Bacc("TRN2", target_bir_lowering=False, num_devices=1)
    aps = [nc.dram_tensor(n, v.shape, mybir.dt.from_np(v.dtype), kind="ExternalInput").ap() for n, v in arrays.items()]
    acc = nc.dram_tensor("acc", (TOK, D), F32, kind="Internal").ap()
    table = nc.dram_tensor("table", (TOK, ROW), F32, kind="Internal").ap()
    qk = nc.dram_tensor("qk", (2, B, 2, H, 3, PAIR, S), BF16, kind="Internal").ap()
    out = nc.dram_tensor("out", (B, S, D), F32, kind="ExternalOutput").ap()
    program(nc, *aps, acc, table, qk, out.rearrange("b s d -> (b s) d"))
    result = run_bass_kernel_spmd(nc, [arrays], core_ids=[0])
    return result.results[0]["out"]
```

```python
from contextlib import ExitStack

import numpy as np
import concourse.bass as bass
from concourse import mybir

F32 = mybir.dt.float32
BF16 = mybir.dt.bfloat16
I32 = mybir.dt.int32
U32 = mybir.dt.uint32
ALU = mybir.AluOpType
ACT = mybir.ActivationFunctionType
AX = mybir.AxisListType

P = 128
B, S, D = 4, 1024, 256
TOK = B * S
H, HD = 16, 16
LAT = 128
SCALE = float(np.float32(1.0) / np.sqrt(np.float32(H + LAT + LAT)))
E, FF = 8, 1024
KEEP = TOK // E
EPS = 1e-5
CH = 512
NCH = TOK // CH
TPC = CH // P
NT = TOK // P
KB = D // P
ROW = D + E
RUN = TOK // 16
G4 = 4
NG = H // G4
KT = S // P
HALVES = 2 * G4 * KT
QT = S // P
VW = HD + 1
ARENA = 18688
TERMS = 6
PAIR = HD // 2
KROWS = TERMS * HD
AUG = KROWS + 3
BISECT = 26
LO, HI = 32, 16


def rope_tables():
    pos = np.arange(S, dtype=np.float32)[:, None]
    ids = np.arange(D // 2, dtype=np.float32)
    theta = (np.float32(10000.0) ** (np.float32(-2.0) * ids)) / np.float32(D // 2)
    r = (pos * theta[None, :].astype(np.float32)).astype(np.float32)
    return np.cos(r).T.astype(np.float32), -np.sin(r).T.astype(np.float32), np.sin(r).T.astype(np.float32)


def constants():
    i = np.arange(P)
    same = i[:, None] // 16 == i[None, :] // 16
    parts = [np.eye(P), same, same & (i[:, None] < i[None, :]), np.tile(np.arange(LO), (P, 1)), i[:, None]]
    return np.ascontiguousarray(np.concatenate([p.astype(np.float32) for p in parts] + list(rope_tables()), 1))


class Chain:

    def __init__(self, eng, sem):
        self.eng, self.sem, self.base, self.k = eng, sem, 0, 0

    def start(self, base):
        self.base, self.k = base, 0

    def __call__(self, ins):
        ins.then_inc(self.sem, 1)
        self.k += 1
        self.eng.wait_ge(self.sem, self.base + self.k)

    def end(self, n):
        assert self.k == n, (self.k, n)
        return self.base + n


SLOTS = 3
MAXES = 2 * G4 * QT
SCORES = (0, 1, 2)
SIDE = (3, 7, 6)
AHEAD = 12


def side_stream(g, first, last):
    steps = G4 * KT
    more = [] if last and g == NG - 1 else [("max", n, 1) for n in range(AHEAD, MAXES)]
    late = [("neg",)] if more else []
    if not (last and g >= NG - 2):
        late = [("max", 0, 2), ("max", 1, 2)] + late + [("max", n, 2) for n in range(2, AHEAD)]
    early = [] if first and g == 0 else [("norm", 0), ("norm", 1)]
    if g == 0 and not first:
        early += more[16:18] + [("turn", n) for n in range(4)]
        seq = more[:16] + early + more[18:] + late
    else:
        if g == 1 and not first:
            early += [("out", n) for n in range(4)]
        seq = more[:16] + early + more[16:] + late
    begin = 0 if more else 8
    busy = steps - begin - (0 if len(late) > 1 or not more else AHEAD // 2)
    out = [[[] for _ in range(SLOTS)] for _ in range(steps)]
    per = len(seq) / busy
    at = 0
    for st in range(begin, steps):
        take = min(len(seq), int(per * (st - begin + 1) + 1e-6)) - at
        places = {0: [], 1: [2], 2: [1, 2], 3: [0, 1, 2]}[take]
        for p in places:
            out[st][p].append(seq[at])
            at += 1
    assert at == len(seq)
    return out


def uses(first, last):
    return [sum(len(p) for st in side_stream(g, first, last) for p in st) for g in range(NG)]


def program(nc, x, wdq, wdkv, wuq, wqr, wkr, wuk, wuv, wo, cols, buv, bo, gate, fc1, b1, fc2, b2, const,
            acc, table, qk, out):
    ctx = ExitStack()
    with ctx:
        def sb(name, shape, dt=F32):
            return ctx.enter_context(nc.sbuf_tensor(name, shape, dt))

        def sem(name):
            return ctx.enter_context(nc.semaphore(name))

        consts = sb("consts", [P, 3 * P + LO + 1 + 3 * S])
        ident, same, before = (consts[:, n * P:(n + 1) * P] for n in range(3))
        ramp = consts[:, 3 * P:3 * P + LO]
        part_id = consts[:, 3 * P + LO:3 * P + LO + 1]
        cos, nsin, sin = (consts[:, 3 * P + LO + 1 + n * S:3 * P + LO + 1 + (n + 1) * S] for n in range(3))
        w_dq = sb("w_dq", [P, KB, LAT])
        w_dkv = sb("w_dkv", [P, KB, LAT])
        w_uq = sb("w_uq", [P, D])
        w_qr = sb("w_qr", [P, D])
        w_kr = sb("w_kr", [P, KB, D])
        w_uk = sb("w_uk", [P, D])
        w_uv = sb("w_uv", [P, D])
        w_o = sb("w_o", [P, KB, D])
        w_gate = sb("w_gate", [P, KB, E])
        col = sb("col", [P, 14])
        b_dq, b_dkv = col[:, 0:1], col[:, 1:2]
        b_uq, b_qr, b_kr, b_uk, gamma, beta = ([col[:, n:n + 1], col[:, n + 1:n + 2]] for n in range(2, 14, 2))
        b_uv = sb("b_uv", [P, D])
        b_o = sb("b_o", [P, D])
        V = sb("V", [P, NT, H, VW])
        Vg = sb("Vg", [P, 2, KT, G4, VW])
        marks = sb("marks", [P, RUN])
        idx = sb("idx", [P, E, 4], U32)
        scores = sb("scores", [P, RUN])
        minus_half = sb("minus_half", [P, TPC])
        eps = sb("eps", [P, TPC])
        held = sb("held", [P, 1])
        ones = sb("ones", [P, RUN])
        thr = sb("thr", [P, 1])
        step = sb("step", [P, 1])
        cand = sb("cand", [P, 1])
        cnt = sb("cnt", [P, 1])
        stat = sb("stat", [P, 2, TPC, 6])
        mv = sb("mv", [P, 2, 2, TPC, 2])
        rstd = sb("rstd", [P, 2, 2, TPC])
        ve = sb("ve", [P, 2, 2, TPC])
        small = sb("small", [P, 16])
        wtok = sb("wtok", [P, NT, E])

        expP = sb("expP", [P, 2, G4, S])
        flat = expP[:, :, :, :].rearrange("p a h s -> p (a h s)")
        fc1_s = [flat[:, n * 4096:n * 4096 + 2048].rearrange("p (k f) -> p k f", k=KB) for n in range(2)]
        fc2_s = [flat[:, n * 4096 + 2048:(n + 1) * 4096].rearrange("p (k d) -> p k d", k=FF // P) for n in range(2)]
        logits = flat[0:E, 4096:4096 + TOK]
        qkbuf = sb("qkbuf", [P, 2, 2, G4, S], BF16)
        tu = qkbuf[:, :, :, :, :].rearrange("p a b h s -> p (a b h s)").bitcast(F32)
        tu = tu.rearrange("p (c o w e t) -> p c o w e t", c=2, o=2, w=2, e=2)
        arena = sb("arena", [P, ARENA])
        at = [0]

        def view(n, dt=F32):
            a = arena[:, at[0]:at[0] + n]
            at[0] += n
            assert at[0] <= ARENA, at[0]
            return a if dt == F32 else a.bitcast(dt)

        xnT = view(KB * TOK).rearrange("p (k t) -> p k t", k=KB)
        after_xnT = at[0]
        xs = view(2 * TPC * D).rearrange("p (c t d) -> p c t d", c=2, t=TPC)
        xn = view(2 * TPC * D).rearrange("p (c t d) -> p c t d", c=2, t=TPC)
        rows = view(2 * TPC * D).rearrange("p (c t d) -> p c t d", c=2, t=TPC)
        base = view(2 * TPC * D).rearrange("p (c t d) -> p c t d", c=2, t=TPC)
        at[0] = after_xnT
        full = view(2 * 2 * 2 * CH).rearrange("p (c o e t) -> p c o e t", c=2, o=2, e=2)
        parts = view(2 * 2 * 3 * CH, BF16).rearrange("p (c o r e t) -> p c o r e t", c=2, o=2, r=3, e=2)
        latents = Vg[:, :, :, :, :].rearrange("p a k h d -> p (a k h d)")
        ctq, ctkv = latents[:, 0:CH], latents[:, CH:2 * CH]
        at[0] = 0
        oh_hi = view(NT * E * 2 * HI // 2, BF16).rearrange("p (t e w l) -> p t e w l", t=NT, e=E, w=2)
        gt = view(RUN)
        eq = view(RUN)
        rank = view(RUN)
        taken = view(RUN)
        pos = view(RUN)
        posi = view(RUN, I32).rearrange("p (t e) -> p t e", t=NT)
        loi = view(RUN, I32).rearrange("p (t e) -> p t e", t=NT)
        hii = view(RUN, I32).rearrange("p (t e) -> p t e", t=NT)
        lof = view(RUN).rearrange("p (t e) -> p t e", t=NT)
        hif = view(RUN).rearrange("p (t e) -> p t e", t=NT)
        tok = view(E * 2 * HI).rearrange("p (e w l) -> p e w l", e=E, w=2)
        idx32 = view(E * HI, U32).rearrange("p (e l) -> p e l", e=E)
        assert at[0] <= after_xnT, at[0]
        at[0] = after_xnT
        oh_lo = view(NT * E * LO // 2, BF16).rearrange("p (t e l) -> p t e l", t=NT, e=E)
        oh = view(NT * E * HI // 2, BF16).rearrange("p (t e l) -> p t e l", t=NT, e=E)
        at[0] = 0
        hT = view(FF // P * KEEP).rearrange("p (f s) -> p f s", f=FF // P)
        yT = view(KB * KEEP).rearrange("p (k s) -> p k s", k=KB)
        got = view(2 * 4 * ROW).rearrange("p (c s r) -> p c s r", c=2, s=4)
        wsel = view(2 * 4).rearrange("p (c s) -> p c s", c=2)
        res = view(2 * 4 * D).rearrange("p (c s d) -> p c s d", c=2, s=4)
        b2_s = view(2 * D).rearrange("p (c d) -> p c d", c=2)
        b1_s = view(2 * FF // P).rearrange("p (c f) -> p c f", c=2)
        hmax = view(2 * MAXES).rearrange("p (c n) -> p c n", c=2)
        nmax = view(G4 * QT)
        rsum = view(2 * 16).rearrange("p (c t h) -> p c t h", c=2, t=4)
        nrest = view(P)[0:G4 * QT, :]
        nparts = view(3 * P // 2, BF16)[0:G4 * QT, :].rearrange("p (r q) -> p r q", r=3)
        assert at[0] <= ARENA - 2 * 4096, at[0]
        at[0] = 0
        accb = view(QT * D).rearrange("p (t d) -> p t d", t=QT)
        outs = view(QT * D).rearrange("p (t d) -> p t d", t=QT)
        O = view(QT * D).rearrange("p (t d) -> p t d", t=QT)
        OT = view(KB * S).rearrange("p (k t) -> p k t", k=KB)
        pvs = view(S)
        qkb = [qkbuf[:, n, :, :, :] for n in range(2)]
        qkb += [arena[:, ARENA - (2 - n) * 4096:ARENA - (1 - n) * 4096].bitcast(BF16).rearrange("p (o h s) -> p o h s", o=2, h=G4)
                for n in range(2)]

        PS = ctx.enter_context(nc.psum_tensor("PS", [P, 8, 512], F32))

        names = """const_in w_in stored x_in0 x_in1 mv_done rstd_done xn_done rows_done base_done xnT_ready xnT_done lg_ready lg_done
            acc_out0 acc_out1 tab_out0 tab_out1 s_in tanh_done
            cnt_ready cnt_sum ct_ready ct_done kr_ready qr_ready qc_ready kc_ready v_ready kr_done qr_done qc_done
            kc_done v_done added cast1 cast2 resid parts_done qk_out0 qk_out1 parts_free res_free
            sum_ready sums_done pos_ready pos_turned pos_done oh_done hi_done hi_part_done tok_ready tok_done idx_in wcol_ready wcol_done wcol_out
            fc_in0 fc_in1 got_in0 got_in1 wsel_done yT_ready yT_done hT_ready hT_done o_ready o_done o_out0 o_out1
            qk_in0 qk_in1 qk_in2 qk_in3 aug_in ones_rows_done side_ready side_done nmax_done sc_ready exp_done pv_half pv_ready pv_done
            vg_done accb_in accb_done out_out ones_done dve_chain pool_chain""".split()
        s = {n: sem(n) for n in names}

        block = ctx.enter_context(nc.Block())

        PER_EXPERT = MAXES // E
        def score_bank(g, st, half):
            return SCORES[(g * HALVES + st * 2 + half) % 3]

        lead_uses = [("max", 0, 2), ("max", 1, 2), ("neg",)] + [("max", n, 2) for n in range(2, AHEAD)]
        LEAD = MAXES + len(lead_uses)
        U_FIRST, U_MID = sum(uses(True, False)), sum(uses(False, False))

        def side_base(b):
            if isinstance(b, int):
                return LEAD if b == 0 else LEAD + U_FIRST + (b - 1) * U_MID
            return b * U_MID + (LEAD + U_FIRST - U_MID)

        assert U_MID % 3 == 0

        def side_bank(first, k):
            return SIDE[(k if first else U_FIRST + k) % 3]

        def lead_bank(k):
            return 6 + k % 2

        def flat_stream(g, first, last):
            return [u for st in side_stream(g, first, last) for p in st for u in p]

        def before_group(g, first, last):
            return sum(uses(first, last)[:g])

        def at_neg(g, first, last):
            return before_group(g, first, last) + flat_stream(g, first, last).index(("neg",)) + 1

        TAIL = side_base(B - 1) + sum(uses(False, True))
        tail_uses = [("norm", 0), ("norm", 1)] + [("turn", n) for n in range(4)] + [("out", n) for n in range(4)]

        @block.sync
        def _(sp):
            x_c = x.rearrange("(c t p) d -> c p t d", p=P, t=TPC)
            acc_c = acc.rearrange("(c t p) d -> c p t d", p=P, t=TPC)
            tab_c = table[:, 0:D].rearrange("(c t p) d -> c p t d", p=P, t=TPC)
            sp.sem_inc(s["parts_free"], 2)
            sp.sem_inc(s["stored"], 2)
            first = 3 * P + LO + 1
            sp.dma_start(xs[:, 0, :, :], x_c[0, :, :, :]).then_inc(s["x_in0"], 16)
            sp.dma_start(consts[:, 0:first], const[:, 0:first]).then_inc(s["const_in"], 16)
            sp.dma_start(w_gate[:, :, :], gate.rearrange("(k p) e -> p k e", p=P)).then_inc(s["const_in"], 16)
            sp.dma_start(xs[:, 1, :, :], x_c[1, :, :, :]).then_inc(s["x_in1"], 16)
            loads = [(consts[:, first:], const[:, first:]), (col[:, :], cols),
                     (w_dq[:, :, :], wdq.rearrange("(k p) m -> p k m", p=P)), (w_dkv[:, :, :], wdkv.rearrange("(k p) m -> p k m", p=P)),
                     (w_uq[:, :], wuq), (w_qr[:, :], wqr), (w_kr[:, :, :], wkr.rearrange("(k p) m -> p k m", p=P)),
                     (w_uk[:, :], wuk), (w_uv[:, :], wuv), (w_o[:, :, :], wo.rearrange("(k p) m -> p k m", p=P)),
                     (b_uv[:, :], buv.partition_broadcast(P)), (b_o[:, :], bo.partition_broadcast(P))]
            for dst, src in loads:
                sp.dma_start(dst, src).then_inc(s["w_in"], 16)

            def norm_chunk(b, cc, load):
                c = b * 2 + cc
                sp.wait_ge(s["base_done"], c + 3)
                sp.dma_start(acc_c[bass.ds(c, 1), :, :, :].rearrange("c p t d -> (c p) t d"), base[:, cc, :, :]).then_inc(s[f"acc_out{cc}"], 16)
                if load:
                    sp.dma_start(xs[:, cc, :, :], x_c[bass.ds(c + 2, 1), :, :, :].rearrange("c p t d -> (c p) t d")).then_inc(s[f"x_in{cc}"], 16)
                sp.wait_ge(s["rows_done"], c + 1)
                sp.dma_start(tab_c[bass.ds(c, 1), :, :, :].rearrange("c p t d -> (c p) t d"), rows[:, cc, :, :]).then_inc(s[f"tab_out{cc}"], 16)
                sp.wait_ge(s[f"acc_out{cc}"], b * 16 + 16)
                sp.wait_ge(s[f"tab_out{cc}"], b * 16 + 16)
                sp.sem_inc(s["stored"], 1)

            with sp.Fori(0, NCH // 2 - 1) as b:
                for cc in range(2):
                    norm_chunk(b, cc, True)
            for cc in range(2):
                norm_chunk(NCH // 2 - 1, cc, False)
            sp.wait_ge(s["lg_done"], NCH + 2)
            sp.dma_start(scores[:, :], logits.rearrange("e (r t) -> e r t", t=RUN)).then_inc(s["s_in"], 16)

            def load_expert(e, cc):
                sem_in = s[f"fc_in{cc}"]
                one = bass.ds(e, 1)
                sp.dma_start(fc1_s[cc], fc1[one, :, :].rearrange("e (k p) f -> p (e k) f", p=P)).then_inc(sem_in, 16)
                sp.dma_start(fc2_s[cc], fc2[one, :, :].rearrange("e (k p) d -> p (e k) d", p=P)).then_inc(sem_in, 16)

            def load_biases(e, cc):
                sem_in = s[f"fc_in{cc}"]
                one = bass.ds(e, 1)
                sp.dma_start(b1_s[:, cc, :], b1[one, :, :].rearrange("e p f -> (e p) f")).then_inc(sem_in, 16)
                sp.dma_start(b2_s[:, cc, :], b2[one, :].rearrange("e d -> (e d)").partition_broadcast(P)).then_inc(sem_in, 16)

            load_expert(0, 0)
            sp.wait_ge(s["s_in"], 16)
            load_expert(1, 1)

            sp.wait_ge(s["wcol_done"], 1)
            with nc.allow_non_contiguous_dma(reason="eight scores of a token"):
                sp.dma_start(table[:, D:ROW].rearrange("(t p) e -> p t e", p=P), wtok[:, :, :]).then_inc(s["wcol_out"], 16)
            with sp.Fori(0, NCH // 2) as b:
                for cc in range(2):
                    sp.wait_ge(s["parts_done"], (b * 2 + cc) * 2 + 6)
                    for o in range(2):
                        for r in range(3):
                            for eo in range(2):
                                dst = qk[o, bass.ds(b, 1), eo, :, r, :, cc * CH:(cc + 1) * CH].rearrange("b h j t -> (b h) j t")
                                sp.dma_start(dst, parts[:, cc, o, r, eo, :]).then_inc(s[f"qk_out{cc}"], 16)
                    sp.wait_ge(s[f"qk_out{cc}"], b * 192 + 192)
                    sp.sem_inc(s["parts_free"], 1)

            def load_qk(b, g):
                sem_in = s[f"qk_in{g}"]
                for eo in range(2):
                    row = eo * KROWS // 2
                    for n0, n in ((0, 3), (3, 2), (5, 1)):
                        src = qk[0, bass.ds(b, 1), eo, g * G4:(g + 1) * G4, 0:n, :, :].rearrange("b h r j t -> (b r j) h t")
                        lo = row + n0 * PAIR
                        sp.dma_start(qkb[g][lo:lo + n * PAIR, 0, :, :], src).then_inc(sem_in, 16)
                    for n, part in enumerate((0, 0, 0, 1, 1, 2)):
                        src = qk[1, bass.ds(b, 1), eo, g * G4:(g + 1) * G4, part, :, :].rearrange("b h j t -> (b j) h t")
                        lo = row + n * PAIR
                        sp.dma_start(qkb[g][lo:lo + PAIR, 1, :, :], src).then_inc(sem_in, 16)

            for c in range(2):
                sp.wait_ge(s[f"qk_out{c}"], 192 * (NCH // 2))
            sp.wait_ge(s["parts_done"], 2 * NCH + 4)

            sp.wait_ge(s["tok_done"], 1)
            for q in range(4):
                sp.dma_start(idx[LO * q:LO * (q + 1), :, :], idx32[0:LO, :, 4 * q:4 * q + 4]).then_inc(s["idx_in"], 16)

            sp.wait_ge(s["idx_in"], 64)
            load_biases(0, 0)
            load_biases(1, 1)
            for g in range(NG):
                load_qk(0, g)

            with sp.Fori(0, E // 2 - 1) as h:
                for cc in range(2):
                    sp.wait_ge(s["o_ready"], h * 2 + cc + 2)
                    sp.wait_ge(s["o_done"], h * 2 + cc + 2)
                    load_expert(h * 2 + cc + 2, cc)
                    load_biases(h * 2 + cc + 2, cc)

            def load_aug(g, count):
                sp.wait_ge(s["side_done"], count)
                for part in range(3):
                    sp.dma_start(qkb[g][KROWS + part:KROWS + part + 1, 0, :, :].rearrange("p h (t q) -> p (h t) q", q=P),
                                 nparts[:, part, :]).then_inc(s["aug_in"], 16)

            load_aug(0, MAXES + 3)

            def attend_row(b, first, last):
                for g in range(NG):
                    if g == 0 and not first:
                        sp.dma_start(accb, acc[bass.ds((b - 1) * S, S), :].rearrange("(t p) d -> p t d", p=P)).then_inc(s["accb_in"], 16)
                    if g == 2 and not first:
                        sp.wait_ge(s["side_done"], side_base(b) + before_group(2, first, last))
                        sp.dma_start(out[bass.ds((b - 1) * S, S), :].rearrange("(t p) d -> p t d", p=P), outs).then_inc(s["out_out"], 16)
                    if not (last and g == NG - 1):
                        load_aug((g + 1) % NG, side_base(b) + at_neg(g, first, last))
                    if g == 3 and not first:
                        sp.wait_ge(s["out_out"], b * 16)
                    if not last:
                        sp.wait_ge(s["sc_ready"], (b * NG + g + 1) * HALVES)
                        load_qk(b + 1, g)

            for c in range(2):
                sp.wait_ge(s[f"o_out{c}"], 64 * E // 2)
            attend_row(0, True, False)
            with sp.Fori(1, B - 1) as b:
                attend_row(b, False, False)
            attend_row(B - 1, False, True)
            sp.dma_start(accb, acc[(B - 1) * S:B * S, :].rearrange("(t p) d -> p t d", p=P)).then_inc(s["accb_in"], 16)
            sp.wait_ge(s["side_done"], TAIL + len(tail_uses))
            sp.dma_start(out[(B - 1) * S:B * S, :].rearrange("(t p) d -> p t d", p=P), outs).then_inc(s["out_out"], 16)
            sp.wait_ge(s["out_out"], 16 * B)
            for c in range(2):
                sp.wait_ge(s[f"acc_out{c}"], 16 * (NCH // 2))
                sp.wait_ge(s[f"tab_out{c}"], 16 * (NCH // 2))

        @block.gpsimd
        def _(pool):
            chain = Chain(pool, s["pool_chain"])
            nc.gpsimd.memset(minus_half[:, :], -0.5)
            nc.gpsimd.memset(eps[:, :], EPS)
            nc.gpsimd.memset(ones[:, :], 1.0)
            nc.gpsimd.memset(V[:, :, :, HD:VW], 1.0).then_inc(s["ones_done"], 1)
            pool.wait_ge(s["ones_done"], 1)
            pool.sem_inc(s["base_done"], 2)
            pool.sem_inc(s["parts_done"], 4)

            def rsqrt(cc, which):
                chain(nc.gpsimd.tensor_tensor(out=ve[:, cc, which, :], in0=mv[:, cc, which, :, 1], in1=eps[:, :], op=ALU.add))
                nc.gpsimd.tensor_tensor(out=rstd[:, cc, which, :], in0=ve[:, cc, which, :], in1=minus_half[:, :],
                                        op=ALU.pow).then_inc(s["rstd_done"], 1)

            with pool.Fori(0, NCH // 2) as b:
                for cc in range(2):
                    c = b * 2 + cc
                    chain.start(c * 2)
                    pool.wait_ge(s["mv_done"], c * 2 + 1)
                    rsqrt(cc, 0)
                    pool.wait_ge(s["xn_done"], c + 1)
                    pool.wait_ge(s["stored"], c + 1)
                    nc.gpsimd.tensor_tensor(out=base[:, cc, :, :], in0=xs[:, cc, :, :], in1=xn[:, cc, :, :],
                                            op=ALU.add).then_inc(s["base_done"], 1)
                    pool.wait_ge(s["mv_done"], c * 2 + 2)
                    rsqrt(cc, 1)
                    chain.end(2)

            with pool.Fori(0, NCH // 2) as b:
                for cc in range(2):
                    c = b * 2 + cc
                    for o, done in ((0, "qc_done"), (1, "kc_done")):
                        pool.wait_ge(s[done], c + 2)
                        nc.gpsimd.tensor_tensor(out=full[:, cc, o, :, :], in0=full[:, cc, o, :, :], in1=tu[:, cc, o, 1, :, :],
                                                op=ALU.add).then_inc(s["added"], 1)
                    for o in range(2):
                        pool.wait_ge(s["cast1"], c * 2 + o + 1)
                        nc.gpsimd.tensor_tensor(out=full[:, cc, o, :, :], in0=full[:, cc, o, :, :], in1=parts[:, cc, o, 0, :, :],
                                                op=ALU.subtract).then_inc(s["resid"], 1)
                    for o in range(2):
                        pool.wait_ge(s["cast2"], c * 2 + o + 1)
                        nc.gpsimd.tensor_tensor(out=parts[:, cc, o, 2, :, :], in0=full[:, cc, o, :, :], in1=parts[:, cc, o, 1, :, :],
                                                op=ALU.subtract).then_inc(s["parts_done"], 1)

            pool.wait_ge(s["oh_done"], 1)
            for half in range(2):
                es = slice(half * E // 2, (half + 1) * E // 2)
                nc.gpsimd.tensor_tensor(out=oh_hi[:, :, es, 1, :], in0=oh[:, :, es, :],
                                        in1=ramp[:, 0:NT].unsqueeze(2).unsqueeze(3).broadcast_to([P, NT, E // 2, HI]),
                                        op=ALU.mult).then_inc(s["hi_done"], 1)

            def gather(e):
                cc = e % 2
                if e >= 2:
                    pool.wait_ge(s["yT_ready"], e - 1)
                    pool.wait_ge(s["wsel_done"], e - 1)
                for sl in range(4):
                    nc.gpsimd.indirect_dma_start(got[:, cc, sl, :], None, table,
                                                 bass.IndirectOffsetOnAxis(ap=idx[:, e, sl:sl + 1], axis=0)).then_inc(s[f"got_in{cc}"], 16)

            for c in range(2):
                pool.wait_ge(s[f"tab_out{c}"], 16 * (NCH // 2))
                pool.wait_ge(s[f"acc_out{c}"], 16 * (NCH // 2))
            pool.wait_ge(s["wcol_out"], 16)
            pool.wait_ge(s["idx_in"], 64)
            pool.sem_inc(s["res_free"], 2)
            gather(0)
            gather(1)
            for c in range(2):
                pool.wait_ge(s[f"qk_out{c}"], 192 * (NCH // 2))
            for g in range(NG):
                nc.gpsimd.memset(qkb[g][KROWS:AUG, 1, :, :], 1.0).then_inc(s["ones_rows_done"], 1)
            pool.wait_ge(s["ones_rows_done"], NG)
            for e in range(E):
                cc = e % 2
                pool.wait_ge(s[f"got_in{cc}"], 64 * (e // 2 + 1))
                if e >= 2:
                    pool.wait_ge(s["o_done"], e)
                nc.gpsimd.tensor_copy(wsel[:, cc, :], got[:, cc, :, D + e]).then_inc(s["wsel_done"], 1)
                if 1 <= e < E - 1:
                    gather(e + 1)
                pool.wait_ge(s["o_done"], e + 2)
                if e >= 1:
                    pool.wait_ge(s[f"o_out{1 - cc}"], 64 * ((e - 1) // 2 + 1))
                    pool.sem_inc(s["res_free"], 1)
                for sl in range(4):
                    nc.gpsimd.indirect_dma_start(acc, bass.IndirectOffsetOnAxis(ap=idx[:, e, sl:sl + 1], axis=0), res[:, cc, sl, :], None,
                                                 compute_op=ALU.add).then_inc(s[f"o_out{cc}"], 16)

            def add_bias(b):
                pool.wait_ge(s["accb_in"], b * 16)
                nc.gpsimd.tensor_tensor(out=accb, in0=accb, in1=b_o[:, :].unsqueeze(1).broadcast_to([P, QT, D]),
                                        op=ALU.add).then_inc(s["accb_done"], 1)

            def values_row(b, first):
                for g in range(NG):
                    if not (first and g < 2):
                        pool.wait_ge(s["pv_ready"], (b * NG + g - 1) * KT)
                    nc.gpsimd.tensor_copy(Vg[:, g % 2, :, :, :], V[:, bass.ds(b * KT, KT), g * G4:(g + 1) * G4, :]).then_inc(s["vg_done"], 1)
                    if g == 0 and not first:
                        add_bias(b)

            pool.wait_ge(s["v_done"], NCH + 1)
            values_row(0, True)
            with pool.Fori(1, B) as b:
                values_row(b, False)
            add_bias(B)

        @block.scalar
        def _(act):
            act.sem_inc(s["xnT_done"], 2)
            act.sem_inc(s["lg_done"], 2)
            def copy_xnT(c, cc):
                act.wait_ge(s["xnT_ready"], c + 3)
                nc.scalar.activation(xnT[:, :, bass.ds(c * CH, CH)], PS[:, 2 * cc:2 * cc + 2, :], ACT.Copy).then_inc(s["xnT_done"], 1)

            def copy_logits(c, cc):
                act.wait_ge(s["lg_ready"], c + 1)
                nc.scalar.activation(logits[:, bass.ds(c * CH, CH)], PS[0:E, 4 + cc, :], ACT.Copy).then_inc(s["lg_done"], 1)

            copy_xnT(0, 0)
            with act.Fori(0, NCH // 2 - 1) as b:
                for cc in range(2):
                    copy_xnT(b * 2 + cc + 1, 1 - cc)
                    copy_logits(b * 2 + cc, cc)
            copy_xnT(NCH - 1, 1)
            for cc in range(2):
                copy_logits(NCH - 2 + cc, cc)
            act.wait_ge(s["s_in"], 16)
            nc.scalar.activation(scores[:, :], scores[:, :], ACT.Tanh).then_inc(s["tanh_done"], 1)

            def copy_latents(c):
                act.wait_ge(s["ct_ready"], c + 1)
                act.wait_ge(s["v_ready"], c + 1)
                nc.scalar.activation(ctq, PS[:, 0, :], ACT.Identity, bias=b_dq)
                nc.scalar.activation(ctkv, PS[:, 1, :], ACT.Identity, bias=b_dkv).then_inc(s["ct_done"], 1)

            def cast_parts(c, cc):
                act.wait_ge(s["parts_free"], c + 1)
                for o in range(2):
                    act.wait_ge(s["added"], c * 2 + o + 1)
                    nc.scalar.activation(parts[:, cc, o, 0, :, :], full[:, cc, o, :, :], ACT.Copy).then_inc(s["cast1"], 1)
                for o in range(2):
                    act.wait_ge(s["resid"], c * 2 + o + 1)
                    nc.scalar.activation(parts[:, cc, o, 1, :, :], full[:, cc, o, :, :], ACT.Copy).then_inc(s["cast2"], 1)

            copy_latents(0)
            for c in range(2):
                act.wait_ge(s[f"tab_out{c}"], 16 * (NCH // 2))
                act.wait_ge(s[f"acc_out{c}"], 16 * (NCH // 2))
            with act.Fori(0, NCH // 2 - 1) as b:
                for cc in range(2):
                    copy_latents(b * 2 + cc + 1)
                    cast_parts(b * 2 + cc, cc)
            copy_latents(NCH - 1)
            for cc in range(2):
                cast_parts(NCH - 2 + cc, cc)

            act.wait_ge(s["oh_done"], 1)
            nc.scalar.activation(oh_hi[:, :, :, 0, :], oh, ACT.Copy, scale=part_id).then_inc(s["hi_part_done"], 1)

            with act.Fori(0, E // 2) as h:
                for cc in range(2):
                    e = h * 2 + cc
                    act.wait_ge(s[f"fc_in{cc}"], h * 64 + 64)
                    for f in range(FF // P):
                        act.wait_ge(s["hT_ready"], e * 8 + f + 1)
                        if f == 0:
                            act.wait_ge(s["o_ready"], e + 1)
                        nc.scalar.activation(hT[:, f, :], PS[:, 2 + f % 2, :], ACT.Gelu_apprx_tanh,
                                             bias=b1_s[:, cc, f:f + 1]).then_inc(s["hT_done"], 1)

            def outputs(n, half):
                if half == 0:
                    act.wait_ge(s["pv_half"], n)
                else:
                    act.wait_ge(s["pv_ready"], n * KT)
                nc.scalar.activation(pvs[:, half * 512:(half + 1) * 512], PS[:, 4 + half, :], ACT.Copy).then_inc(s["pv_done"], 1)

            def attend_row(b, first, last):
                for g in range(NG):
                    n = b * NG + g
                    if first and g == 1:
                        for c in range(2):
                            act.wait_ge(s[f"o_out{c}"], 64 * E // 2)
                    for st in range(G4 * KT):
                        kt, j = divmod(st, G4)
                        if not (first and g == 0 and kt < 2):
                            act.wait_ge(s["pv_ready"], n * KT + kt - 1)
                        for half in range(2):
                            act.wait_ge(s["sc_ready"], n * HALVES + st * 2 + half + 1)
                            nc.scalar.activation(expP[:, kt % 2, j, half * 512:(half + 1) * 512], PS[:, score_bank(g, st, half), :],
                                                 ACT.Exp, scale=SCALE).then_inc(s["exp_done"], 1)
                        if not (first and g == 0) and st in (2, 4):
                            outputs(n, st // 2 - 1)

            attend_row(0, True, False)
            with act.Fori(1, B - 1) as b:
                attend_row(b, False, False)
            attend_row(B - 1, False, True)
            for half in range(2):
                outputs(B * NG, half)

        @block.vector
        def _(dve):
            chain = Chain(dve, s["dve_chain"])
            dve.sem_inc(s["qc_done"], 1)
            dve.sem_inc(s["kc_done"], 1)
            dve.sem_inc(s["v_done"], 1)
            dve.sem_inc(s["o_done"], 1)
            chain.start(0)
            nc.vector.memset(thr[:, :], 0.0)
            chain(nc.vector.memset(step[:, :], 1.0))
            chain.end(1)
            NORM = 2

            def stats(src, cc, which):
                for t in range(TPC):
                    last = nc.vector.bn_stats(stat[:, which, t, :], src[:, cc, t, :])
                chain(last)
                nc.vector.memset(held[:, :], 0.0)
                for t in range(TPC):
                    last = nc.vector.bn_aggr(mv[:, cc, which, t, :], stat[:, which, t, :])
                last.then_inc(s["mv_done"], 1)

            def apply_rows(c, cc):
                dve.wait_ge(s["mv_done"], c * 2 + 2)
                dve.wait_ge(s["rstd_done"], c * 2 + 2)
                dve.wait_ge(s["stored"], c + 1)
                for t in range(TPC):
                    last = nc.vector.tensor_scalar(rows[:, cc, t, :], xn[:, cc, t, :], mv[:, cc, 1, t, 0:1], rstd[:, cc, 1, t:t + 1],
                                                   ALU.subtract, ALU.mult)
                last.then_inc(s["rows_done"], 1)

            def norm_chunk(b, c, cc):
                chain.start(c * NORM + 1)
                dve.wait_ge(s[f"x_in{cc}"], b * 16 + 16)
                stats(xs, cc, 0)
                if not (isinstance(c, int) and c == 0):
                    apply_rows(c - 1, 1 - cc)
                dve.wait_ge(s["mv_done"], c * 2 + 1)
                dve.wait_ge(s["rstd_done"], c * 2 + 1)
                dve.wait_ge(s["xnT_ready"], c + 1)
                dve.wait_ge(s["base_done"], c + 1)
                for t in range(TPC):
                    last = nc.vector.tensor_scalar(xn[:, cc, t, :], xs[:, cc, t, :], mv[:, cc, 0, t, 0:1], rstd[:, cc, 0, t:t + 1],
                                                   ALU.subtract, ALU.mult)
                last.then_inc(s["xn_done"], 1)
                dve.wait_ge(s["xn_done"], c + 1)
                stats(xn, cc, 1)
                chain.end(NORM)

            norm_chunk(0, 0, 0)
            with dve.Fori(0, NCH // 2 - 1) as b:
                for cc in range(2):
                    norm_chunk(b + cc, b * 2 + cc + 1, 1 - cc)
            norm_chunk(NCH // 2 - 1, NCH - 1, 1)
            apply_rows(NCH - 1, 1)
            done = 1 + NCH * NORM

            chain.start(done)
            dve.wait_ge(s["tanh_done"], 1)
            chain(nc.vector.tensor_scalar(scores[:, :], scores[:, :], 1.0, 0.5, ALU.add, ALU.mult))

            def probe_start():
                chain(nc.vector.tensor_tensor(out=cand[:, :], in0=thr[:, :], in1=step[:, :], op=ALU.add))
                nc.vector.tensor_scalar(marks[:, :], scores[:, :], cand[:, :], None, ALU.is_ge, ALU.add,
                                        accum_out=cnt[:, :]).then_inc(s["cnt_ready"], 1)

            def probe_end(n):
                dve.wait_ge(s["cnt_sum"], n)
                chain(nc.vector.tensor_scalar(cand[:, :], PS[:, 7, 0:1], float(KEEP), step[:, :], ALU.is_ge, ALU.mult))
                nc.vector.tensor_tensor(out=thr[:, :], in0=thr[:, :], in1=cand[:, :], op=ALU.add)
                chain(nc.vector.tensor_scalar(step[:, :], step[:, :], 0.5, None, ALU.mult))

            PROBE = 3
            lead = BISECT - 3 * NCH
            probe_start()
            for n in range(lead):
                probe_end(n + 1)
                probe_start()
            dve.wait_ge(s["wcol_ready"], 1)
            for i in range(2):
                last = nc.vector.tensor_copy(wtok[:, i::2, :], PS[:, 6, i * P:(i + 1) * P].rearrange("p (e r) -> p r e", e=E))
            last.then_inc(s["wcol_done"], 1)
            done = chain.end(2 + lead * PROBE)

            dve.wait_ge(s["w_in"], 16 * 12)
            dve.wait_ge(s["xnT_ready"], NCH + 2)
            dve.wait_ge(s["base_done"], NCH + 2)
            for c in range(2):
                dve.wait_ge(s[f"tab_out{c}"], 16 * (NCH // 2))
                dve.wait_ge(s[f"acc_out{c}"], 16 * (NCH // 2))
            dve.wait_ge(s["ones_done"], 1)
            with dve.Fori(0, NCH // 2) as b:
                for cc in range(2):
                    c = b * 2 + cc
                    chain.start(c * 9 + done)
                    csl = slice(cc * CH, (cc + 1) * CH)

                    def rotate(o, banks, bias):
                        for eo in range(2):
                            nc.vector.scalar_tensor_tensor(out=tu[:, cc, o, 0, eo, :], in0=PS[:, banks[eo], :], scalar=bias[eo],
                                                           in1=cos[:, csl], op0=ALU.add, op1=ALU.mult)
                        for eo, tab in ((1, nsin), (0, sin)):
                            last = nc.vector.scalar_tensor_tensor(out=tu[:, cc, o, 1, 1 - eo, :], in0=PS[:, banks[eo], :], scalar=bias[eo],
                                                                  in1=tab[:, csl], op0=ALU.add, op1=ALU.mult)
                        return last

                    def combine(o, banks, bias):
                        for eo in range(2):
                            last = nc.vector.scalar_tensor_tensor(out=full[:, cc, o, eo, :], in0=PS[:, banks[eo], :], scalar=bias[eo],
                                                                  in1=tu[:, cc, o, 0, eo, :], op0=ALU.add, op1=ALU.add)
                        return last

                    dve.wait_ge(s["kr_ready"], c + 1)
                    dve.wait_ge(s["parts_done"], c * 2 + 2)
                    rotate(1, (2, 3), b_kr).then_inc(s["kr_done"], 1)
                    dve.wait_ge(s["qr_ready"], c + 1)
                    rotate(0, (4, 5), b_qr).then_inc(s["qr_done"], 1)
                    dve.wait_ge(s["qr_done"], c + 1)
                    dve.wait_ge(s["kr_done"], c + 1)
                    dve.wait_ge(s["qc_ready"], c + 1)
                    combine(0, (0, 1), b_uq).then_inc(s["qc_done"], 1)
                    dve.wait_ge(s["kc_ready"], c + 1)
                    combine(1, (2, 3), b_uk).then_inc(s["kc_done"], 1)
                    probe_end(c * 3 + lead + 1)
                    probe_start()
                    dve.wait_ge(s["v_ready"], c + 2)
                    for i in range(2):
                        last = nc.vector.tensor_tensor(
                            out=V[:, bass.ds(c * TPC + 2 * i, 2), :, 0:HD],
                            in0=PS[:, 4 + i, :].rearrange("p (t h d) -> p t h d", t=2, h=H),
                            in1=b_uv[:, :].rearrange("p (h d) -> p h d", h=H).unsqueeze(1).broadcast_to([P, 2, H, HD]), op=ALU.add)
                    last.then_inc(s["v_done"], 1)
                    for n in range(2):
                        probe_end(c * 3 + lead + 2 + n)
                        probe_start()
                    chain.end(9)
            done = done + 9 * NCH

            chain.start(done)
            nc.vector.tensor_scalar(gt, scores[:, :], thr[:, :], None, ALU.is_gt, ALU.add, accum_out=small[:, 0:1])
            nc.vector.tensor_scalar(eq, scores[:, :], thr[:, :], None, ALU.is_equal, ALU.add, accum_out=small[:, 1:2]).then_inc(s["sum_ready"], 1)
            dve.wait_ge(s["sum_ready"], 1)
            chain(nc.vector.tensor_tensor_scan(out=rank, data0=ones[:, :], data1=eq, initial=0.0, op0=ALU.mult, op1=ALU.add))
            dve.wait_ge(s["sums_done"], 1)
            chain(nc.vector.tensor_scalar(small[:, 2:3], PS[:, 7, 1:2], -1.0, float(KEEP), ALU.mult, ALU.add))
            chain(nc.vector.tensor_tensor(out=small[:, 3:4], in0=small[:, 2:3], in1=PS[:, 7, 2:3], op=ALU.subtract))
            chain(nc.vector.scalar_tensor_tensor(out=taken, in0=rank, scalar=small[:, 3:4], in1=eq, op0=ALU.is_le, op1=ALU.mult))
            nc.vector.scalar_tensor_tensor(out=gt, in0=taken, scalar=1.0, in1=gt, op0=ALU.mult, op1=ALU.add,
                                           accum_out=small[:, 4:5]).then_inc(s["sum_ready"], 1)
            dve.wait_ge(s["sum_ready"], 2)
            chain(nc.vector.tensor_tensor_scan(out=rank, data0=ones[:, :], data1=gt, initial=0.0, op0=ALU.mult, op1=ALU.add))
            dve.wait_ge(s["sums_done"], 2)
            chain(nc.vector.tensor_scalar(rank, rank, PS[:, 7, 3:4], -1025.0, ALU.add, ALU.add))
            nc.vector.tensor_tensor(out=pos, in0=rank, in1=gt, op=ALU.mult).then_inc(s["pos_ready"], 1)
            dve.wait_ge(s["pos_turned"], 1)
            for i in range(2):
                last = nc.vector.tensor_scalar(posi[:, i::2, :], PS[:, 0, i * P:(i + 1) * P].rearrange("p (e r) -> p r e", e=E),
                                               1024.0, None, ALU.add)
            chain(last)
            nc.vector.tensor_scalar(loi, posi, LO - 1, None, ALU.bitwise_and)
            chain(nc.vector.tensor_scalar(hii, posi, 5, None, ALU.logical_shift_right))
            nc.vector.tensor_copy(lof, loi)
            nc.vector.tensor_copy(hif, hii).then_inc(s["pos_done"], 1)
            dve.wait_ge(s["pos_done"], 1)
            wide = [P, NT, E, HI]
            dve.wait_ge(s["qk_out0"], 192 * (NCH // 2))
            nc.vector.tensor_tensor(out=oh, in0=hif.unsqueeze(3).broadcast_to(wide),
                                    in1=ramp[:, 0:HI].unsqueeze(1).unsqueeze(1).broadcast_to(wide), op=ALU.is_equal).then_inc(s["oh_done"], 1)
            dve.wait_ge(s["parts_done"], 2 * NCH + 4)
            for half in range(2):
                es = slice(half * E // 2, (half + 1) * E // 2)
                wide = [P, NT, E // 2, LO]
                nc.vector.tensor_tensor(out=oh_lo[:, :, es, :], in0=lof[:, :, es].unsqueeze(3).broadcast_to(wide),
                                        in1=ramp[:, :].unsqueeze(1).unsqueeze(1).broadcast_to(wide),
                                        op=ALU.is_equal).then_inc(s["oh_done"], 1)
            dve.wait_ge(s["tok_ready"], 1)
            chain(nc.vector.tensor_copy(tok[0:LO, :, :, :].rearrange("p e w l -> p (e w l)"), PS[0:LO, 0, 0:E * 2 * HI]))
            nc.vector.scalar_tensor_tensor(out=idx32[0:LO, :, :], in0=tok[0:LO, :, 1, :], scalar=float(P), in1=tok[0:LO, :, 0, :],
                                           op0=ALU.mult, op1=ALU.add).then_inc(s["tok_done"], 1)
            done = chain.end(9)

            def negate_maxima(which, count):
                dve.wait_ge(s["side_done"], count)
                nc.vector.tensor_reduce(nmax, hmax[:, which, :].rearrange("p (t k) -> p t k", k=2), AX.X, ALU.max, negate=True).then_inc(s["nmax_done"], 1)

            def run_side(seq, count, bank_of, g, row):
                for k, u in enumerate(seq):
                    bank = bank_of(k)
                    dve.wait_ge(s["side_ready"], count + k + 1)
                    if u[0] == "max":
                        which = (g + u[2]) % 2
                        nc.vector.tensor_reduce(hmax[:, which, u[1]:u[1] + 1], PS[:, bank, :], AX.X, ALU.max).then_inc(s["side_done"], 1)
                        if u == ("max", 0, 2):
                            negate_maxima(1 - which, count + k)
                        elif u[1] == MAXES - 1 and seq[k + 1] == ("neg",):
                            negate_maxima(which, count + k + 1)
                    elif u[0] == "neg":
                        m = PS[0:G4 * QT, bank, 0:P]
                        chain(nc.vector.tensor_copy(nparts[:, 0, :], m))
                        chain(nc.vector.tensor_tensor(out=nrest, in0=m, in1=nparts[:, 0, :], op=ALU.subtract))
                        chain(nc.vector.tensor_copy(nparts[:, 1, :], nrest))
                        nc.vector.tensor_tensor(out=nparts[:, 2, :], in0=nrest, in1=nparts[:, 1, :], op=ALU.subtract).then_inc(s["side_done"], 1)
                    elif u[0] == "norm":
                        half, pg = u[1], (g - 1) % NG
                        o4 = PS[:, bank, :].rearrange("p (t h d) -> p t h d", t=4, h=G4)
                        dst = O[:, half * 4:half * 4 + 4, pg * G4 * HD:(pg + 1) * G4 * HD].rearrange("p t (h d) -> p t h d", h=G4)
                        chain(nc.vector.reciprocal(rsum[:, half, :, :], o4[:, :, :, HD]))
                        nc.vector.tensor_tensor(out=dst, in0=o4[:, :, :, 0:HD], in1=rsum[:, half, :, :].unsqueeze(3).broadcast_to([P, 4, G4, HD]),
                                                op=ALU.mult).then_inc(s["side_done"], 1)
                    elif u[0] == "turn":
                        kb, half = divmod(u[1], 2)
                        nc.vector.tensor_copy(OT[:, kb, half * 512:(half + 1) * 512], PS[:, bank, :]).then_inc(s["side_done"], 1)
                    else:
                        if u[1] == 0:
                            dve.wait_ge(s["accb_done"], row)
                        i = u[1]
                        nc.vector.tensor_tensor(out=outs[:, 2 * i:2 * i + 2, :], in0=PS[:, bank, :].rearrange("p (t d) -> p t d", t=2),
                                                in1=accb[:, 2 * i:2 * i + 2, :], op=ALU.add).then_inc(s["side_done"], 1)

            def yT_out(e):
                dve.wait_ge(s["yT_ready"], e + 1)
                for k in range(KB):
                    last = nc.vector.tensor_scalar(yT[:, k, :], PS[:, k, :], gamma[k], beta[k], ALU.mult, ALU.add)
                last.then_inc(s["yT_done"], 1)

            def expert(h, cc, more):
                e = h * 2 + cc
                chain.start(e + done)
                for i in range(PER_EXPERT):
                    dve.wait_ge(s["side_ready"], e * PER_EXPERT + i + 1)
                    nc.vector.tensor_reduce(hmax[:, 0, bass.ds(e * PER_EXPERT + i, 1)], PS[:, 6 + i % 2, :], AX.X,
                                            ALU.max).then_inc(s["side_done"], 1)
                if more:
                    yT_out(e + 1)
                else:
                    run_side(lead_uses, MAXES, lead_bank, NG - 1, None)
                dve.wait_ge(s[f"fc_in{cc}"], h * 64 + 64)
                dve.wait_ge(s["wsel_done"], e + 1)
                dve.wait_ge(s["res_free"], e + 1)
                dve.wait_ge(s["o_ready"], e + 2)
                chain(nc.vector.tensor_tensor(out=res[:, cc, :, :], in0=PS[:, 4:6, :].rearrange("p a (b d) -> p (a b) d", b=2),
                                              in1=b2_s[:, cc, :].unsqueeze(1).broadcast_to([P, 4, D]), op=ALU.add))
                for sl in range(4):
                    last = nc.vector.tensor_scalar(res[:, cc, sl, :], res[:, cc, sl, :], wsel[:, cc, sl:sl + 1], None, ALU.mult)
                last.then_inc(s["o_done"], 1)
                chain.end(1 if more else 4)

            yT_out(0)
            with dve.Fori(0, E // 2 - 1) as h:
                for cc in range(2):
                    expert(h, cc, True)
            for cc in range(2):
                expert(E // 2 - 1, cc, cc == 0)
            done = done + E + 3


            def chained(first, last):
                kinds = [u[0] for g in range(NG) for u in flat_stream(g, first, last)]
                return 3 * kinds.count("neg") + kinds.count("norm")

            C_FIRST, C_MID, C_LAST = chained(True, False), chained(False, False), chained(False, True)

            def attend_row(b, first, last):
                chain.start(done if first else b * C_MID + (done + C_FIRST - C_MID))
                for g in range(NG):
                    if first and g == 1:
                        for c in range(2):
                            dve.wait_ge(s[f"o_out{c}"], 64 * E // 2)
                    ahead = before_group(g, first, last)
                    run_side(flat_stream(g, first, last), side_base(b) + ahead, lambda k: side_bank(first, ahead + k), g, b)
                chain.end(chained(first, last))

            attend_row(0, True, False)
            with dve.Fori(1, B - 1) as b:
                attend_row(b, False, False)
            attend_row(B - 1, False, True)
            chain.start(done + C_FIRST + C_MID * (B - 2) + C_LAST)
            run_side(tail_uses, TAIL, lambda k: side_bank(True, TAIL - LEAD + k), 0, B)

        @block.tensor
        def _(pe):
            pe.sem_inc(s["xnT_ready"], 2)
            pe.sem_inc(s["v_ready"], 1)
            pe.sem_inc(s["o_ready"], 1)
            mm = nc.tensor.matmul
            pe.wait_ge(s["const_in"], 32)

            def turn_xn(c, cc):
                pe.wait_ge(s["xn_done"], c + 1)
                pe.wait_ge(s["xnT_done"], c + 1)
                for k in range(KB):
                    for t in range(TPC):
                        last = nc.tensor.transpose(PS[:, 2 * cc + k, t * P:(t + 1) * P], xn[:, cc, t, k * P:(k + 1) * P], ident)
                last.then_inc(s["xnT_ready"], 1)

            def gate_logits(c, cc):
                pe.wait_ge(s["xnT_done"], c + 3)
                pe.wait_ge(s["lg_done"], c + 1)
                for k in range(KB):
                    last = mm(PS[0:E, 4 + cc, :], w_gate[:, k, :], xnT[:, k, bass.ds(c * CH, CH)], start=k == 0, stop=k == KB - 1)
                last.then_inc(s["lg_ready"], 1)

            turn_xn(0, 0)
            with pe.Fori(0, NCH // 2 - 1) as b:
                for cc in range(2):
                    turn_xn(b * 2 + cc + 1, 1 - cc)
                    gate_logits(b * 2 + cc, cc)
            turn_xn(NCH - 1, 1)
            for cc in range(2):
                gate_logits(NCH - 2 + cc, cc)
            pe.wait_ge(s["w_in"], 16 * 12)

            def count(n):
                pe.wait_ge(s["cnt_ready"], n)
                mm(PS[:, 7, 0:1], same, cnt[:, :], start=True, stop=True).then_inc(s["cnt_sum"], 1)

            lead = BISECT - 3 * NCH

            def from_x(c, probe):
                def xT(k):
                    return xnT[:, k, bass.ds(c * CH, CH)]

                pe.wait_ge(s["qc_done"], c + 1)
                for bank, w in ((0, w_dq), (1, w_dkv)):
                    for k in range(KB):
                        last = mm(PS[:, bank, :], w[:, k, :], xT(k), start=k == 0, stop=k == KB - 1)
                    if bank == 0 and probe is not None:
                        count(probe)
                last.then_inc(s["ct_ready"], 1)
                pe.wait_ge(s["kc_done"], c + 1)
                for eo in range(2):
                    for k in range(KB):
                        last = mm(PS[:, 2 + eo, :], w_kr[:, k, eo * P:(eo + 1) * P], xT(k), start=k == 0, stop=k == KB - 1)
                    if eo == 0 and probe is not None:
                        count(probe + 1)
                last.then_inc(s["kr_ready"], 1)

            def from_latents(c):
                def single(bank, w, src):
                    return mm(PS[:, bank, :], w, src, start=True, stop=True)

                pe.wait_ge(s["ct_done"], c + 1)
                pe.wait_ge(s["v_done"], c + 1)
                for eo in range(2):
                    last = single(4 + eo, w_qr[:, eo * P:(eo + 1) * P], ctq)
                last.then_inc(s["qr_ready"], 1)
                count(c * 3 + lead + 1)
                for eo in range(2):
                    last = single(eo, w_uq[:, eo * P:(eo + 1) * P], ctq)
                last.then_inc(s["qc_ready"], 1)
                pe.wait_ge(s["kr_done"], c + 1)
                for eo in range(2):
                    last = single(2 + eo, w_uk[:, eo * P:(eo + 1) * P], ctkv)
                last.then_inc(s["kc_ready"], 1)
                pe.wait_ge(s["qr_done"], c + 1)
                for t in range(TPC):
                    last = mm(PS[:, 4 + t // 2, (t % 2) * D:(t % 2 + 1) * D], ctkv[:, t * P:(t + 1) * P], w_uv[:, :], start=True, stop=True)
                last.then_inc(s["v_ready"], 1)

            pe.wait_ge(s["xnT_done"], NCH + 2)
            from_x(0, None)
            for n in range(lead):
                count(n + 1)
            for i in range(2):
                last = nc.tensor.transpose(PS[:, 6, i * P:(i + 1) * P], scores[:, i * P:(i + 1) * P], ident)
            last.then_inc(s["wcol_ready"], 1)
            pe.wait_ge(s["lg_done"], NCH + 2)
            with pe.Fori(0, NCH - 1) as c:
                from_latents(c)
                from_x(c + 1, c * 3 + lead + 2)
            from_latents(NCH - 1)
            for n in range(2):
                count(BISECT - 1 + n)

            pe.wait_ge(s["sum_ready"], 1)
            mm(PS[:, 7, 1:2], same, small[:, 0:1], start=True, stop=True)
            mm(PS[:, 7, 2:3], before, small[:, 1:2], start=True, stop=True).then_inc(s["sums_done"], 1)
            pe.wait_ge(s["sum_ready"], 2)
            mm(PS[:, 7, 3:4], before, small[:, 4:5], start=True, stop=True).then_inc(s["sums_done"], 1)
            pe.wait_ge(s["v_done"], NCH + 1)
            pe.wait_ge(s["kc_done"], NCH + 1)
            pe.wait_ge(s["pos_ready"], 1)
            for i in range(2):
                last = nc.tensor.transpose(PS[:, 0, i * P:(i + 1) * P], pos[:, i * P:(i + 1) * P], ident)
            last.then_inc(s["pos_turned"], 1)
            pe.wait_ge(s["hi_part_done"], 1)
            for e in range(E):
                pe.wait_ge(s["hi_done"], 1 + e // (E // 2))
                pe.wait_ge(s["oh_done"], 2 + e // (E // 2))
                for t in range(NT):
                    last = mm(PS[0:LO, 0, e * 2 * HI:(e + 1) * 2 * HI], oh_lo[:, t, e, :], oh_hi[:, t, e, :, :].rearrange("p w l -> p (w l)"),
                              start=t == 0, stop=t == NT - 1)
            last.then_inc(s["tok_ready"], 1)

            def side_use(u, count, bank, g, n):
                pe.wait_ge(s["side_done"], count - (1 if g is None else 2))
                if g is None:
                    g = NG - 1
                if u[0] == "max":
                    q, k = (qkb[(g + u[2]) % NG][0:KROWS, o, :, :] for o in range(2))
                    j, rest = divmod(u[1], 2 * QT)
                    qt, half = divmod(rest, 2)
                    ins = mm(PS[:, bank, :], q[:, j, qt * P:(qt + 1) * P], k[:, j, half * 512:(half + 1) * 512], start=True, stop=True)
                elif u[0] == "neg":
                    pe.wait_ge(s["nmax_done"], n + 2)
                    ins = nc.tensor.transpose(PS[0:G4 * QT, bank, 0:P], nmax, ident)
                elif u[0] == "norm":
                    pe.wait_ge(s["pv_done"], 2 * n - 1 + u[1])
                    for t in range(4):
                        q0 = (u[1] * 4 + t) * P
                        ins = nc.tensor.transpose(PS[:, bank, t * P:(t + 1) * P], pvs[:, q0:q0 + P], ident)
                elif u[0] == "turn":
                    if u[1] == 0 and isinstance(count, int) and count >= TAIL:
                        pe.wait_ge(s["side_done"], count)
                    kb, half = divmod(u[1], 2)
                    for t in range(4):
                        ins = nc.tensor.transpose(PS[:, bank, t * P:(t + 1) * P], O[:, half * 4 + t, kb * P:(kb + 1) * P], ident)
                else:
                    if u[1] == 0 and isinstance(count, int) and count >= TAIL:
                        pe.wait_ge(s["side_done"], count)
                    for t in range(2):
                        q0 = (u[1] * 2 + t) * P
                        for kb in range(KB):
                            ins = mm(PS[:, bank, t * D:(t + 1) * D], OT[:, kb, q0:q0 + P], w_o[:, kb, :], start=kb == 0, stop=kb == KB - 1)
                ins.then_inc(s["side_ready"], 1)

            def turn_rows(e, h, cc):
                pe.wait_ge(s[f"got_in{cc}"], h * 64 + 64)
                for k in range(KB):
                    for sl in range(4):
                        last = nc.tensor.transpose(PS[:, k, sl * P:(sl + 1) * P], got[:, cc, sl, k * P:(k + 1) * P], ident)
                last.then_inc(s["yT_ready"], 1)

            def expert(h, cc, more):
                e = h * 2 + cc
                pe.wait_ge(s["yT_done"], e + 1)
                pe.wait_ge(s[f"fc_in{cc}"], h * 64 + 64)
                for f in range(FF // P):
                    if f >= 2:
                        pe.wait_ge(s["hT_done"], e * 8 + f - 1)
                    for k in range(KB):
                        last = mm(PS[:, 2 + f % 2, :], fc1_s[cc][:, k, f * P:(f + 1) * P], yT[:, k, :], start=k == 0, stop=k == KB - 1)
                    last.then_inc(s["hT_ready"], 1)
                    if f == 0:
                        pe.wait_ge(s["o_done"], e + 1)
                        pe.wait_ge(s["qk_in0"], 18 * 16)
                    if f >= 2:
                        pe.wait_ge(s["side_done"], e * PER_EXPERT + f - 1)
                    qt, half = cc * QT // 2 + f // 2, f % 2
                    q, k2 = (qkb[0][0:KROWS, o, bass.ds(h, 1), :].rearrange("p h s -> p (h s)") for o in range(2))
                    mm(PS[:, 6 + f % 2, :], q[:, qt * P:(qt + 1) * P], k2[:, half * 512:(half + 1) * 512],
                       start=True, stop=True).then_inc(s["side_ready"], 1)
                if more:
                    turn_rows(e + 1, h + cc, 1 - cc)
                else:
                    pe.wait_ge(s["qk_in1"], 18 * 16)
                for sl in range(4):
                    for f in range(FF // P):
                        if sl == 0:
                            pe.wait_ge(s["hT_done"], e * 8 + f + 1)
                        k, at_place = divmod(sl * (FF // P) + f - 4, 2)
                        if not more and at_place == 0 and 0 <= k < len(lead_uses):
                            side_use(lead_uses[k], MAXES + k, lead_bank(k), None, -1)
                        last = mm(PS[:, 4 + sl // 2, sl % 2 * D:(sl % 2 + 1) * D], hT[:, f, sl * P:(sl + 1) * P], fc2_s[cc][:, f, :], start=f == 0, stop=f == FF // P - 1)
                last.then_inc(s["o_ready"], 1)

            pe.wait_ge(s["tok_done"], 1)
            turn_rows(0, 0, 0)
            with pe.Fori(0, E // 2 - 1) as h:
                for cc in range(2):
                    expert(h, cc, True)
            for cc in range(2):
                expert(E // 2 - 1, cc, cc == 0)

            pe.wait_ge(s["o_done"], E + 1)
            pe.wait_ge(s["ones_rows_done"], NG)

            def values(g, n, kt, quarter, first):
                if quarter == 0:
                    pe.wait_ge(s["exp_done"], n * HALVES + (kt + 1) * G4 * 2)
                    if kt == 0:
                        pe.wait_ge(s["vg_done"], n + 1)
                if kt == 0 and quarter % 2 == 0 and not (first and g == 0):
                    pe.wait_ge(s["pv_done"], 2 * n - 1 + quarter // 2)
                half, q0 = quarter // 2, quarter % 2 * 256
                for j in range(G4):
                    ins = mm(PS[LO * j:LO * j + VW, 4 + half, q0:q0 + 256], Vg[:, g % 2, kt, j, :], expP[:, kt % 2, j, quarter * 256:(quarter + 1) * 256],
                             start=kt == 0 and q0 == 0, stop=kt == KT - 1, skip_group_check=True)
                if quarter == 1 and kt == KT - 1:
                    ins.then_inc(s["pv_half"], 1)
                if quarter == 3:
                    ins.then_inc(s["pv_ready"], 1)

            def attend_row(b, first, last):
                for g in range(NG):
                    n = b * NG + g
                    k = before_group(g, first, last)
                    pe.wait_ge(s["aug_in"], n * 48 + 48)
                    if not (last and g >= NG - 2):
                        pe.wait_ge(s[f"qk_in{(g + 2) % NG}"], (b + (g + 2) // NG) * 288 + 288)
                    for st, places in enumerate(side_stream(g, first, last)):
                        kt, j = divmod(st, G4)
                        for place, todo in enumerate(places):
                            if place == 1:
                                for half in range(2):
                                    number = n * HALVES + st * 2 + half
                                    if g == 0 and st + half == 0:
                                        if not first:
                                            pe.wait_ge(s["exp_done"], number)
                                    elif not (first and g == 0 and st * 2 + half < 3):
                                        pe.wait_ge(s["exp_done"], number - 2)
                                    mm(PS[:, score_bank(g, st, half), :], qkb[g][0:AUG, 1, j, kt * P:(kt + 1) * P],
                                       qkb[g][0:AUG, 0, j, half * 512:(half + 1) * 512], start=True, stop=True).then_inc(s["sc_ready"], 1)
                            if place == 2 and kt > 0:
                                values(g, n, kt - 1, j, first)
                            if place == 2 and kt == 0 and not (first and g == 0):
                                values((g - 1) % NG, n - 1, KT - 1, j, first)
                            for u in todo:
                                side_use(u, side_base(b) + k, side_bank(first, k), g, n)
                                k += 1

            attend_row(0, True, False)
            with pe.Fori(1, B - 1) as b:
                attend_row(b, False, False)
            attend_row(B - 1, False, True)
            for quarter in range(4):
                values(NG - 1, B * NG - 1, KT - 1, quarter, False)
            for k, u in enumerate(tail_uses):
                side_use(u, TAIL + k, side_bank(True, TAIL - LEAD + k), 0, B * NG)


def kernel(**inputs):
    import concourse.bacc as bacc
    from concourse.bass_utils import run_bass_kernel_spmd

    a = {n.removeprefix("L0_"): np.asarray(v) for n, v in inputs.items()}

    def apart(w):
        return np.ascontiguousarray(np.concatenate([w[..., 0::2], w[..., 1::2]], -1))

    def halves(v):
        return np.ascontiguousarray(v.reshape(2, P).T)

    cols = [a["attn_Wd_q_b"][:, None], a["attn_Wd_kv_b"][:, None]]
    cols += [halves(apart(a[f"attn_{n}_b"])) for n in ("Wu_q", "Wq_r", "Wk_r", "Wu_k")]
    cols += [halves(a["ffn_ln_gamma"]), halves(a["ffn_ln_beta"])]
    arrays = {
        "x": a["attn_x"].reshape(TOK, D), "wdq": a["attn_Wd_q_w"], "wdkv": a["attn_Wd_kv_w"],
        "wuq": apart(a["attn_Wu_q_w"]), "wqr": apart(a["attn_Wq_r_w"]), "wkr": apart(a["attn_Wk_r_w"]), "wuk": apart(a["attn_Wu_k_w"]),
        "wuv": a["attn_Wu_v_w"], "wo": a["attn_Wo_w"], "cols": np.concatenate(cols, 1), "buv": a["attn_Wu_v_b"], "bo": a["attn_Wo_b"],
        "gate": a["ffn_gate_w"].T, "fc1": a["ffn_fc1s"].transpose(0, 2, 1),
        "b1": a["ffn_b1s"].reshape(E, FF // P, P).transpose(0, 2, 1), "fc2": a["ffn_fc2s"].transpose(0, 2, 1), "b2": a["ffn_b2s"],
        "const": constants(),
    }
    arrays = {n: np.ascontiguousarray(v) for n, v in arrays.items()}
    nc = bacc.Bacc("TRN2", target_bir_lowering=False, num_devices=1)
    aps = [nc.dram_tensor(n, v.shape, mybir.dt.from_np(v.dtype), kind="ExternalInput").ap() for n, v in arrays.items()]
    acc = nc.dram_tensor("acc", (TOK, D), F32, kind="Internal").ap()
    table = nc.dram_tensor("table", (TOK, ROW), F32, kind="Internal").ap()
    qk = nc.dram_tensor("qk", (2, B, 2, H, 3, PAIR, S), BF16, kind="Internal").ap()
    out = nc.dram_tensor("out", (B, S, D), F32, kind="ExternalOutput").ap()
    program(nc, *aps, acc, table, qk, out.rearrange("b s d -> (b s) d"))
    result = run_bass_kernel_spmd(nc, [arrays], core_ids=[0])
    return result.results[0]["out"]
```

```python
from contextlib import ExitStack

import numpy as np
import concourse.bass as bass
from concourse import mybir

F32 = mybir.dt.float32
BF16 = mybir.dt.bfloat16
I32 = mybir.dt.int32
U32 = mybir.dt.uint32
ALU = mybir.AluOpType
ACT = mybir.ActivationFunctionType
AX = mybir.AxisListType

P = 128
B, S, D = 4, 1024, 256
TOK = B * S
H, HD = 16, 16
LAT = 128
SCALE = float(np.float32(1.0) / np.sqrt(np.float32(H + LAT + LAT)))
E, FF = 8, 1024
KEEP = TOK // E
EPS = 1e-5
CH = 512
NCH = TOK // CH
TPC = CH // P
NT = TOK // P
KB = D // P
ROW = D + E
RUN = TOK // 16
G4 = 4
NG = H // G4
KT = S // P
HALVES = 2 * G4 * KT
QT = S // P
VW = HD + 1
ARENA = 18688
TERMS = 6
PAIR = HD // 2
KROWS = TERMS * HD
AUG = KROWS + 3
BISECT = 26
LO, HI = 32, 16


def rope_tables():
    pos = np.arange(S, dtype=np.float32)[:, None]
    ids = np.arange(D // 2, dtype=np.float32)
    theta = (np.float32(10000.0) ** (np.float32(-2.0) * ids)) / np.float32(D // 2)
    r = (pos * theta[None, :].astype(np.float32)).astype(np.float32)
    return np.cos(r).T.astype(np.float32), -np.sin(r).T.astype(np.float32), np.sin(r).T.astype(np.float32)


def constants():
    i = np.arange(P)
    same = i[:, None] // 16 == i[None, :] // 16
    parts = [np.eye(P), same, same & (i[:, None] < i[None, :]), np.tile(np.arange(LO), (P, 1)), i[:, None]]
    return np.ascontiguousarray(np.concatenate([p.astype(np.float32) for p in parts] + list(rope_tables()), 1))


class Chain:

    def __init__(self, eng, sem):
        self.eng, self.sem, self.base, self.k = eng, sem, 0, 0

    def start(self, base):
        self.base, self.k = base, 0

    def __call__(self, ins):
        ins.then_inc(self.sem, 1)
        self.k += 1
        self.eng.wait_ge(self.sem, self.base + self.k)

    def end(self, n):
        assert self.k == n, (self.k, n)
        return self.base + n


SLOTS = 3
MAXES = 2 * G4 * QT
AHEAD = 14
SCORES = (0, 1, 2)
SIDE = (3, 7, 6)


def side_stream(g, first, last):
    steps = G4 * KT
    more = [] if last and g == NG - 1 else [("max", n, 1) for n in range(AHEAD, MAXES)]
    late = [("neg",)] if more else []
    if not (last and g >= NG - 2):
        late = [("max", 0, 2), ("max", 1, 2)] + late + [("max", n, 2) for n in range(2, AHEAD)]
    early = [] if first and g == 0 else [("norm", 0), ("norm", 1)]
    if g == 0 and not first:
        early += more[16:18] + [("turn", n) for n in range(4)]
        seq = more[:16] + early + more[18:] + late
    else:
        if g == 1 and not first:
            early += [("out", n) for n in range(4)]
        seq = more[:16] + early + more[16:] + late
    begin = 0 if more else 8
    busy = steps - begin - (0 if len(late) > 1 or not more else AHEAD // 2)
    out = [[[] for _ in range(SLOTS)] for _ in range(steps)]
    per = len(seq) / busy
    at = 0
    for st in range(begin, steps):
        take = min(len(seq), int(per * (st - begin + 1) + 1e-6)) - at
        places = {0: [], 1: [2], 2: [0, 1], 3: [0, 1, 2]}[take]
        for p in places:
            out[st][p].append(seq[at])
            at += 1
    assert at == len(seq)
    return out


def uses(first, last):
    return [sum(len(p) for st in side_stream(g, first, last) for p in st) for g in range(NG)]


def program(nc, x, wdq, wdkv, wuq, wqr, wkr, wuk, wuv, wo, cols, buv, bo, gate, fc1, b1, fc2, b2, const,
            acc, table, qk, out):
    ctx = ExitStack()
    with ctx:
        def sb(name, shape, dt=F32):
            return ctx.enter_context(nc.sbuf_tensor(name, shape, dt))

        def sem(name):
            return ctx.enter_context(nc.semaphore(name))

        consts = sb("consts", [P, 3 * P + LO + 1 + 3 * S])
        ident, same, before = (consts[:, n * P:(n + 1) * P] for n in range(3))
        ramp = consts[:, 3 * P:3 * P + LO]
        part_id = consts[:, 3 * P + LO:3 * P + LO + 1]
        cos, nsin, sin = (consts[:, 3 * P + LO + 1 + n * S:3 * P + LO + 1 + (n + 1) * S] for n in range(3))
        w_dq = sb("w_dq", [P, KB, LAT])
        w_dkv = sb("w_dkv", [P, KB, LAT])
        w_uq = sb("w_uq", [P, D])
        w_qr = sb("w_qr", [P, D])
        w_kr = sb("w_kr", [P, KB, D])
        w_uk = sb("w_uk", [P, D])
        w_uv = sb("w_uv", [P, D])
        w_o = sb("w_o", [P, KB, D])
        w_gate = sb("w_gate", [P, KB, E])
        col = sb("col", [P, 14])
        b_dq, b_dkv = col[:, 0:1], col[:, 1:2]
        b_uq, b_qr, b_kr, b_uk, gamma, beta = ([col[:, n:n + 1], col[:, n + 1:n + 2]] for n in range(2, 14, 2))
        b_uv = sb("b_uv", [P, D])
        b_o = sb("b_o", [P, D])
        V = sb("V", [P, NT, H, VW])
        Vg = sb("Vg", [P, 2, KT, G4, VW])
        marks = sb("marks", [P, RUN])
        idx = sb("idx", [P, E, 4], U32)
        scores = sb("scores", [P, RUN])
        minus_half = sb("minus_half", [P, TPC])
        eps = sb("eps", [P, TPC])
        held = sb("held", [P, 1])
        ones = sb("ones", [P, RUN])
        thr = sb("thr", [P, 1])
        step = sb("step", [P, 1])
        cand = sb("cand", [P, 1])
        cnt = sb("cnt", [P, 1])
        stat = sb("stat", [P, 2, 2, TPC, 6])
        mv = sb("mv", [P, 2, 2, TPC, 2])
        rstd = sb("rstd", [P, 2, 2, TPC])
        ve = sb("ve", [P, 2, 2, TPC])
        shift = sb("shift", [P, 2, TPC])
        zeros = sb("zeros", [P, TPC])
        small = sb("small", [P, 16])
        wtok = sb("wtok", [P, NT, E])

        expP = sb("expP", [P, 2, G4, S])
        flat = expP[:, :, :, :].rearrange("p a h s -> p (a h s)")
        fc1_s = [flat[:, n * 4096:n * 4096 + 2048].rearrange("p (k f) -> p k f", k=KB) for n in range(2)]
        fc2_s = [flat[:, n * 4096 + 2048:(n + 1) * 4096].rearrange("p (k d) -> p k d", k=FF // P) for n in range(2)]
        logits = flat[0:E, 4096:4096 + TOK]
        qkbuf = sb("qkbuf", [P, 2, 2, G4, S], BF16)
        tu = qkbuf[:, :, :, :, :].rearrange("p a b h s -> p (a b h s)").bitcast(F32)
        xs = tu.rearrange("p (c t d) -> p c t d", c=NCH, t=TPC)
        tu = tu.rearrange("p (c o w e t) -> p c o w e t", c=2, o=2, w=2, e=2)
        arena = sb("arena", [P, ARENA])
        at = [0]

        def view(n, dt=F32):
            a = arena[:, at[0]:at[0] + n]
            at[0] += n
            assert at[0] <= ARENA, at[0]
            return a if dt == F32 else a.bitcast(dt)

        xnT = view(KB * TOK).rearrange("p (k t) -> p k t", k=KB)
        after_xnT = at[0]
        xn = view(2 * TPC * D).rearrange("p (c t d) -> p c t d", c=2, t=TPC)
        rows = view(2 * TPC * D).rearrange("p (c t d) -> p c t d", c=2, t=TPC)
        base = view(2 * TPC * D).rearrange("p (c t d) -> p c t d", c=2, t=TPC)
        at[0] = after_xnT
        full = view(2 * 2 * 2 * CH).rearrange("p (c o e t) -> p c o e t", c=2, o=2, e=2)
        parts = view(2 * 2 * 3 * CH, BF16).rearrange("p (c o r e t) -> p c o r e t", c=2, o=2, r=3, e=2)
        latents = Vg[:, :, :, :, :].rearrange("p a k h d -> p (a k h d)")
        ctq, ctkv = latents[:, 0:CH], latents[:, CH:2 * CH]
        at[0] = 0
        gt = view(RUN)
        eq = view(RUN)
        rank = view(RUN)
        taken = view(RUN)
        pos = view(RUN)
        posi = view(RUN, I32).rearrange("p (t e) -> p t e", t=NT)
        loi = view(RUN, I32).rearrange("p (t e) -> p t e", t=NT)
        hii = view(RUN, I32).rearrange("p (t e) -> p t e", t=NT)
        lof = view(RUN // 2, BF16).rearrange("p (t e) -> p t e", t=NT)
        hif = view(RUN // 2, BF16).rearrange("p (t e) -> p t e", t=NT)
        tok = view(E * 2 * HI).rearrange("p (e w l) -> p e w l", e=E, w=2)
        token = view(E * HI).rearrange("p (e l) -> p e l", e=E)
        assert at[0] <= (NCH - 2) * CH, at[0]
        at[0] = TOK
        oh = view(NT * E * HI // 2, BF16).rearrange("p (l t e) -> p l t e", t=NT, e=E)
        assert at[0] <= TOK + (NCH - 2) * CH, at[0]
        oh_hi, oh_lo = (flat[:, n * 4096:(n + 1) * 4096].bitcast(BF16) for n in range(2))
        oh_hi = oh_hi.rearrange("p (w l t e) -> p w l t e", t=NT, e=E, w=2)
        oh_lo = oh_lo.rearrange("p (l t e) -> p l t e", t=NT, e=E)
        at[0] = 0
        hT = view(FF // P * KEEP).rearrange("p (f s) -> p f s", f=FF // P)
        yT = view(KB * KEEP).rearrange("p (k s) -> p k s", k=KB)
        got = view(2 * 4 * ROW).rearrange("p (c s r) -> p c s r", c=2, s=4)
        wsel = view(2 * 4).rearrange("p (c s) -> p c s", c=2)
        b2_s = view(2 * D).rearrange("p (c d) -> p c d", c=2)
        b1_s = view(2 * FF // P).rearrange("p (c f) -> p c f", c=2)
        assert at[0] <= after_xnT, at[0]
        res = view(2 * 4 * D).rearrange("p (c s d) -> p c s d", c=2, s=4)
        hmax = marks[:, 0:2 * MAXES].rearrange("p (c n) -> p c n", c=2)
        nmax = marks[:, 2 * MAXES:2 * MAXES + G4 * QT]
        rsum = view(2 * 16).rearrange("p (c t h) -> p c t h", c=2, t=4)
        nrest = view(P)[0:G4 * QT, :]
        nparts = view(3 * P // 2, BF16)[0:G4 * QT, :].rearrange("p (r q) -> p r q", r=3)
        assert at[0] <= ARENA - 2 * 4096, at[0]
        at[0] = 0
        accb = view(QT * D).rearrange("p (t d) -> p t d", t=QT)
        outs = view(QT * D).rearrange("p (t d) -> p t d", t=QT)
        O = view(QT * D).rearrange("p (t d) -> p t d", t=QT)
        OT = view(KB * S).rearrange("p (k t) -> p k t", k=KB)
        pvs = view(S)
        qkb = [qkbuf[:, n, :, :, :] for n in range(2)]
        qkb += [arena[:, ARENA - (2 - n) * 4096:ARENA - (1 - n) * 4096].bitcast(BF16).rearrange("p (o h s) -> p o h s", o=2, h=G4)
                for n in range(2)]

        PS = ctx.enter_context(nc.psum_tensor("PS", [P, 8, 512], F32))

        PROBED = NCH - 2
        lead = BISECT - 4 * PROBED

        names = """const_in w_in stored x_in0 x_in1 mv1_done mv2_done rstd1_done rstd2_done shift_done xn_done rows_done base_done xnT_ready xnT_done lg_ready lg_done
            acc_out0 acc_out1 tab_out0 tab_out1 s_in tanh_done
            cnt_ready cnt_sum ct_ready ct_done kr_ready qr_ready qc_ready kc_ready v_ready kr_done qr_done qc_done
            kc_done v_done added cast1 cast2 resid parts_done qk_out0 qk_out1 parts_free res_free
            sum_ready sums_done pos_ready pos_turned pos_done oh_done hi_done hi_part_done tok_ready tok_done idx_ready idx_done wcol_ready wcol_done wcol_out
            fc_in0 fc_in1 got_in0 got_in1 wsel_done yT_ready yT_done hT_ready hT_done o_ready o_done o_out0 o_out1
            qk_in0 qk_in1 qk_in2 qk_in3 aug_in ones_rows_done side_ready side_done nmax_done sc_ready exp_done pv_half pv_ready pv_done
            vg_done accb_in accb_done out_out ones_done dve_chain pool_chain""".split()
        s = {n: sem(n) for n in names}

        block = ctx.enter_context(nc.Block())

        PER_EXPERT = MAXES // E
        def score_bank(g, st, half):
            return SCORES[(g * HALVES + st * 2 + half) % 3]

        lead_uses = [("max", 0, 2), ("max", 1, 2), ("neg",)] + [("max", n, 2) for n in range(2, AHEAD)]
        LEAD = MAXES + len(lead_uses)
        U_FIRST, U_MID = sum(uses(True, False)), sum(uses(False, False))

        def side_base(b):
            if isinstance(b, int):
                return LEAD if b == 0 else LEAD + U_FIRST + (b - 1) * U_MID
            return b * U_MID + (LEAD + U_FIRST - U_MID)

        assert U_MID % 3 == 0

        def side_bank(first, k):
            return SIDE[(k if first else U_FIRST + k) % 3]

        def lead_bank(k):
            return 6 + k % 2

        def flat_stream(g, first, last):
            return [u for st in side_stream(g, first, last) for p in st for u in p]

        def before_group(g, first, last):
            return sum(uses(first, last)[:g])

        def at_neg(g, first, last):
            return before_group(g, first, last) + flat_stream(g, first, last).index(("neg",)) + 1

        TAIL = side_base(B - 1) + sum(uses(False, True))
        tail_uses = [("norm", 0), ("norm", 1)] + [("turn", n) for n in range(4)] + [("out", n) for n in range(4)]
        tail_needs = {2: 1, 4: 2, 6: 4, 8: 6}

        @block.sync
        def _(sp):
            x_c = x.rearrange("(c t p) d -> c p t d", p=P, t=TPC)
            acc_c = acc.rearrange("(c t p) d -> c p t d", p=P, t=TPC)
            tab_c = table[:, 0:D].rearrange("(c t p) d -> c p t d", p=P, t=TPC)
            sp.sem_inc(s["parts_free"], 2)
            sp.sem_inc(s["stored"], 2)
            first = 3 * P + LO + 1
            for c in range(NCH):
                if c >= 2:
                    sp.wait_ge(s[f"x_in{c % 2}"], c // 2 * 16)
                sp.dma_start(xs[:, c, :, :], x_c[c, :, :, :]).then_inc(s[f"x_in{c % 2}"], 16)
                if c == 0:
                    sp.dma_start(consts[:, 0:first], const[:, 0:first]).then_inc(s["const_in"], 16)
                    sp.dma_start(w_gate[:, :, :], gate.rearrange("(k p) e -> p k e", p=P)).then_inc(s["const_in"], 16)
            loads = [(consts[:, first:], const[:, first:]), (col[:, :], cols),
                     (w_dq[:, :, :], wdq.rearrange("(k p) m -> p k m", p=P)), (w_dkv[:, :, :], wdkv.rearrange("(k p) m -> p k m", p=P)),
                     (w_uq[:, :], wuq), (w_qr[:, :], wqr), (w_kr[:, :, :], wkr.rearrange("(k p) m -> p k m", p=P)),
                     (w_uk[:, :], wuk), (w_uv[:, :], wuv), (w_o[:, :, :], wo.rearrange("(k p) m -> p k m", p=P)),
                     (b_uv[:, :], buv.partition_broadcast(P)), (b_o[:, :], bo.partition_broadcast(P))]

            for c in range(NCH):
                cc = c % 2
                sp.wait_ge(s["base_done"], c + 3)
                sp.dma_start(acc_c[c, :, :, :], base[:, cc, :, :]).then_inc(s[f"acc_out{cc}"], 16)
                if c == NCH - 1:
                    sp.wait_ge(s["lg_done"], NCH + 2)
                    sp.dma_start(scores[:, :], logits.rearrange("e (r t) -> e r t", t=RUN)).then_inc(s["s_in"], 16)
                sp.wait_ge(s["rows_done"], c + 3)
                sp.dma_start(tab_c[c, :, :, :], rows[:, cc, :, :]).then_inc(s[f"tab_out{cc}"], 16)
                for dst, src in loads[2 * c:2 * c + 2]:
                    sp.dma_start(dst, src).then_inc(s["w_in"], 16)
                if c < NCH - 2:
                    sp.wait_ge(s[f"acc_out{cc}"], c // 2 * 16 + 16)
                    sp.wait_ge(s[f"tab_out{cc}"], c // 2 * 16 + 16)
                    sp.sem_inc(s["stored"], 1)

            def load_expert(e, cc):
                sem_in = s[f"fc_in{cc}"]
                one = bass.ds(e, 1)
                sp.dma_start(fc1_s[cc], fc1[one, :, :].rearrange("e (k p) f -> p (e k) f", p=P)).then_inc(sem_in, 16)
                sp.dma_start(fc2_s[cc], fc2[one, :, :].rearrange("e (k p) d -> p (e k) d", p=P)).then_inc(sem_in, 16)

            def load_biases(e, cc):
                sem_in = s[f"fc_in{cc}"]
                one = bass.ds(e, 1)
                sp.dma_start(b1_s[:, cc, :], b1[one, :, :].rearrange("e p f -> (e p) f")).then_inc(sem_in, 16)
                sp.dma_start(b2_s[:, cc, :], b2[one, :].rearrange("e d -> (e d)").partition_broadcast(P)).then_inc(sem_in, 16)

            sp.wait_ge(s["wcol_done"], 1)
            with nc.allow_non_contiguous_dma(reason="eight scores of a token"):
                sp.dma_start(table[:, D:ROW].rearrange("(t p) e -> p t e", p=P), wtok[:, :, :]).then_inc(s["wcol_out"], 16)
            def store_parts(b, cc):
                sp.wait_ge(s["parts_done"], (b * 2 + cc) * 2 + 6)
                for o in range(2):
                    for r in range(3):
                        for eo in range(2):
                            dst = qk[o, bass.ds(b, 1), eo, :, r, :, cc * CH:(cc + 1) * CH].rearrange("b h j t -> (b h) j t")
                            sp.dma_start(dst, parts[:, cc, o, r, eo, :]).then_inc(s[f"qk_out{cc}"], 16)

            with sp.Fori(0, NCH // 2 - 1) as b:
                for cc in range(2):
                    store_parts(b, cc)
                    sp.wait_ge(s[f"qk_out{cc}"], b * 192 + 192)
                    sp.sem_inc(s["parts_free"], 1)

            def load_qk(b, g):
                sem_in = s[f"qk_in{g}"]
                for eo in range(2):
                    row = eo * KROWS // 2
                    for n0, n in ((0, 3), (3, 2), (5, 1)):
                        src = qk[0, bass.ds(b, 1), eo, g * G4:(g + 1) * G4, 0:n, :, :].rearrange("b h r j t -> (b r j) h t")
                        lo = row + n0 * PAIR
                        sp.dma_start(qkb[g][lo:lo + n * PAIR, 0, :, :], src).then_inc(sem_in, 16)
                    for n, part in enumerate((0, 0, 0, 1, 1, 2)):
                        src = qk[1, bass.ds(b, 1), eo, g * G4:(g + 1) * G4, part, :, :].rearrange("b h j t -> (b j) h t")
                        lo = row + n * PAIR
                        sp.dma_start(qkb[g][lo:lo + PAIR, 1, :, :], src).then_inc(sem_in, 16)

            sp.wait_ge(s["added"], 2 * (NCH - 1))
            load_qk(0, 0)
            sp.wait_ge(s["tok_ready"], 1)
            load_expert(0, 0)
            load_biases(0, 0)
            store_parts(NCH // 2 - 1, 0)
            load_expert(1, 1)
            load_biases(1, 1)
            store_parts(NCH // 2 - 1, 1)
            for e in range(E - 2):
                if 1 <= e < NG:
                    if e == 1:
                        for c in range(2):
                            sp.wait_ge(s[f"qk_out{c}"], 192 * (NCH // 2))
                    sp.wait_ge(s["yT_ready"], e + 2)
                    load_qk(0, e)
                sp.wait_ge(s["o_ready"], e + 2)
                sp.wait_ge(s["o_done"], e + 2)
                load_expert(e + 2, e % 2)
                load_biases(e + 2, e % 2)

            def load_aug(g, count):
                sp.wait_ge(s["side_done"], count)
                for part in range(3):
                    sp.dma_start(qkb[g][KROWS + part:KROWS + part + 1, 0, :, :].rearrange("p h (t q) -> p (h t) q", q=P),
                                 nparts[:, part, :]).then_inc(s["aug_in"], 16)

            load_aug(0, MAXES + 3)

            def attend_row(b, first, last):
                for g in range(NG):
                    if g == 0 and not first:
                        sp.dma_start(accb, acc[bass.ds((b - 1) * S, S), :].rearrange("(t p) d -> p t d", p=P)).then_inc(s["accb_in"], 16)
                    if g == 2 and not first:
                        sp.wait_ge(s["side_done"], side_base(b) + before_group(2, first, last))
                        sp.dma_start(out[bass.ds((b - 1) * S, S), :].rearrange("(t p) d -> p t d", p=P), outs).then_inc(s["out_out"], 16)
                    if not (last and g == NG - 1):
                        load_aug((g + 1) % NG, side_base(b) + at_neg(g, first, last))
                    if g == 3 and not first:
                        sp.wait_ge(s["out_out"], b * 16)
                    if not last:
                        sp.wait_ge(s["sc_ready"], (b * NG + g + 1) * HALVES)
                        load_qk(b + 1, g)

            for c in range(2):
                sp.wait_ge(s[f"o_out{c}"], 64 * E // 2)
            attend_row(0, True, False)
            with sp.Fori(1, B - 1) as b:
                attend_row(b, False, False)
            attend_row(B - 1, False, True)
            sp.dma_start(accb, acc[(B - 1) * S:B * S, :].rearrange("(t p) d -> p t d", p=P)).then_inc(s["accb_in"], 16)
            for half in range(2):
                sp.wait_ge(s["side_done"], TAIL + len(tail_uses) - 2 + 2 * half)
                rows_of = slice((B - 1) * S + half * S // 2, (B - 1) * S + (half + 1) * S // 2)
                sp.dma_start(out[rows_of, :].rearrange("(t p) d -> p t d", p=P), outs[:, half * QT // 2:(half + 1) * QT // 2, :]).then_inc(s["out_out"], 16)
            sp.wait_ge(s["out_out"], 16 * (B + 1))
            for c in range(2):
                sp.wait_ge(s[f"acc_out{c}"], 16 * (NCH // 2))
                sp.wait_ge(s[f"tab_out{c}"], 16 * (NCH // 2))

        @block.gpsimd
        def _(pool):
            chain = Chain(pool, s["pool_chain"])
            nc.gpsimd.memset(minus_half[:, :], -0.5)
            nc.gpsimd.memset(eps[:, :], EPS)
            nc.gpsimd.memset(zeros[:, :], 0.0)
            nc.gpsimd.memset(ones[:, :], 1.0)
            nc.gpsimd.memset(V[:, :, :, HD:VW], 1.0).then_inc(s["ones_done"], 1)
            pool.wait_ge(s["ones_done"], 1)
            pool.sem_inc(s["base_done"], 2)
            pool.sem_inc(s["shift_done"], 2)
            pool.sem_inc(s["parts_done"], 4)

            def rsqrt(c, cc, which):
                pool.wait_ge(s[f"mv{which + 1}_done"], c + 1)
                chain(nc.gpsimd.tensor_tensor(out=ve[:, cc, which, :], in0=mv[:, cc, which, :, 1], in1=eps[:, :], op=ALU.add))
                nc.gpsimd.tensor_tensor(out=rstd[:, cc, which, :], in0=ve[:, cc, which, :], in1=minus_half[:, :],
                                        op=ALU.pow).then_inc(s[f"rstd{which + 1}_done"], 1)

            def norm_chunk(c, cc, more):
                chain.start(c * 3 + 1)
                if more:
                    rsqrt(c + 1, 1 - cc, 0)
                pool.wait_ge(s["xn_done"], c + 1)
                pool.wait_ge(s["stored"], c + 1)
                nc.gpsimd.tensor_tensor(out=base[:, cc, :, :], in0=xs[:, bass.ds(c, 1), :, :].rearrange("p c t d -> p (c t) d"),
                                        in1=xn[:, cc, :, :], op=ALU.add).then_inc(s["base_done"], 1)
                rsqrt(c, cc, 1)
                pool.wait_ge(s["rstd2_done"], c + 1)
                chain(nc.gpsimd.tensor_tensor(out=shift[:, cc, :], in0=mv[:, cc, 1, :, 0], in1=rstd[:, cc, 1, :], op=ALU.mult))
                nc.gpsimd.tensor_tensor(out=shift[:, cc, :], in0=zeros[:, :], in1=shift[:, cc, :],
                                        op=ALU.subtract).then_inc(s["shift_done"], 1)
                chain.end(3 if more else 2)

            chain.start(0)
            rsqrt(0, 0, 0)
            with pool.Fori(0, NCH // 2 - 1) as b:
                for cc in range(2):
                    norm_chunk(b * 2 + cc, cc, True)
            for cc in range(2):
                norm_chunk(NCH - 2 + cc, cc, cc == 0)

            def add_crossed(c, cc):
                for o, done in ((0, "qc_done"), (1, "kc_done")):
                    pool.wait_ge(s[done], c + 2)
                    nc.gpsimd.tensor_tensor(out=full[:, cc, o, :, :], in0=full[:, cc, o, :, :], in1=tu[:, cc, o, 1, :, :],
                                            op=ALU.add).then_inc(s["added"], 1)

            def split_rest(c, cc):
                for o in range(2):
                    pool.wait_ge(s["cast1"], c * 2 + o + 1)
                    nc.gpsimd.tensor_tensor(out=full[:, cc, o, :, :], in0=full[:, cc, o, :, :], in1=parts[:, cc, o, 0, :, :],
                                            op=ALU.subtract).then_inc(s["resid"], 1)
                for o in range(2):
                    pool.wait_ge(s["cast2"], c * 2 + o + 1)
                    nc.gpsimd.tensor_tensor(out=parts[:, cc, o, 2, :, :], in0=full[:, cc, o, :, :], in1=parts[:, cc, o, 1, :, :],
                                            op=ALU.subtract).then_inc(s["parts_done"], 1)

            with pool.Fori(0, PROBED // 2) as b:
                for cc in range(2):
                    add_crossed(b * 2 + cc, cc)
                    split_rest(b * 2 + cc, cc)
            add_crossed(NCH - 2, 0)

            pool.wait_ge(s["oh_done"], 1)
            for half in range(2):
                es = slice(half * E // 2, (half + 1) * E // 2)
                nc.gpsimd.tensor_tensor(out=oh_hi[:, 1, :, :, es], in0=oh[:, :, :, es],
                                        in1=ramp[:, 0:NT].unsqueeze(1).unsqueeze(3).broadcast_to([P, HI, NT, E // 2]),
                                        op=ALU.mult).then_inc(s["hi_done"], 1)

            def copy_values(b, g):
                nc.gpsimd.tensor_copy(Vg[:, g % 2, :, :, :], V[:, bass.ds(b * KT, KT), g * G4:(g + 1) * G4, :]).then_inc(s["vg_done"], 1)

            def gather(e):
                cc = e % 2
                if e >= 2:
                    pool.wait_ge(s["yT_ready"], e - 1)
                    pool.wait_ge(s["wsel_done"], e - 1)
                for sl in range(4):
                    nc.gpsimd.indirect_dma_start(got[:, cc, sl, :], None, table,
                                                 bass.IndirectOffsetOnAxis(ap=idx[:, e, sl:sl + 1], axis=0)).then_inc(s[f"got_in{cc}"], 16)

            for c in range(2):
                pool.wait_ge(s[f"tab_out{c}"], 16 * (NCH // 2))
                pool.wait_ge(s[f"acc_out{c}"], 16 * (NCH // 2))
            pool.wait_ge(s["wcol_out"], 16)
            pool.wait_ge(s["idx_done"], 1)
            pool.sem_inc(s["res_free"], 2)
            gather(0)
            split_rest(NCH - 2, 0)
            add_crossed(NCH - 1, 1)
            gather(1)
            split_rest(NCH - 1, 1)
            for e in range(E):
                cc = e % 2
                pool.wait_ge(s[f"got_in{cc}"], 64 * (e // 2 + 1))
                if e >= 2:
                    pool.wait_ge(s["o_done"], e)
                nc.gpsimd.tensor_copy(wsel[:, cc, :], got[:, cc, :, D + e]).then_inc(s["wsel_done"], 1)
                if 1 <= e < E - 1:
                    gather(e + 1)
                if e == E - 1:
                    pool.wait_ge(s["v_done"], NCH + 1)
                    for g in range(2):
                        copy_values(0, g)
                if e == 2:
                    for c in range(2):
                        pool.wait_ge(s[f"qk_out{c}"], 192 * (NCH // 2))
                if 2 <= e < 2 + NG:
                    pool.wait_ge(s["wsel_done"], e + 1)
                    nc.gpsimd.memset(qkb[e - 2][KROWS:AUG, 1, :, :], 1.0).then_inc(s["ones_rows_done"], 1)
                    pool.wait_ge(s["ones_rows_done"], e - 1)
                pool.wait_ge(s["o_done"], e + 2)
                if e >= 1:
                    pool.wait_ge(s[f"o_out{1 - cc}"], 64 * ((e - 1) // 2 + 1))
                    pool.sem_inc(s["res_free"], 1)
                for sl in range(4):
                    nc.gpsimd.indirect_dma_start(acc, bass.IndirectOffsetOnAxis(ap=idx[:, e, sl:sl + 1], axis=0), res[:, cc, sl, :], None,
                                                 compute_op=ALU.add).then_inc(s[f"o_out{cc}"], 16)

            def add_bias(b):
                pool.wait_ge(s["accb_in"], b * 16)
                nc.gpsimd.tensor_tensor(out=accb, in0=accb, in1=b_o[:, :].unsqueeze(1).broadcast_to([P, QT, D]),
                                        op=ALU.add).then_inc(s["accb_done"], 1)

            def values_row(b, first):
                for g in range(2 if first else 0, NG):
                    pool.wait_ge(s["pv_ready"], (b * NG + g - 1) * KT)
                    copy_values(b, g)
                    if g == 0 and not first:
                        add_bias(b)

            values_row(0, True)
            with pool.Fori(1, B) as b:
                values_row(b, False)
            add_bias(B)

        @block.scalar
        def _(act):
            act.sem_inc(s["xnT_done"], 2)
            act.sem_inc(s["lg_done"], 2)
            act.sem_inc(s["rows_done"], 2)
            def copy_xnT(c, cc):
                act.wait_ge(s["xnT_ready"], c + 3)
                nc.scalar.activation(xnT[:, :, bass.ds(c * CH, CH)], PS[:, 2 * cc:2 * cc + 2, :], ACT.Copy).then_inc(s["xnT_done"], 1)

            def copy_logits(c, cc):
                act.wait_ge(s["lg_ready"], c + 1)
                nc.scalar.activation(logits[:, bass.ds(c * CH, CH)], PS[0:E, 4 + cc, :], ACT.Copy).then_inc(s["lg_done"], 1)

            def apply_rows(c, cc):
                act.wait_ge(s["shift_done"], c + 3)
                act.wait_ge(s["stored"], c + 1)
                for t in range(TPC):
                    last = nc.scalar.activation(rows[:, cc, t, :], xn[:, cc, t, :], ACT.Identity, bias=shift[:, cc, t:t + 1],
                                                scale=rstd[:, cc, 1, t:t + 1])
                last.then_inc(s["rows_done"], 1)

            copy_xnT(0, 0)
            with act.Fori(0, NCH // 2 - 1) as b:
                for cc in range(2):
                    apply_rows(b * 2 + cc, cc)
                    copy_xnT(b * 2 + cc + 1, 1 - cc)
                    copy_logits(b * 2 + cc, cc)
            apply_rows(NCH - 2, 0)
            copy_xnT(NCH - 1, 1)
            for cc in range(2):
                copy_logits(NCH - 2 + cc, cc)
            apply_rows(NCH - 1, 1)
            act.wait_ge(s["s_in"], 16)
            nc.scalar.activation(scores[:, :], scores[:, :], ACT.Tanh).then_inc(s["tanh_done"], 1)

            def copy_latents(c):
                act.wait_ge(s["ct_ready"], c + 1)
                act.wait_ge(s["v_ready"], c + 1)
                nc.scalar.activation(ctq, PS[:, 0, :], ACT.Identity, bias=b_dq)
                nc.scalar.activation(ctkv, PS[:, 1, :], ACT.Identity, bias=b_dkv).then_inc(s["ct_done"], 1)

            def cast_parts(c, cc):
                act.wait_ge(s["parts_free"], c + 1)
                for o in range(2):
                    act.wait_ge(s["added"], c * 2 + o + 1)
                    nc.scalar.activation(parts[:, cc, o, 0, :, :], full[:, cc, o, :, :], ACT.Copy).then_inc(s["cast1"], 1)
                for o in range(2):
                    act.wait_ge(s["resid"], c * 2 + o + 1)
                    nc.scalar.activation(parts[:, cc, o, 1, :, :], full[:, cc, o, :, :], ACT.Copy).then_inc(s["cast2"], 1)

            copy_latents(0)
            for c in range(2):
                act.wait_ge(s[f"tab_out{c}"], 16 * (NCH // 2))
                act.wait_ge(s[f"acc_out{c}"], 16 * (NCH // 2))
            with act.Fori(0, NCH // 2 - 1) as b:
                for cc in range(2):
                    copy_latents(b * 2 + cc + 1)
                    cast_parts(b * 2 + cc, cc)
            act.wait_ge(s["oh_done"], 1)
            nc.scalar.activation(oh_hi[:, 0, :, :, :], oh, ACT.Copy, scale=part_id).then_inc(s["hi_part_done"], 1)
            copy_latents(NCH - 1)
            cast_parts(NCH - 2, 0)

            def expert(h, cc):
                e = h * 2 + cc
                act.wait_ge(s[f"fc_in{cc}"], h * 64 + 64)
                for f in range(FF // P):
                    act.wait_ge(s["hT_ready"], e * 8 + f + 1)
                    if f == 0:
                        act.wait_ge(s["o_ready"], e + 1)
                    nc.scalar.activation(hT[:, f, :], PS[:, 2 + f % 2, :], ACT.Gelu_apprx_tanh,
                                         bias=b1_s[:, cc, f:f + 1]).then_inc(s["hT_done"], 1)

            expert(0, 0)
            cast_parts(NCH - 1, 1)
            expert(0, 1)
            with act.Fori(1, E // 2) as h:
                for cc in range(2):
                    expert(h, cc)

            def outputs(n, half):
                if half == 0:
                    act.wait_ge(s["pv_half"], n)
                else:
                    act.wait_ge(s["pv_ready"], n * KT)
                nc.scalar.activation(pvs[:, half * 512:(half + 1) * 512], PS[:, 4 + half, :], ACT.Copy).then_inc(s["pv_done"], 1)

            def attend_row(b, first, last):
                for g in range(NG):
                    n = b * NG + g
                    if first and g == 1:
                        for c in range(2):
                            act.wait_ge(s[f"o_out{c}"], 64 * E // 2)
                    for st in range(G4 * KT):
                        kt, j = divmod(st, G4)
                        if not (first and g == 0 and kt < 2):
                            act.wait_ge(s["pv_ready"], n * KT + kt - 1)
                        for half in range(2):
                            act.wait_ge(s["sc_ready"], n * HALVES + st * 2 + half + 1)
                            nc.scalar.activation(expP[:, kt % 2, j, half * 512:(half + 1) * 512], PS[:, score_bank(g, st, half), :],
                                                 ACT.Exp, scale=SCALE).then_inc(s["exp_done"], 1)
                        if not (first and g == 0) and st in (2, 4):
                            outputs(n, st // 2 - 1)

            attend_row(0, True, False)
            with act.Fori(1, B - 1) as b:
                attend_row(b, False, False)
            attend_row(B - 1, False, True)
            for half in range(2):
                outputs(B * NG, half)

        @block.vector
        def _(dve):
            chain = Chain(dve, s["dve_chain"])
            dve.sem_inc(s["qc_done"], 1)
            dve.sem_inc(s["kc_done"], 1)
            dve.sem_inc(s["v_done"], 1)
            dve.sem_inc(s["o_done"], 1)
            chain.start(0)
            nc.vector.memset(thr[:, :], 0.0)
            chain(nc.vector.memset(step[:, :], 1.0))
            chain.end(1)
            NORM = 2

            def stats(src, cc, which):
                for t in range(TPC):
                    last = nc.vector.bn_stats(stat[:, cc, which, t, :], src(t))
                chain(last)
                nc.vector.memset(held[:, :], 0.0)
                for t in range(TPC):
                    last = nc.vector.bn_aggr(mv[:, cc, which, t, :], stat[:, cc, which, t, :])
                last.then_inc(s[f"mv{which + 1}_done"], 1)

            def x_tile(c, t):
                return xs[:, bass.ds(c, 1), t, :].rearrange("p c d -> p (c d)")

            def first_stats(b, c, cc):
                dve.wait_ge(s[f"x_in{cc}"], b * 16 + 16)
                stats(lambda t: x_tile(c, t), cc, 0)

            def norm_chunk(b, c, cc, more):
                chain.start(c * NORM + 2)
                if more:
                    first_stats(b + cc, c + 1, 1 - cc)
                dve.wait_ge(s["rstd1_done"], c + 1)
                dve.wait_ge(s["mv1_done"], c + 1)
                dve.wait_ge(s["xnT_ready"], c + 1)
                dve.wait_ge(s["base_done"], c + 1)
                dve.wait_ge(s["rows_done"], c + 1)
                for t in range(TPC):
                    last = nc.vector.tensor_scalar(xn[:, cc, t, :], x_tile(c, t), mv[:, cc, 0, t, 0:1], rstd[:, cc, 0, t:t + 1],
                                                   ALU.subtract, ALU.mult)
                last.then_inc(s["xn_done"], 1)
                dve.wait_ge(s["xn_done"], c + 1)
                dve.wait_ge(s["shift_done"], c + 1)
                stats(lambda t: xn[:, cc, t, :], cc, 1)
                chain.end(NORM if more else 1)

            chain.start(1)
            first_stats(0, 0, 0)
            with dve.Fori(0, NCH // 2 - 1) as b:
                for cc in range(2):
                    norm_chunk(b, b * 2 + cc, cc, True)
            for cc in range(2):
                norm_chunk(NCH // 2 - 1, NCH - 2 + cc, cc, cc == 0)
            done = 1 + NCH * NORM

            chain.start(done)
            dve.wait_ge(s["tanh_done"], 1)
            chain(nc.vector.tensor_scalar(scores[:, :], scores[:, :], 1.0, 0.5, ALU.add, ALU.mult))

            def probe_start():
                chain(nc.vector.tensor_tensor(out=cand[:, :], in0=thr[:, :], in1=step[:, :], op=ALU.add))
                nc.vector.tensor_scalar(marks[:, :], scores[:, :], cand[:, :], None, ALU.is_ge, ALU.add,
                                        accum_out=cnt[:, :]).then_inc(s["cnt_ready"], 1)

            def probe_end(n):
                dve.wait_ge(s["cnt_sum"], n)
                chain(nc.vector.tensor_scalar(cand[:, :], PS[:, 7, 0:1], float(KEEP), step[:, :], ALU.is_ge, ALU.mult))
                nc.vector.tensor_tensor(out=thr[:, :], in0=thr[:, :], in1=cand[:, :], op=ALU.add)
                chain(nc.vector.tensor_scalar(step[:, :], step[:, :], 0.5, None, ALU.mult))

            PROBE = 3
            probe_start()
            for n in range(lead):
                probe_end(n + 1)
                probe_start()
            dve.wait_ge(s["wcol_ready"], 1)
            for i in range(2):
                last = nc.vector.tensor_copy(wtok[:, i::2, :], PS[:, 6, i * P:(i + 1) * P].rearrange("p (e r) -> p r e", e=E))
            last.then_inc(s["wcol_done"], 1)
            done = chain.end(2 + lead * PROBE)

            dve.wait_ge(s["w_in"], 16 * 12)
            dve.wait_ge(s["xnT_ready"], NCH + 2)
            dve.wait_ge(s["base_done"], NCH + 2)
            for c in range(2):
                dve.wait_ge(s[f"tab_out{c}"], 16 * (NCH // 2))
                dve.wait_ge(s[f"acc_out{c}"], 16 * (NCH // 2))
            dve.wait_ge(s["ones_done"], 1)
            def rotate(c, cc, o):
                banks, bias, name = ((4, 5), b_qr, "qr") if o == 0 else ((2, 3), b_kr, "kr")
                csl = slice(cc * CH, (cc + 1) * CH)
                dve.wait_ge(s[name + "_ready"], c + 1)
                if o == 1:
                    dve.wait_ge(s["parts_done"], c * 2 + 2)
                for eo in range(2):
                    nc.vector.scalar_tensor_tensor(out=tu[:, cc, o, 0, eo, :], in0=PS[:, banks[eo], :], scalar=bias[eo],
                                                   in1=cos[:, csl], op0=ALU.add, op1=ALU.mult)
                for eo, tab in ((1, nsin), (0, sin)):
                    last = nc.vector.scalar_tensor_tensor(out=tu[:, cc, o, 1, 1 - eo, :], in0=PS[:, banks[eo], :], scalar=bias[eo],
                                                          in1=tab[:, csl], op0=ALU.add, op1=ALU.mult)
                last.then_inc(s[name + "_done"], 1)

            def combine(c, cc, o):
                banks, bias, name = ((0, 1), b_uq, "q") if o == 0 else ((2, 3), b_uk, "k")
                dve.wait_ge(s[name + "r_done"], c + 1)
                dve.wait_ge(s[name + "c_ready"], c + 1)
                for eo in range(2):
                    last = nc.vector.scalar_tensor_tensor(out=full[:, cc, o, eo, :], in0=PS[:, banks[eo], :], scalar=bias[eo],
                                                          in1=tu[:, cc, o, 0, eo, :], op0=ALU.add, op1=ALU.add)
                last.then_inc(s[name + "c_done"], 1)

            def values_out(c):
                dve.wait_ge(s["v_ready"], c + 2)
                for i in range(2):
                    last = nc.vector.tensor_tensor(
                        out=V[:, bass.ds(c * TPC + 2 * i, 2), :, 0:HD],
                        in0=PS[:, 4 + i, :].rearrange("p (t h d) -> p t h d", t=2, h=H),
                        in1=b_uv[:, :].rearrange("p (h d) -> p h d", h=H).unsqueeze(1).broadcast_to([P, 2, H, HD]), op=ALU.add)
                last.then_inc(s["v_done"], 1)

            with dve.Fori(0, PROBED // 2) as b:
                for cc in range(2):
                    c = b * 2 + cc
                    chain.start(c * 4 * PROBE + done)

                    def probe(n):
                        probe_end(c * 4 + lead + n)
                        probe_start()

                    rotate(c, cc, 1)
                    rotate(c, cc, 0)
                    combine(c, cc, 0)
                    probe(1)
                    combine(c, cc, 1)
                    probe(2)
                    values_out(c)
                    probe(3)
                    probe(4)
                    chain.end(4 * PROBE)
            done = done + 4 * PROBE * PROBED

            chain.start(done)
            nc.vector.tensor_scalar(gt, scores[:, :], thr[:, :], None, ALU.is_gt, ALU.add, accum_out=small[:, 0:1])
            nc.vector.tensor_scalar(eq, scores[:, :], thr[:, :], None, ALU.is_equal, ALU.add, accum_out=small[:, 1:2]).then_inc(s["sum_ready"], 1)
            dve.wait_ge(s["sum_ready"], 1)
            chain(nc.vector.tensor_tensor_scan(out=rank, data0=ones[:, :], data1=eq, initial=0.0, op0=ALU.mult, op1=ALU.add))
            rotate(NCH - 2, 0, 1)
            dve.wait_ge(s["sums_done"], 1)
            chain(nc.vector.tensor_scalar(small[:, 2:3], PS[:, 7, 1:2], -1.0, float(KEEP), ALU.mult, ALU.add))
            chain(nc.vector.tensor_tensor(out=small[:, 3:4], in0=small[:, 2:3], in1=PS[:, 7, 2:3], op=ALU.subtract))
            chain(nc.vector.scalar_tensor_tensor(out=taken, in0=rank, scalar=small[:, 3:4], in1=eq, op0=ALU.is_le, op1=ALU.mult))
            nc.vector.scalar_tensor_tensor(out=gt, in0=taken, scalar=1.0, in1=gt, op0=ALU.mult, op1=ALU.add,
                                           accum_out=small[:, 4:5]).then_inc(s["sum_ready"], 1)
            dve.wait_ge(s["sum_ready"], 2)
            chain(nc.vector.tensor_tensor_scan(out=rank, data0=ones[:, :], data1=gt, initial=0.0, op0=ALU.mult, op1=ALU.add))
            rotate(NCH - 2, 0, 0)
            dve.wait_ge(s["sums_done"], 2)
            chain(nc.vector.tensor_scalar(rank, rank, PS[:, 7, 3:4], -1025.0, ALU.add, ALU.add))
            nc.vector.tensor_tensor(out=pos, in0=rank, in1=gt, op=ALU.mult).then_inc(s["pos_ready"], 1)
            for o in range(2):
                combine(NCH - 2, 0, o)
            dve.wait_ge(s["pos_turned"], 1)
            for i in range(2):
                last = nc.vector.tensor_scalar(posi[:, i::2, :], PS[:, 6, i * P:(i + 1) * P].rearrange("p (e r) -> p r e", e=E),
                                               1024.0, None, ALU.add)
            chain(last)
            nc.vector.tensor_scalar(loi, posi, LO - 1, None, ALU.bitwise_and)
            chain(nc.vector.tensor_scalar(hii, posi, 5, None, ALU.logical_shift_right))
            nc.vector.tensor_copy(lof, loi)
            nc.vector.tensor_copy(hif, hii).then_inc(s["pos_done"], 1)
            dve.wait_ge(s["pos_done"], 1)
            for l in range(HI):
                last = nc.vector.tensor_scalar(oh[:, l, :, :], hif, float(l), None, ALU.is_equal)
            last.then_inc(s["oh_done"], 1)
            for l in range(LO):
                last = nc.vector.tensor_scalar(oh_lo[:, l, :, :], lof, float(l), None, ALU.is_equal)
            last.then_inc(s["oh_done"], 1)
            values_out(NCH - 2)
            rotate(NCH - 1, 1, 1)
            dve.wait_ge(s["tok_ready"], 1)
            chain(nc.vector.tensor_copy(tok[0:LO, :, :, :].rearrange("p e w l -> p (e w l)"), PS[0:LO, 6, 0:E * 2 * HI]))
            nc.vector.scalar_tensor_tensor(out=token[0:LO, :, :], in0=tok[0:LO, :, 1, :], scalar=float(P), in1=tok[0:LO, :, 0, :],
                                           op0=ALU.mult, op1=ALU.add).then_inc(s["tok_done"], 1)
            dve.wait_ge(s["idx_ready"], 1)
            nc.vector.tensor_copy(idx[:, :, :], PS[:, 6, 0:E * 4].rearrange("p (e l) -> p e l", e=E)).then_inc(s["idx_done"], 1)
            done = chain.end(9)
            rotate(NCH - 1, 1, 0)
            for o in range(2):
                combine(NCH - 1, 1, o)
            values_out(NCH - 1)

            def negate_maxima(which, count):
                dve.wait_ge(s["side_done"], count)
                nc.vector.tensor_reduce(nmax, hmax[:, which, :].rearrange("p (t k) -> p t k", k=2), AX.X, ALU.max, negate=True).then_inc(s["nmax_done"], 1)

            def run_side(seq, count, bank_of, g, row):
                for k, u in enumerate(seq):
                    bank = bank_of(k)
                    dve.wait_ge(s["side_ready"], count + k + 1)
                    if u[0] == "max":
                        which = (g + u[2]) % 2
                        nc.vector.tensor_reduce(hmax[:, which, u[1]:u[1] + 1], PS[:, bank, :], AX.X, ALU.max).then_inc(s["side_done"], 1)
                        if u == ("max", 0, 2):
                            negate_maxima(1 - which, count + k)
                        elif u[1] == MAXES - 1 and seq[k + 1] == ("neg",):
                            negate_maxima(which, count + k + 1)
                    elif u[0] == "neg":
                        m = PS[0:G4 * QT, bank, 0:P]
                        chain(nc.vector.tensor_copy(nparts[:, 0, :], m))
                        chain(nc.vector.tensor_tensor(out=nrest, in0=m, in1=nparts[:, 0, :], op=ALU.subtract))
                        chain(nc.vector.tensor_copy(nparts[:, 1, :], nrest))
                        nc.vector.tensor_tensor(out=nparts[:, 2, :], in0=nrest, in1=nparts[:, 1, :], op=ALU.subtract).then_inc(s["side_done"], 1)
                    elif u[0] == "norm":
                        half, pg = u[1], (g - 1) % NG
                        o4 = PS[:, bank, :].rearrange("p (t h d) -> p t h d", t=4, h=G4)
                        dst = O[:, half * 4:half * 4 + 4, pg * G4 * HD:(pg + 1) * G4 * HD].rearrange("p t (h d) -> p t h d", h=G4)
                        chain(nc.vector.reciprocal(rsum[:, half, :, :], o4[:, :, :, HD]))
                        nc.vector.tensor_tensor(out=dst, in0=o4[:, :, :, 0:HD], in1=rsum[:, half, :, :].unsqueeze(3).broadcast_to([P, 4, G4, HD]),
                                                op=ALU.mult).then_inc(s["side_done"], 1)
                    elif u[0] == "turn":
                        half, kb = divmod(u[1], 2)
                        nc.vector.tensor_copy(OT[:, kb, half * 512:(half + 1) * 512], PS[:, bank, :]).then_inc(s["side_done"], 1)
                    else:
                        if u[1] == 0:
                            dve.wait_ge(s["accb_done"], row)
                        i = u[1]
                        nc.vector.tensor_tensor(out=outs[:, 2 * i:2 * i + 2, :], in0=PS[:, bank, :].rearrange("p (t d) -> p t d", t=2),
                                                in1=accb[:, 2 * i:2 * i + 2, :], op=ALU.add).then_inc(s["side_done"], 1)

            def yT_out(e):
                dve.wait_ge(s["yT_ready"], e + 1)
                for k in range(KB):
                    last = nc.vector.tensor_scalar(yT[:, k, :], PS[:, k, :], gamma[k], beta[k], ALU.mult, ALU.add)
                last.then_inc(s["yT_done"], 1)

            def expert(h, cc, more):
                e = h * 2 + cc
                chain.start(e + done)
                for i in range(PER_EXPERT):
                    dve.wait_ge(s["side_ready"], e * PER_EXPERT + i + 1)
                    nc.vector.tensor_reduce(hmax[:, 0, bass.ds(e * PER_EXPERT + i, 1)], PS[:, 6 + i % 2, :], AX.X,
                                            ALU.max).then_inc(s["side_done"], 1)
                if more:
                    yT_out(e + 1)
                else:
                    run_side(lead_uses, MAXES, lead_bank, NG - 1, None)
                dve.wait_ge(s[f"fc_in{cc}"], h * 64 + 64)
                dve.wait_ge(s["parts_done"], 2 * NCH + 4)
                dve.wait_ge(s["wsel_done"], e + 1)
                dve.wait_ge(s["res_free"], e + 1)
                dve.wait_ge(s["o_ready"], e + 2)
                chain(nc.vector.tensor_tensor(out=res[:, cc, :, :], in0=PS[:, 4:6, :].rearrange("p a (b d) -> p (a b) d", b=2),
                                              in1=b2_s[:, cc, :].unsqueeze(1).broadcast_to([P, 4, D]), op=ALU.add))
                for sl in range(4):
                    last = nc.vector.tensor_scalar(res[:, cc, sl, :], res[:, cc, sl, :], wsel[:, cc, sl:sl + 1], None, ALU.mult)
                last.then_inc(s["o_done"], 1)
                chain.end(1 if more else 4)

            yT_out(0)
            with dve.Fori(0, E // 2 - 1) as h:
                for cc in range(2):
                    expert(h, cc, True)
            for cc in range(2):
                expert(E // 2 - 1, cc, cc == 0)
            done = done + E + 3


            def chained(first, last):
                kinds = [u[0] for g in range(NG) for u in flat_stream(g, first, last)]
                return 3 * kinds.count("neg") + kinds.count("norm")

            C_FIRST, C_MID, C_LAST = chained(True, False), chained(False, False), chained(False, True)

            def attend_row(b, first, last):
                chain.start(done if first else b * C_MID + (done + C_FIRST - C_MID))
                for g in range(NG):
                    if first and g == 1:
                        for c in range(2):
                            dve.wait_ge(s[f"o_out{c}"], 64 * E // 2)
                    ahead = before_group(g, first, last)
                    run_side(flat_stream(g, first, last), side_base(b) + ahead, lambda k: side_bank(first, ahead + k), g, b)
                chain.end(chained(first, last))

            attend_row(0, True, False)
            with dve.Fori(1, B - 1) as b:
                attend_row(b, False, False)
            attend_row(B - 1, False, True)
            chain.start(done + C_FIRST + C_MID * (B - 2) + C_LAST)
            run_side(tail_uses, TAIL, lambda k: side_bank(True, TAIL - LEAD + k), 0, B)

        @block.tensor
        def _(pe):
            pe.sem_inc(s["xnT_ready"], 2)
            pe.sem_inc(s["v_ready"], 1)
            pe.sem_inc(s["o_ready"], 1)
            mm = nc.tensor.matmul
            pe.wait_ge(s["const_in"], 32)

            def turn_xn(c, cc):
                pe.wait_ge(s["xn_done"], c + 1)
                pe.wait_ge(s["xnT_done"], c + 1)
                for k in range(KB):
                    for t in range(TPC):
                        last = nc.tensor.transpose(PS[:, 2 * cc + k, t * P:(t + 1) * P], xn[:, cc, t, k * P:(k + 1) * P], ident)
                last.then_inc(s["xnT_ready"], 1)

            def gate_logits(c, cc):
                pe.wait_ge(s["xnT_done"], c + 3)
                pe.wait_ge(s["lg_done"], c + 1)
                for k in range(KB):
                    last = mm(PS[0:E, 4 + cc, :], w_gate[:, k, :], xnT[:, k, bass.ds(c * CH, CH)], start=k == 0, stop=k == KB - 1)
                last.then_inc(s["lg_ready"], 1)

            turn_xn(0, 0)
            with pe.Fori(0, NCH // 2 - 1) as b:
                for cc in range(2):
                    turn_xn(b * 2 + cc + 1, 1 - cc)
                    gate_logits(b * 2 + cc, cc)
            turn_xn(NCH - 1, 1)
            for cc in range(2):
                gate_logits(NCH - 2 + cc, cc)
            pe.wait_ge(s["w_in"], 16 * 12)

            def count(n):
                pe.wait_ge(s["cnt_ready"], n)
                mm(PS[:, 7, 0:1], same, cnt[:, :], start=True, stop=True).then_inc(s["cnt_sum"], 1)

            def from_x(c, probe):
                def xT(k):
                    return xnT[:, k, bass.ds(c * CH, CH)]

                pe.wait_ge(s["qc_done"], c + 1)
                for bank, w in ((0, w_dq), (1, w_dkv)):
                    for k in range(KB):
                        last = mm(PS[:, bank, :], w[:, k, :], xT(k), start=k == 0, stop=k == KB - 1)
                    if bank == 1:
                        last.then_inc(s["ct_ready"], 1)
                    if probe is not None:
                        count(probe + bank)
                pe.wait_ge(s["kc_done"], c + 1)
                for eo in range(2):
                    for k in range(KB):
                        last = mm(PS[:, 2 + eo, :], w_kr[:, k, eo * P:(eo + 1) * P], xT(k), start=k == 0, stop=k == KB - 1)
                    if eo == 0 and probe is not None:
                        count(probe + 2)
                last.then_inc(s["kr_ready"], 1)

            def single(bank, w, src):
                return mm(PS[:, bank, :], w, src, start=True, stop=True)

            def queries(c, probe=None):
                pe.wait_ge(s["ct_done"], c + 1)
                pe.wait_ge(s["v_done"], c + 1)
                for eo in range(2):
                    last = single(4 + eo, w_qr[:, eo * P:(eo + 1) * P], ctq)
                last.then_inc(s["qr_ready"], 1)
                if probe is not None:
                    count(probe)
                for eo in range(2):
                    last = single(eo, w_uq[:, eo * P:(eo + 1) * P], ctq)
                last.then_inc(s["qc_ready"], 1)

            def keys(c):
                pe.wait_ge(s["kr_done"], c + 1)
                for eo in range(2):
                    last = single(2 + eo, w_uk[:, eo * P:(eo + 1) * P], ctkv)
                last.then_inc(s["kc_ready"], 1)

            def vals(c):
                pe.wait_ge(s["qr_done"], c + 1)
                for t in range(TPC):
                    last = mm(PS[:, 4 + t // 2, (t % 2) * D:(t % 2 + 1) * D], ctkv[:, t * P:(t + 1) * P], w_uv[:, :], start=True, stop=True)
                last.then_inc(s["v_ready"], 1)

            pe.wait_ge(s["xnT_done"], NCH + 2)
            from_x(0, None)
            for n in range(lead):
                count(n + 1)
            for i in range(2):
                last = nc.tensor.transpose(PS[:, 6, i * P:(i + 1) * P], scores[:, i * P:(i + 1) * P], ident)
            last.then_inc(s["wcol_ready"], 1)
            pe.wait_ge(s["lg_done"], NCH + 2)
            with pe.Fori(0, PROBED) as c:
                queries(c, c * 4 + lead + 1)
                keys(c)
                vals(c)
                from_x(c + 1, c * 4 + lead + 2)

            pe.wait_ge(s["sum_ready"], 1)
            mm(PS[:, 7, 1:2], same, small[:, 0:1], start=True, stop=True)
            mm(PS[:, 7, 2:3], before, small[:, 1:2], start=True, stop=True).then_inc(s["sums_done"], 1)
            queries(NCH - 2)
            pe.wait_ge(s["sum_ready"], 2)
            mm(PS[:, 7, 3:4], before, small[:, 4:5], start=True, stop=True).then_inc(s["sums_done"], 1)
            keys(NCH - 2)
            pe.wait_ge(s["pos_ready"], 1)
            for i in range(2):
                last = nc.tensor.transpose(PS[:, 6, i * P:(i + 1) * P], pos[:, i * P:(i + 1) * P], ident)
            last.then_inc(s["pos_turned"], 1)
            vals(NCH - 2)
            from_x(NCH - 1, None)
            pe.wait_ge(s["hi_part_done"], 1)
            pe.wait_ge(s["oh_done"], 2)
            for e in range(E):
                pe.wait_ge(s["hi_done"], 1 + e // (E // 2))
                for t in range(NT):
                    last = mm(PS[0:LO, 6, e * 2 * HI:(e + 1) * 2 * HI], oh_lo[:, :, t, e], oh_hi[:, :, :, t, e].rearrange("p w l -> p (w l)"),
                              start=t == 0, stop=t == NT - 1)
            last.then_inc(s["tok_ready"], 1)
            pe.wait_ge(s["tok_done"], 1)
            for q in range(4):
                last = mm(PS[LO * q:LO * (q + 1), 6, 0:E * 4], ident[0:LO, 0:LO], token[0:LO, :, 4 * q:4 * q + 4],
                          start=True, stop=True)
            last.then_inc(s["idx_ready"], 1)
            queries(NCH - 1)
            keys(NCH - 1)
            vals(NCH - 1)

            def side_use(u, count, bank, g, n):
                pe.wait_ge(s["side_done"], count - (1 if g is None else 2))
                if g is None:
                    g = NG - 1
                if u[0] == "max":
                    q, k = (qkb[(g + u[2]) % NG][0:KROWS, o, :, :] for o in range(2))
                    j, rest = divmod(u[1], 2 * QT)
                    qt, half = divmod(rest, 2)
                    ins = mm(PS[:, bank, :], q[:, j, qt * P:(qt + 1) * P], k[:, j, half * 512:(half + 1) * 512], start=True, stop=True)
                elif u[0] == "neg":
                    pe.wait_ge(s["nmax_done"], n + 2)
                    ins = nc.tensor.transpose(PS[0:G4 * QT, bank, 0:P], nmax, ident)
                elif u[0] == "norm":
                    pe.wait_ge(s["pv_done"], 2 * n - 1 + u[1])
                    for t in range(4):
                        q0 = (u[1] * 4 + t) * P
                        ins = nc.tensor.transpose(PS[:, bank, t * P:(t + 1) * P], pvs[:, q0:q0 + P], ident)
                elif u[0] == "turn":
                    half, kb = divmod(u[1], 2)
                    for t in range(4):
                        ins = nc.tensor.transpose(PS[:, bank, t * P:(t + 1) * P], O[:, half * 4 + t, kb * P:(kb + 1) * P], ident)
                else:
                    for t in range(2):
                        q0 = (u[1] * 2 + t) * P
                        for kb in range(KB):
                            ins = mm(PS[:, bank, t * D:(t + 1) * D], OT[:, kb, q0:q0 + P], w_o[:, kb, :], start=kb == 0, stop=kb == KB - 1)
                ins.then_inc(s["side_ready"], 1)

            def turn_rows(e, h, cc):
                pe.wait_ge(s[f"got_in{cc}"], h * 64 + 64)
                for k in range(KB):
                    for sl in range(4):
                        last = nc.tensor.transpose(PS[:, k, sl * P:(sl + 1) * P], got[:, cc, sl, k * P:(k + 1) * P], ident)
                last.then_inc(s["yT_ready"], 1)

            def first_max(h, cc, i):
                e = h * 2 + cc
                if i == 0:
                    pe.wait_ge(s["o_done"], e + 1)
                    pe.wait_ge(s["qk_in0"], 18 * 16)
                if i >= 2:
                    pe.wait_ge(s["side_done"], e * PER_EXPERT + i - 1)
                qt, half = cc * QT // 2 + i // 2, i % 2
                q, k = (qkb[0][0:KROWS, o, bass.ds(h, 1), :].rearrange("p h s -> p (h s)") for o in range(2))
                mm(PS[:, 6 + i % 2, :], q[:, qt * P:(qt + 1) * P], k[:, half * 512:(half + 1) * 512],
                   start=True, stop=True).then_inc(s["side_ready"], 1)

            def expert(h, cc, more):
                e = h * 2 + cc
                pe.wait_ge(s["yT_done"], e + 1)
                pe.wait_ge(s[f"fc_in{cc}"], h * 64 + 64)
                for f in range(FF // P):
                    if f >= 2:
                        pe.wait_ge(s["hT_done"], e * 8 + f - 1)
                    for k in range(KB):
                        last = mm(PS[:, 2 + f % 2, :], fc1_s[cc][:, k, f * P:(f + 1) * P], yT[:, k, :], start=k == 0, stop=k == KB - 1)
                    last.then_inc(s["hT_ready"], 1)
                    if f > 0:
                        first_max(h, cc, f - 1)
                first_max(h, cc, PER_EXPERT - 1)
                if more:
                    turn_rows(e + 1, h + cc, 1 - cc)
                else:
                    pe.wait_ge(s["qk_in1"], 18 * 16)
                for sl in range(4):
                    for f in range(FF // P):
                        if sl == 0:
                            pe.wait_ge(s["hT_done"], e * 8 + f + 1)
                        k, at_place = divmod(sl * (FF // P) + f - 2, 2)
                        if not more and at_place == 0 and 0 <= k < len(lead_uses):
                            side_use(lead_uses[k], MAXES + k, lead_bank(k), None, -1)
                        last = mm(PS[:, 4 + sl // 2, sl % 2 * D:(sl % 2 + 1) * D], hT[:, f, sl * P:(sl + 1) * P], fc2_s[cc][:, f, :], start=f == 0, stop=f == FF // P - 1)
                last.then_inc(s["o_ready"], 1)

            for done in ("qc_done", "kc_done", "v_done"):
                pe.wait_ge(s[done], NCH + 1)
            turn_rows(0, 0, 0)
            with pe.Fori(0, E // 2 - 1) as h:
                for cc in range(2):
                    expert(h, cc, True)
            for cc in range(2):
                expert(E // 2 - 1, cc, cc == 0)

            pe.wait_ge(s["ones_rows_done"], NG)

            def values(g, n, kt, quarter, first):
                if quarter == 0:
                    pe.wait_ge(s["exp_done"], n * HALVES + (kt + 1) * G4 * 2)
                    if kt == 0:
                        pe.wait_ge(s["vg_done"], n + 1)
                    if kt == 0 and first and g == 0:
                        pe.wait_ge(s["o_done"], E + 1)
                if kt == 0 and quarter % 2 == 0 and not (first and g == 0):
                    pe.wait_ge(s["pv_done"], 2 * n - 1 + quarter // 2)
                half, q0 = quarter // 2, quarter % 2 * 256
                for j in range(G4):
                    ins = mm(PS[LO * j:LO * j + VW, 4 + half, q0:q0 + 256], Vg[:, g % 2, kt, j, :], expP[:, kt % 2, j, quarter * 256:(quarter + 1) * 256],
                             start=kt == 0 and q0 == 0, stop=kt == KT - 1, skip_group_check=True)
                if quarter == 1 and kt == KT - 1:
                    ins.then_inc(s["pv_half"], 1)
                if quarter == 3:
                    ins.then_inc(s["pv_ready"], 1)

            def attend_row(b, first, last):
                for g in range(NG):
                    n = b * NG + g
                    k = before_group(g, first, last)
                    pe.wait_ge(s["aug_in"], n * 48 + 48)
                    if not (last and g >= NG - 2):
                        pe.wait_ge(s[f"qk_in{(g + 2) % NG}"], (b + (g + 2) // NG) * 288 + 288)
                    for st, places in enumerate(side_stream(g, first, last)):
                        kt, j = divmod(st, G4)
                        for place, todo in enumerate(places):
                            if place == 1:
                                for half in range(2):
                                    number = n * HALVES + st * 2 + half
                                    if g == 0 and st + half == 0:
                                        if not first:
                                            pe.wait_ge(s["exp_done"], number)
                                    elif not (first and g == 0 and st * 2 + half < 3):
                                        pe.wait_ge(s["exp_done"], number - 2)
                                    mm(PS[:, score_bank(g, st, half), :], qkb[g][0:AUG, 1, j, kt * P:(kt + 1) * P],
                                       qkb[g][0:AUG, 0, j, half * 512:(half + 1) * 512], start=True, stop=True).then_inc(s["sc_ready"], 1)
                            if place == 2 and kt > 0:
                                values(g, n, kt - 1, j, first)
                            if place == 2 and kt == 0 and not (first and g == 0):
                                values((g - 1) % NG, n - 1, KT - 1, j, first)
                            for u in todo:
                                side_use(u, side_base(b) + k, side_bank(first, k), g, n)
                                k += 1

            attend_row(0, True, False)
            with pe.Fori(1, B - 1) as b:
                attend_row(b, False, False)
            attend_row(B - 1, False, True)
            for quarter in range(4):
                values(NG - 1, B * NG - 1, KT - 1, quarter, False)
            for k, u in enumerate(tail_uses):
                if k in tail_needs:
                    pe.wait_ge(s["side_done"], TAIL + tail_needs[k])
                side_use(u, TAIL + k, side_bank(True, TAIL - LEAD + k), 0, B * NG)


def kernel(**inputs):
    import concourse.bacc as bacc
    from concourse.bass_utils import run_bass_kernel_spmd

    a = {n.removeprefix("L0_"): np.asarray(v) for n, v in inputs.items()}

    def apart(w):
        return np.ascontiguousarray(np.concatenate([w[..., 0::2], w[..., 1::2]], -1))

    def halves(v):
        return np.ascontiguousarray(v.reshape(2, P).T)

    cols = [a["attn_Wd_q_b"][:, None], a["attn_Wd_kv_b"][:, None]]
    cols += [halves(apart(a[f"attn_{n}_b"])) for n in ("Wu_q", "Wq_r", "Wk_r", "Wu_k")]
    cols += [halves(a["ffn_ln_gamma"]), halves(a["ffn_ln_beta"])]
    arrays = {
        "x": a["attn_x"].reshape(TOK, D), "wdq": a["attn_Wd_q_w"], "wdkv": a["attn_Wd_kv_w"],
        "wuq": apart(a["attn_Wu_q_w"]), "wqr": apart(a["attn_Wq_r_w"]), "wkr": apart(a["attn_Wk_r_w"]), "wuk": apart(a["attn_Wu_k_w"]),
        "wuv": a["attn_Wu_v_w"], "wo": a["attn_Wo_w"], "cols": np.concatenate(cols, 1), "buv": a["attn_Wu_v_b"], "bo": a["attn_Wo_b"],
        "gate": a["ffn_gate_w"].T, "fc1": a["ffn_fc1s"].transpose(0, 2, 1),
        "b1": a["ffn_b1s"].reshape(E, FF // P, P).transpose(0, 2, 1), "fc2": a["ffn_fc2s"].transpose(0, 2, 1), "b2": a["ffn_b2s"],
        "const": constants(),
    }
    arrays = {n: np.ascontiguousarray(v) for n, v in arrays.items()}
    nc = bacc.Bacc("TRN2", target_bir_lowering=False, num_devices=1)
    aps = [nc.dram_tensor(n, v.shape, mybir.dt.from_np(v.dtype), kind="ExternalInput").ap() for n, v in arrays.items()]
    acc = nc.dram_tensor("acc", (TOK, D), F32, kind="Internal").ap()
    table = nc.dram_tensor("table", (TOK, ROW), F32, kind="Internal").ap()
    qk = nc.dram_tensor("qk", (2, B, 2, H, 3, PAIR, S), BF16, kind="Internal").ap()
    out = nc.dram_tensor("out", (B, S, D), F32, kind="ExternalOutput").ap()
    program(nc, *aps, acc, table, qk, out.rearrange("b s d -> (b s) d"))
    result = run_bass_kernel_spmd(nc, [arrays], core_ids=[0])
    return result.results[0]["out"]
```
